# Optimizing a Trainium2 kernel written in Bass

```python
import numpy as np
import jax
import jax.numpy as jnp

def _softmax(x, axis=-1):
    return jax.nn.softmax(x, axis=axis)

def _gelu(x):
    return jax.nn.gelu(x, approximate=True)

def _silu(x):
    return jax.nn.silu(x)

def _sigmoid(x):
    return jax.nn.sigmoid(x)

def _layernorm(x, axis=-1, eps=1e-05):
    m = jnp.mean(x, axis=axis, keepdims=True)
    v = jnp.var(x, axis=axis, keepdims=True)
    return (x - m) / jnp.sqrt(v + eps)

def _scatter_add(tgt, idx, src, axis=0):
    return tgt.at[idx].add(src)

def _segment_sum(src, seg, n):
    return jax.ops.segment_sum(src, seg, n)
kernel_name = 'mk_flamingo_gated_d4_seqx_r8_2cd954'

def setup_inputs(seed: int=0):
    np.random.seed(seed)
    _w = jnp.asarray

    def _rec_inputs():
        import jax
        import jax.numpy as jnp
        _rk = jax.random.key(seed)
        x = -0.000125 + 0.9999 * jax.random.normal(jax.random.fold_in(_rk, 1), (32, 64, 256), jnp.float32)
        _lenS = 64 - jax.random.randint(jax.random.fold_in(_rk, 7), (32,), 0, max(1, 64 // 4) + 1, jnp.int32)
        _lenS2 = 64 - jax.random.randint(jax.random.fold_in(_rk, 8), (32,), 0, max(1, 64 // 4) + 1, jnp.int32)
        _ctx_2048P = jax.random.normal(jax.random.fold_in(_rk, 11), (32, 16, 256), jnp.float32)
        _ctx_2048c = jax.random.dirichlet(jax.random.fold_in(_rk, 511), 0.3 * jnp.ones((16,), jnp.float32), (32, 64))
        _ctx_2048t = jnp.einsum('bsk,bkd->bsd', _ctx_2048c, _ctx_2048P)
        _ctx_2048t = _ctx_2048t * jax.lax.rsqrt(jnp.mean(jnp.square(_ctx_2048t)) + 1e-12) * 0.953939
        ctx_2048 = -0.000514642 + 1.00011 * (_ctx_2048t + 0.3 * jax.random.normal(jax.random.fold_in(_rk, 611), (32, 64, 256), jnp.float32))
        _validS = jnp.arange(64)[None, :] < _lenS[:, None]
        _validS2 = jnp.arange(64)[None, :] < _lenS2[:, None]
        _causal = jnp.tril(jnp.ones((64, 64), dtype=bool))
        mask_BxS2_bk0 = jnp.logical_not(jnp.broadcast_to(_validS2[:, :], (32, 64)))
        _g = jax.random.normal(jax.random.fold_in(_rk, 9001), (2, 4), jnp.float32)
        _g = jnp.sign(_g) * jnp.maximum(jnp.abs(_g), 1.0) + (_g == 0) * 1.0
        g_xattn = _g[0]
        g_ffn = _g[1]
        return (x, ctx_2048, mask_BxS2_bk0, g_xattn, g_ffn)
    x, ctx_2048, mask_BxS2_bk0, g_xattn, g_ffn = _rec_inputs()

    def _L0_xattn_setup():
        import jax, jax.numpy as jnp
        import numpy as np
        key = jax.random.key(seed)
        k1, k2, k3 = jax.random.split(key, 3)
        B, S, D, M = (8, 256, 256, 128)
        hidden_states = jax.random.normal(k1, (B, S, D), dtype=jnp.float32)
        memory_tokens = jax.random.normal(k2, (B, M, D), dtype=jnp.float32)
        memory_mask = jax.random.randint(k3, (B, M), 0, 2).astype(jnp.bool_)
        return {'hidden_states': hidden_states, 'memory_tokens': memory_tokens, 'memory_mask': memory_mask}
    _L0_xattn_all = _L0_xattn_setup()
    _L0_xattn_in = {k: v for k, v in _L0_xattn_all.items() if k in ()}
    del _L0_xattn_all

    def _L0_ffn_setup():
        import jax, jax.numpy as jnp
        import numpy as np
        B, S, H = (2, 256, 256)
        E, I, K = (8, 176, 2)
        SHARED_I = 176 * 2

        def _moe_forward(hidden_states, gate_w, w1, w3, w2, sw1, sw3, sw2):
            x = hidden_states.reshape(-1, H)
            T = x.shape[0]
            logits = x @ gate_w.T
            scores = jax.nn.softmax(logits, axis=-1)
            topk_w, topk_idx = jax.lax.top_k(scores, K)
            topk_w = topk_w / jnp.sum(topk_w, axis=-1, keepdims=True)
            h = jnp.einsum('th,ehi->eti', x, w1)
            g = jnp.einsum('th,ehi->eti', x, w3)
            y_all = jnp.einsum('eti,eih->eth', jax.nn.silu(h) * g, w2)
            tok = jnp.arange(T)[:, None]
            y_sel = y_all[topk_idx, tok]
            y = jnp.sum(y_sel * topk_w[..., None], axis=1)
            shared = jax.nn.silu(x @ sw1) * (x @ sw3) @ sw2
            return (y + shared).reshape(hidden_states.shape)
        key = jax.random.key(seed)
        ks = jax.random.split(key, 8)
        s = 0.02
        return {'hidden_states': jax.random.normal(ks[0], (B, S, H), jnp.float32), 'gate_w': jax.random.normal(ks[1], (E, H), jnp.float32) * s, 'w1': jax.random.normal(ks[2], (E, H, I), jnp.float32) * s, 'w3': jax.random.normal(ks[3], (E, H, I), jnp.float32) * s, 'w2': jax.random.normal(ks[4], (E, I, H), jnp.float32) * s, 'sw1': jax.random.normal(ks[5], (H, SHARED_I), jnp.float32) * s, 'sw3': jax.random.normal(ks[6], (H, SHARED_I), jnp.float32) * s, 'sw2': jax.random.normal(ks[7], (SHARED_I, H), jnp.float32) * s}
    _L0_ffn_all = _L0_ffn_setup()
    _L0_ffn_in = {k: v for k, v in _L0_ffn_all.items() if k in ('gate_w', 'w1', 'w3', 'w2', 'sw1', 'sw3', 'sw2')}
    del _L0_ffn_all

    def _L1_xattn_setup():
        import jax, jax.numpy as jnp
        import numpy as np
        EPS = 1e-06
        NUM_HEADS = 16

        def _feature_map(x):
            return jnp.where(x > 0, x + 1.0, jnp.exp(x))
        key = jax.random.key(seed)
        ks = jax.random.split(key, 7)
        B, L, S, D = (4, 512, 512, 256)
        sc = 1.0 / np.sqrt(D)
        return {'query': jax.random.normal(ks[0], (B, L, D), jnp.float32), 'kv': jax.random.normal(ks[1], (B, S, D), jnp.float32), 'Wq': jax.random.normal(ks[2], (D, D), jnp.float32) * sc, 'Wg': jax.random.normal(ks[3], (D, D), jnp.float32) * sc, 'bg': jnp.ones((D,), jnp.float32), 'Wkv': jax.random.normal(ks[4], (2 * D, D), jnp.float32) * sc, 'Wo': jax.random.normal(ks[5], (D, D), jnp.float32) * sc}
    _L1_xattn_all = _L1_xattn_setup()
    _L1_xattn_in = {k: v for k, v in _L1_xattn_all.items() if k in ('Wq', 'Wg', 'bg', 'Wkv', 'Wo')}
    del _L1_xattn_all

    def _L1_ffn_setup():
        import jax, jax.numpy as jnp
        import numpy as np
        EPS = 1e-05
        TOP_K = 2

        def weight_quant(w):
            scale = 1.0 / jnp.maximum(jnp.mean(jnp.abs(w)), EPS)
            return jnp.clip(jnp.round(w * scale), -1.0, 1.0) / scale

        def activation_quant(x):
            scale = 127.0 / jnp.maximum(jnp.max(jnp.abs(x), axis=-1, keepdims=True), EPS)
            return jnp.clip(jnp.round(x * scale), -128.0, 127.0) / scale

        def bitlinear(x, w):
            w_q = w + jax.lax.stop_gradient(weight_quant(w) - w)
            x_q = x + jax.lax.stop_gradient(activation_quant(x) - x)
            return x_q @ w_q.T

        def expert_ffn(x, gw, uw, dw):
            gate = bitlinear(x, gw)
            up = bitlinear(x, uw)
            activated = up * jnp.square(jax.nn.relu(gate))
            return bitlinear(activated, dw)
        key = jax.random.key(seed)
        ks = jax.random.split(key, 5)
        B, S, H, I, E = (2, 256, 256, 512, 8)
        return {'hidden_states': jax.random.normal(ks[0], (B, S, H), dtype=jnp.float32), 'router_w': jax.random.normal(ks[1], (E, H), dtype=jnp.float32) * 0.02, 'gate_w': jax.random.normal(ks[2], (E, I, H), dtype=jnp.float32) * 0.02, 'up_w': jax.random.normal(ks[3], (E, I, H), dtype=jnp.float32) * 0.02, 'down_w': jax.random.normal(ks[4], (E, H, I), dtype=jnp.float32) * 0.02}
    _L1_ffn_all = _L1_ffn_setup()
    _L1_ffn_in = {k: v for k, v in _L1_ffn_all.items() if k in ('router_w', 'gate_w', 'up_w', 'down_w')}
    del _L1_ffn_all

    def _L2_xattn_setup():
        import jax, jax.numpy as jnp
        import numpy as np
        import math
        EMBED = 256
        HEADS = 32
        GROUPS = 8
        GROUP_HEADS = HEADS // GROUPS
        HEAD_DIM = EMBED // HEADS
        B, S = (4, 128)
        key = jax.random.key(seed)
        ks = jax.random.split(key, 8)
        sc = 0.02
        return {'q': jax.random.normal(ks[0], (B, S, EMBED), jnp.float32), 'k': jax.random.normal(ks[1], (B, S, EMBED), jnp.float32), 'v': jax.random.normal(ks[2], (B, S, EMBED), jnp.float32), 'Wq': jax.random.normal(ks[3], (EMBED, EMBED), jnp.float32) * sc, 'Wk': jax.random.normal(ks[4], (GROUPS * HEAD_DIM, EMBED), jnp.float32) * sc, 'Wv': jax.random.normal(ks[5], (GROUPS * HEAD_DIM, EMBED), jnp.float32) * sc, 'Wfc': jax.random.normal(ks[6], (EMBED, EMBED), jnp.float32) * sc, 'bfc': jnp.zeros((EMBED,), jnp.float32)}
    _L2_xattn_all = _L2_xattn_setup()
    _L2_xattn_in = {k: v for k, v in _L2_xattn_all.items() if k in ('Wq', 'Wk', 'Wv', 'Wfc', 'bfc')}
    del _L2_xattn_all

    def _L2_ffn_setup():
        import jax, jax.numpy as jnp
        import numpy as np
        NUM_ROUTED = 7
        TOP_K = 3
        D = 256
        H = 256
        B, S = (4, 256)

        def _expert_ffn(x, w1, wg, w2):
            return jax.nn.silu(x @ w1) * (x @ wg) @ w2
        key = jax.random.key(seed)
        ks = jax.random.split(key, 8)
        s = 0.02
        return {'x': jax.random.normal(ks[0], (B, S, D), jnp.float32), 'W1': jax.random.normal(ks[1], (NUM_ROUTED, D, H), jnp.float32) * s, 'Wg': jax.random.normal(ks[2], (NUM_ROUTED, D, H), jnp.float32) * s, 'W2': jax.random.normal(ks[3], (NUM_ROUTED, H, D), jnp.float32) * s, 'Ws1': jax.random.normal(ks[4], (D, H), jnp.float32) * s, 'Wsg': jax.random.normal(ks[5], (D, H), jnp.float32) * s, 'Ws2': jax.random.normal(ks[6], (H, D), jnp.float32) * s, 'gate_w': jax.random.normal(ks[7], (D, NUM_ROUTED), jnp.float32) * s, 'gate_b': jnp.zeros((NUM_ROUTED,), jnp.float32), 'biases': jnp.zeros((NUM_ROUTED,), jnp.float32)}
    _L2_ffn_all = _L2_ffn_setup()
    _L2_ffn_in = {k: v for k, v in _L2_ffn_all.items() if k in ('W1', 'Wg', 'W2', 'Ws1', 'Wsg', 'Ws2', 'gate_w', 'gate_b', 'biases')}
    del _L2_ffn_all

    def _L3_xattn_setup():
        import jax, jax.numpy as jnp
        import numpy as np
        from jax import lax
        LN_EPS = 1e-05
        key = jax.random.key(seed)
        ks = jax.random.split(key, 8)
        B, S, T, D = (4, 128, 256, 256)
        scale = 0.02
        return {'Z': jax.random.normal(ks[0], (B, S, D), dtype=jnp.float32), 'kv': jax.random.normal(ks[1], (B, T, D), dtype=jnp.float32), 'decay': jnp.float32(0.9), 'W_in': jax.random.normal(ks[2], (D, D), dtype=jnp.float32) * scale, 'b_in': jnp.zeros((D,), dtype=jnp.float32), 'W_out': jax.random.normal(ks[3], (D, D), dtype=jnp.float32) * scale, 'b_out': jnp.zeros((D,), dtype=jnp.float32), 'gamma': jnp.ones((D,), dtype=jnp.float32), 'beta': jnp.zeros((D,), dtype=jnp.float32)}
    _L3_xattn_all = _L3_xattn_setup()
    _L3_xattn_in = {k: v for k, v in _L3_xattn_all.items() if k in ('decay', 'W_in', 'b_in', 'W_out', 'b_out', 'gamma', 'beta')}
    del _L3_xattn_all

    def _L3_ffn_setup():
        import jax, jax.numpy as jnp
        import numpy as np
        EPS = 1e-05

        def activation_quant(x):
            scale = 127.0 / jnp.clip(jnp.max(jnp.abs(x), axis=-1, keepdims=True), EPS, None)
            return jnp.clip(jnp.round(x * scale), -128.0, 127.0) / scale

        def weight_quant(w):
            scale = 1.0 / jnp.clip(jnp.mean(jnp.abs(w)), EPS, None)
            return jnp.clip(jnp.round(w * scale), -1.0, 1.0) / scale

        def bitlinear(x, w):
            xq = x + jax.lax.stop_gradient(activation_quant(x) - x)
            wq = w + jax.lax.stop_gradient(weight_quant(w) - w)
            return jnp.einsum('bsd,hd->bsh', xq, wq)
        key = jax.random.key(seed)
        k1, k2, k3 = jax.random.split(key, 3)
        B, S, D, H = (4, 256, 256, 1024)
        x = jax.random.normal(k1, (B, S, D), dtype=jnp.float32)
        w1 = jax.random.normal(k2, (H, D), dtype=jnp.float32) * 0.02
        w2 = jax.random.normal(k3, (D, H), dtype=jnp.float32) * 0.02
        return {'x': x, 'w1': w1, 'w2': w2}
    _L3_ffn_all = _L3_ffn_setup()
    _L3_ffn_in = {k: v for k, v in _L3_ffn_all.items() if k in ('w1', 'w2')}
    del _L3_ffn_all
    return {'x': x, 'ctx_2048': ctx_2048, 'mask_BxS2_bk0': mask_BxS2_bk0, 'g_xattn': g_xattn, 'g_ffn': g_ffn, 'L0_ffn_gate_w': _L0_ffn_in['gate_w'], 'L0_ffn_w1': _L0_ffn_in['w1'], 'L0_ffn_w3': _L0_ffn_in['w3'], 'L0_ffn_w2': _L0_ffn_in['w2'], 'L0_ffn_sw1': _L0_ffn_in['sw1'], 'L0_ffn_sw3': _L0_ffn_in['sw3'], 'L0_ffn_sw2': _L0_ffn_in['sw2'], 'L1_xattn_Wq': _L1_xattn_in['Wq'], 'L1_xattn_Wg': _L1_xattn_in['Wg'], 'L1_xattn_bg': _L1_xattn_in['bg'], 'L1_xattn_Wkv': _L1_xattn_in['Wkv'], 'L1_xattn_Wo': _L1_xattn_in['Wo'], 'L1_ffn_router_w': _L1_ffn_in['router_w'], 'L1_ffn_gate_w': _L1_ffn_in['gate_w'], 'L1_ffn_up_w': _L1_ffn_in['up_w'], 'L1_ffn_down_w': _L1_ffn_in['down_w'], 'L2_xattn_Wq': _L2_xattn_in['Wq'], 'L2_xattn_Wk': _L2_xattn_in['Wk'], 'L2_xattn_Wv': _L2_xattn_in['Wv'], 'L2_xattn_Wfc': _L2_xattn_in['Wfc'], 'L2_xattn_bfc': _L2_xattn_in['bfc'], 'L2_ffn_W1': _L2_ffn_in['W1'], 'L2_ffn_Wg': _L2_ffn_in['Wg'], 'L2_ffn_W2': _L2_ffn_in['W2'], 'L2_ffn_Ws1': _L2_ffn_in['Ws1'], 'L2_ffn_Wsg': _L2_ffn_in['Wsg'], 'L2_ffn_Ws2': _L2_ffn_in['Ws2'], 'L2_ffn_gate_w': _L2_ffn_in['gate_w'], 'L2_ffn_gate_b': _L2_ffn_in['gate_b'], 'L2_ffn_biases': _L2_ffn_in['biases'], 'L3_xattn_decay': _L3_xattn_in['decay'], 'L3_xattn_W_in': _L3_xattn_in['W_in'], 'L3_xattn_b_in': _L3_xattn_in['b_in'], 'L3_xattn_W_out': _L3_xattn_in['W_out'], 'L3_xattn_b_out': _L3_xattn_in['b_out'], 'L3_xattn_gamma': _L3_xattn_in['gamma'], 'L3_xattn_beta': _L3_xattn_in['beta'], 'L3_ffn_w1': _L3_ffn_in['w1'], 'L3_ffn_w2': _L3_ffn_in['w2']}

def reference(x, ctx_2048, mask_BxS2_bk0, g_xattn, g_ffn, L0_ffn_gate_w, L0_ffn_w1, L0_ffn_w3, L0_ffn_w2, L0_ffn_sw1, L0_ffn_sw3, L0_ffn_sw2, L1_xattn_Wq, L1_xattn_Wg, L1_xattn_bg, L1_xattn_Wkv, L1_xattn_Wo, L1_ffn_router_w, L1_ffn_gate_w, L1_ffn_up_w, L1_ffn_down_w, L2_xattn_Wq, L2_xattn_Wk, L2_xattn_Wv, L2_xattn_Wfc, L2_xattn_bfc, L2_ffn_W1, L2_ffn_Wg, L2_ffn_W2, L2_ffn_Ws1, L2_ffn_Wsg, L2_ffn_Ws2, L2_ffn_gate_w, L2_ffn_gate_b, L2_ffn_biases, L3_xattn_decay, L3_xattn_W_in, L3_xattn_b_in, L3_xattn_W_out, L3_xattn_b_out, L3_xattn_gamma, L3_xattn_beta, L3_ffn_w1, L3_ffn_w2):
    import jax
    import jax.numpy as jnp

    def _L0_xattn_ref(hidden_states, memory_tokens, memory_mask):
        import jax, jax.numpy as jnp
        import numpy as np
        B, S, D = hidden_states.shape
        scale = 1.0 / jnp.sqrt(jnp.asarray(D, hidden_states.dtype))
        scores = jnp.einsum('bsd,bmd->bsm', hidden_states, memory_tokens) * scale
        neg_inf = jnp.asarray(-1e+30, scores.dtype)
        scores = jnp.where(memory_mask[:, None, :], scores, neg_inf)
        attn = jax.nn.softmax(scores, axis=-1)
        readout = jnp.einsum('bsm,bmd->bsd', attn, memory_tokens)
        valid_b = jnp.any(memory_mask, axis=-1)
        out = jnp.where(valid_b[:, None, None], readout, jnp.zeros_like(readout))
        return out

    def _L0_ffn_ref(hidden_states, gate_w, w1, w3, w2, sw1, sw3, sw2):
        import jax, jax.numpy as jnp
        import numpy as np
        B, S, H = (2, 256, 256)
        E, I, K = (8, 176, 2)
        SHARED_I = 176 * 2

        def _moe_forward(hidden_states, gate_w, w1, w3, w2, sw1, sw3, sw2):
            x = hidden_states.reshape(-1, H)
            T = x.shape[0]
            logits = x @ gate_w.T
            scores = jax.nn.softmax(logits, axis=-1)
            topk_w, topk_idx = jax.lax.top_k(scores, K)
            topk_w = topk_w / jnp.sum(topk_w, axis=-1, keepdims=True)
            h = jnp.einsum('th,ehi->eti', x, w1)
            g = jnp.einsum('th,ehi->eti', x, w3)
            y_all = jnp.einsum('eti,eih->eth', jax.nn.silu(h) * g, w2)
            tok = jnp.arange(T)[:, None]
            y_sel = y_all[topk_idx, tok]
            y = jnp.sum(y_sel * topk_w[..., None], axis=1)
            shared = jax.nn.silu(x @ sw1) * (x @ sw3) @ sw2
            return (y + shared).reshape(hidden_states.shape)
        return _moe_forward(hidden_states, gate_w, w1, w3, w2, sw1, sw3, sw2)

    def _L1_xattn_ref(query, kv, Wq, Wg, bg, Wkv, Wo):
        import jax, jax.numpy as jnp
        import numpy as np
        EPS = 1e-06
        NUM_HEADS = 16

        def _feature_map(x):
            return jnp.where(x > 0, x + 1.0, jnp.exp(x))
        B, L, D = query.shape
        S = kv.shape[1]
        H = NUM_HEADS
        hd = D // H
        q = query @ Wq.T
        gate = jax.nn.sigmoid(query @ Wg.T + bg)
        kvp = kv @ Wkv.T
        k, v = jnp.split(kvp, 2, axis=-1)
        q = _feature_map(q.reshape(B, L, H, hd).transpose(0, 2, 1, 3))
        k = _feature_map(k.reshape(B, S, H, hd).transpose(0, 2, 1, 3))
        v = v.reshape(B, S, H, hd).transpose(0, 2, 1, 3)
        kv_summary = jnp.einsum('bhsd,bhse->bhde', k, v)
        k_sum = k.sum(axis=-2)
        z = 1.0 / (jnp.einsum('bhld,bhd->bhl', q, k_sum)[..., None] + EPS)
        attn = jnp.einsum('bhld,bhde->bhle', q, kv_summary) * z
        attn = attn.transpose(0, 2, 1, 3).reshape(B, L, D)
        out = attn * gate @ Wo.T
        return out

    def _L1_ffn_ref(hidden_states, router_w, gate_w, up_w, down_w):
        import jax, jax.numpy as jnp
        import numpy as np
        EPS = 1e-05
        TOP_K = 2

        def weight_quant(w):
            scale = 1.0 / jnp.maximum(jnp.mean(jnp.abs(w)), EPS)
            return jnp.clip(jnp.round(w * scale), -1.0, 1.0) / scale

        def activation_quant(x):
            scale = 127.0 / jnp.maximum(jnp.max(jnp.abs(x), axis=-1, keepdims=True), EPS)
            return jnp.clip(jnp.round(x * scale), -128.0, 127.0) / scale

        def bitlinear(x, w):
            w_q = w + jax.lax.stop_gradient(weight_quant(w) - w)
            x_q = x + jax.lax.stop_gradient(activation_quant(x) - x)
            return x_q @ w_q.T

        def expert_ffn(x, gw, uw, dw):
            gate = bitlinear(x, gw)
            up = bitlinear(x, uw)
            activated = up * jnp.square(jax.nn.relu(gate))
            return bitlinear(activated, dw)
        B, S, H = hidden_states.shape
        E = router_w.shape[0]
        x = hidden_states.reshape(-1, H)
        logits = x @ router_w.T
        probs = jax.nn.softmax(logits, axis=-1)
        top_w, top_i = jax.lax.top_k(probs, TOP_K)
        top_w = top_w / jnp.sum(top_w, axis=-1, keepdims=True)
        combine = jnp.sum(top_w[..., None] * jax.nn.one_hot(top_i, E, dtype=x.dtype), axis=1)
        out = jnp.zeros_like(x)
        for e in range(E):
            y_e = expert_ffn(x, gate_w[e], up_w[e], down_w[e])
            out = out + combine[:, e:e + 1] * y_e
        return out.reshape(B, S, H)

    def _L2_xattn_ref(q, k, v, Wq, Wk, Wv, Wfc, bfc):
        import jax, jax.numpy as jnp
        import numpy as np
        import math
        EMBED = 256
        HEADS = 32
        GROUPS = 8
        GROUP_HEADS = HEADS // GROUPS
        HEAD_DIM = EMBED // HEADS
        B, S = (4, 128)
        N, S_, _ = q.shape
        qh = (q @ Wq.T).reshape(N, S_, HEADS, HEAD_DIM).transpose(0, 2, 1, 3)
        kh = (k @ Wk.T).reshape(N, S_, GROUPS, HEAD_DIM).transpose(0, 2, 1, 3)
        vh = (v @ Wv.T).reshape(N, S_, GROUPS, HEAD_DIM).transpose(0, 2, 1, 3)
        kh = jnp.repeat(kh, GROUP_HEADS, axis=1)
        vh = jnp.repeat(vh, GROUP_HEADS, axis=1)
        score = jnp.einsum('bhqd,bhkd->bhqk', qh, kh) / math.sqrt(HEAD_DIM)
        attn = jax.nn.softmax(score, axis=-1)
        out = jnp.einsum('bhqk,bhkd->bhqd', attn, vh)
        out = out.transpose(0, 2, 1, 3).reshape(N, S_, EMBED)
        return out @ Wfc.T + bfc

    def _L2_ffn_ref(x, W1, Wg, W2, Ws1, Wsg, Ws2, gate_w, gate_b, biases):
        import jax, jax.numpy as jnp
        import numpy as np
        NUM_ROUTED = 7
        TOP_K = 3
        D = 256
        H = 256
        B, S = (4, 256)

        def _expert_ffn(x, w1, wg, w2):
            return jax.nn.silu(x @ w1) * (x @ wg) @ w2
        output = _expert_ffn(x, Ws1, Wsg, Ws2)
        gate_logits = x @ gate_w + gate_b
        gate_probas = jax.nn.softmax(gate_logits, axis=-1)
        biased_probas = gate_probas + biases
        _, topk_idxs = jax.lax.top_k(biased_probas, TOP_K)
        topk_probas = jnp.take_along_axis(gate_probas, topk_idxs, axis=-1)
        topk_probas = topk_probas / jnp.sum(topk_probas, axis=-1, keepdims=True)
        for e in range(NUM_ROUTED):
            w_e = jnp.sum(topk_probas * (topk_idxs == e), axis=-1)
            output = output + _expert_ffn(x, W1[e], Wg[e], W2[e]) * w_e[..., None]
        return output

    def _L3_xattn_ref(Z, kv, decay, W_in, b_in, W_out, b_out, gamma, beta):
        import jax, jax.numpy as jnp
        import numpy as np
        from jax import lax
        LN_EPS = 1e-05
        B, T, D = kv.shape
        K = jax.nn.sigmoid(decay)
        x = jnp.einsum('btd,ed->bte', kv, W_in) + b_in

        def scan_fn(s, xt):
            s = K * s + xt
            return (s, s)
        s0 = jnp.zeros((B, D), dtype=kv.dtype)
        _, states = lax.scan(scan_fn, s0, jnp.swapaxes(x, 0, 1))
        states = jnp.swapaxes(states, 0, 1)
        proj = jnp.einsum('btd,ed->bte', states, W_out) + b_out
        summary = jnp.mean(proj, axis=1, keepdims=True)
        y = Z + summary
        mu = jnp.mean(y, axis=-1, keepdims=True)
        var = jnp.mean((y - mu) ** 2, axis=-1, keepdims=True)
        return (y - mu) / jnp.sqrt(var + LN_EPS) * gamma + beta

    def _L3_ffn_ref(x, w1, w2):
        import jax, jax.numpy as jnp
        import numpy as np
        EPS = 1e-05

        def activation_quant(x):
            scale = 127.0 / jnp.clip(jnp.max(jnp.abs(x), axis=-1, keepdims=True), EPS, None)
            return jnp.clip(jnp.round(x * scale), -128.0, 127.0) / scale

        def weight_quant(w):
            scale = 1.0 / jnp.clip(jnp.mean(jnp.abs(w)), EPS, None)
            return jnp.clip(jnp.round(w * scale), -1.0, 1.0) / scale

        def bitlinear(x, w):
            xq = x + jax.lax.stop_gradient(activation_quant(x) - x)
            wq = w + jax.lax.stop_gradient(weight_quant(w) - w)
            return jnp.einsum('bsd,hd->bsh', xq, wq)
        h = bitlinear(x, w1)
        h = jax.nn.gelu(h, approximate=False)
        return bitlinear(h, w2)
    x = x + jnp.tanh(g_xattn[0]) * _L0_xattn_ref(_layernorm(x, axis=-1), ctx_2048, mask_BxS2_bk0)
    x = x + jnp.tanh(g_ffn[0]) * _L0_ffn_ref(_layernorm(x, axis=-1), L0_ffn_gate_w, L0_ffn_w1, L0_ffn_w3, L0_ffn_w2, L0_ffn_sw1, L0_ffn_sw3, L0_ffn_sw2)
    x = x + jnp.tanh(g_xattn[1]) * _L1_xattn_ref(_layernorm(x, axis=-1), ctx_2048, L1_xattn_Wq, L1_xattn_Wg, L1_xattn_bg, L1_xattn_Wkv, L1_xattn_Wo)
    x = x + jnp.tanh(g_ffn[1]) * _L1_ffn_ref(_layernorm(x, axis=-1), L1_ffn_router_w, L1_ffn_gate_w, L1_ffn_up_w, L1_ffn_down_w)
    x = x + jnp.tanh(g_xattn[2]) * _L2_xattn_ref(_layernorm(x, axis=-1), ctx_2048, ctx_2048, L2_xattn_Wq, L2_xattn_Wk, L2_xattn_Wv, L2_xattn_Wfc, L2_xattn_bfc)
    x = x + jnp.tanh(g_ffn[2]) * _L2_ffn_ref(_layernorm(x, axis=-1), L2_ffn_W1, L2_ffn_Wg, L2_ffn_W2, L2_ffn_Ws1, L2_ffn_Wsg, L2_ffn_Ws2, L2_ffn_gate_w, L2_ffn_gate_b, L2_ffn_biases)
    x = x + jnp.tanh(g_xattn[3]) * _L3_xattn_ref(_layernorm(x, axis=-1), ctx_2048, L3_xattn_decay, L3_xattn_W_in, L3_xattn_b_in, L3_xattn_W_out, L3_xattn_b_out, L3_xattn_gamma, L3_xattn_beta)
    x = x + jnp.tanh(g_ffn[3]) * _L3_ffn_ref(_layernorm(x, axis=-1), L3_ffn_w1, L3_ffn_w2)
    return x

_drawn_inputs = setup_inputs


def setup_inputs(seed=0):
    import zlib

    import numpy as np

    out = dict(_drawn_inputs(seed))
    spreads = {'L1_xattn_bg': (1.0, 0.6),
     'L2_xattn_bfc': (0.0, 0.8),
     'L2_ffn_gate_b': (0.0, 0.8),
     'L2_ffn_biases': (0.0, 0.8),
     'L3_xattn_b_in': (0.0, 0.8),
     'L3_xattn_b_out': (0.0, 0.8),
     'L3_xattn_gamma': (1.0, 0.6),
     'L3_xattn_beta': (0.0, 0.8)}
    factors = {'g_ffn': 8.0,
     'L0_ffn_gate_w': 8.0,
     'L0_ffn_w1': 8.0,
     'L0_ffn_w3': 8.0,
     'L0_ffn_w2': 8.0,
     'L0_ffn_sw1': 4.881,
     'L0_ffn_sw3': 4.84,
     'L0_ffn_sw2': 4.828,
     'L1_xattn_Wq': 4.81,
     'L1_ffn_router_w': 8.0,
     'L1_ffn_gate_w': 8.0,
     'L1_ffn_up_w': 8.0,
     'L1_ffn_down_w': 8.0,
     'L2_xattn_Wq': 64.0,
     'L2_xattn_Wk': 64.0,
     'L2_ffn_W1': 8.0,
     'L2_ffn_Wg': 8.0,
     'L2_ffn_W2': 8.0,
     'L2_ffn_Ws1': 5.454,
     'L2_ffn_Wsg': 5.49,
     'L2_ffn_Ws2': 5.418,
     'L2_ffn_gate_w': 8.0,
     'L2_xattn_Wv': 8.0,
     'L2_xattn_Wfc': 8.0,
     'L3_xattn_W_in': 7.234,
     'L3_xattn_W_out': 6.173,
     'L3_ffn_w1': 8.0,
     'L3_ffn_w2': 8.0}
    for name, (base, spread) in spreads.items():
        noise = np.random.default_rng([zlib.crc32(name.encode()), seed]).standard_normal(out[name].shape)
        drawn = base * np.exp(spread * noise) if base else spread * noise
        out[name] = jnp.asarray(drawn.astype(out[name].dtype))
    for name, factor in factors.items():
        out[name] = (out[name] * factor).astype(out[name].dtype)
    return out
```

```python
from contextlib import ExitStack

import numpy as np

import concourse.bass as bass
from concourse import mybir

ACT = mybir.ActivationFunctionType
ALU = mybir.AluOpType
AX = mybir.AxisListType
F32 = mybir.dt.float32
F32R = mybir.dt.float32r
BF16 = mybir.dt.bfloat16
U8 = mybir.dt.uint8
ds = bass.ds

P = 128
D = 256
DC = D // P
BATCH, SEQ = 32, 64
TOK = BATCH * SEQ
TILES = TOK // P
BT = 4
BLK = BT * P
BLOCKS = TILES // BT
LN_EPS = 1e-5
QUANT_EPS = 1e-5
MAGIC = 1.5 * 2.0 ** 23
L0_I = 176
PAIR = 2 * L0_I + 16
RAW = 4096
SPLIT = 2 * DC * 3 * P + 3 * D
SYNC, GPSIMD, SCALAR, VECTOR, TENSOR = range(5)
WORK = 19600
L3_ATTENTION = 6600


class Names:
    pass


def build_program(nc, io):
    ctx = ExitStack()
    with ctx:
        def sb(name, shape, dt=F32):
            return ctx.enter_context(nc.sbuf_tensor(name, shape, dt))

        def sem(name):
            return ctx.enter_context(nc.semaphore(name))

        def sems(prefix, names):
            return [sem(prefix + "_" + name) for name in names.split()]

        X = sb("resid", [P, TILES, D])
        ident = sb("ident", [P, P])
        identb = sb("identb", [P, P], BF16)
        ones = sb("ones", [P, P])
        neg_half = sb("neg_half", [P, BT])
        magic = sb("magic", [P, 1])
        gates = sb("gates", [P, 8])
        xn = sb("xn", [P, BT, D])
        ln_stat = sb("ln_stat", [P, BT, 6])
        ln_mv = sb("ln_mv", [P, BT, 2])
        ln_ve = sb("ln_ve", [P, BT])
        ln_rstd = sb("ln_rstd", [P, BT])
        xhi = sb("xhi", [P, DC, TOK], F32R)
        xlo = sb("xlo", [P, DC, TOK], F32R)
        ctx_in = sb("ctx_in", [P, BT, D])
        ctx_sb = sb("ctx_sb", [P, BT, D])
        work = sb("work", [P, WORK])
        raw = sb("raw", [P, RAW])
        whi = sb("whi", [P, 2, SPLIT], F32R)
        wlo = sb("wlo", [P, 2, SPLIT], F32R)
        ahi = sb("ahi", [P, 2, BLK], F32R)
        alo = sb("alo", [P, 2, BLK], F32R)
        route_hi = sb("route_hi", [P, DC, P], F32R)
        route_lo = sb("route_lo", [P, DC, P], F32R)
        bank = [ctx.enter_context(nc.psum_tensor(f"bank{i}", [P, 512], F32)) for i in range(8)]

        class Layout:

            def __init__(self):
                self.at = 0

            def __call__(self, *shape, dt=F32):
                n = int(np.prod(shape))
                n32 = n if dt == F32 else (n + 1) // 2
                v = work[:, self.at:self.at + n32]
                self.at += n32
                assert self.at <= WORK, self.at
                if dt != F32:
                    v = v.bitcast(dt)
                if len(shape) == 2:
                    v = v.rearrange("p (a b) -> p a b", a=shape[0])
                if len(shape) == 3:
                    v = v.rearrange("p (a b c) -> p a b c", a=shape[0], b=shape[1])
                if len(shape) == 4:
                    v = v.rearrange("p (a b c d) -> p a b c d", a=shape[0], b=shape[1], c=shape[2])
                return v

        def flat(ap):
            return ap.rearrange("p a b -> p (a b)")

        def x_tile(t):
            return flat(X[:, ds(t, 1), :])

        def block_of(dram, i):
            v = dram.rearrange("b s d -> (b s) d").rearrange("(i k p) d -> i p k d", k=BT, p=P)
            return v[ds(i, 1)].rearrange("o p k d -> p (o k) d")

        passed = sem("passed")

        def hold(eng, s, value):
            eng.wait_ge(s, value)
            eng.sem_inc(passed, 1)

        def linker(eng, s, base=0):
            count = [0]

            def link(ins):
                ins.then_inc(s, 1)
                count[0] += 1
                eng.wait_ge(s, base + count[0])
            link.count = count
            return link

        weight = Names()
        weight.loaded, weight.turned, weight.ready = sems("weight", "loaded turned ready")
        weight_counts = [(0, 0, 0)]

        def count_weights(loaded, turned, ready):
            was = Names()
            was.loaded, was.turned, was.ready = weight_counts[-1]
            weight_counts.append((was.loaded + loaded, was.turned + turned, was.ready + ready))
            return was

        x_loaded, g_loaded = sem("x_loaded"), sem("g_loaded")
        const_set, gates_set, ident_set = sem("const_set"), sem("gates_set"), sem("ident_set")

        def setup_sync(sp):
            for i in range(BLOCKS):
                sp.dma_start(X[:, BT * i:BT * i + BT, :], block_of(io["x"], i)).then_inc(x_loaded, 16)
            sp.dma_start(gates[:, 0:4], io["g_xattn"].partition_broadcast(P)).then_inc(g_loaded, 16)
            sp.dma_start(gates[:, 4:8], io["g_ffn"].partition_broadcast(P)).then_inc(g_loaded, 16)

        def setup_gpsimd(pool):
            pool.memset(ident[:, :], 0.0).then_inc(const_set, 1)
            pool.memset(ones[:, :], 1.0).then_inc(const_set, 1)
            pool.memset(neg_half[:, :], -0.5).then_inc(const_set, 1)
            pool.memset(magic[:, :], MAGIC).then_inc(const_set, 1)
            pool.wait_ge(const_set, 4)
            pool.affine_select(out=ident[:, :], in_=ident[:, :], compare_op=ALU.not_equal, fill=1.0, base=0,
                               pattern=[[-1, P]], channel_multiplier=1).then_inc(ident_set, 1)
            pool.wait_ge(ident_set, 1)
            pool.tensor_copy(identb[:, :], ident[:, :]).then_inc(ident_set, 1)

        def setup_scalar(act):
            act.wait_ge(g_loaded, 32)
            act.activation(gates[:, :], gates[:, :], ACT.Tanh).then_inc(gates_set, 1)

        def setup_vector(dve):
            dve.wait_ge(x_loaded, 16 * BLOCKS)
            dve.wait_ge(gates_set, 1)

        def setup_tensor(pe):
            pe.wait_ge(ident_set, 2)

        norm_sems = sems("norm", "stat rstd xn tp hi lo")

        def make_norm(sublayer, parts=None, split=None):
            n = Names()
            n.stat, n.rstd, n.xn, n.tp, n.hi, n.lo = norm_sems
            n.first = sublayer * BLOCKS
            n.first_lo = (split or 0) * BLOCKS

            def vector_norm(dve, i):
                g = n.first + i
                for k in range(BT):
                    dve.bn_stats(ln_stat[:, k, :], x_tile(i * BT + k)).then_inc(n.stat, 1)
                hold(dve, n.stat, g * 2 * BT + BT)
                for k in range(BT):
                    dve.bn_aggr(ln_mv[:, k, :], ln_stat[:, k, :]).then_inc(n.stat, 1)
                dve.wait_ge(n.rstd, g * 2 + 2)
                for k in range(BT):
                    dve.tensor_scalar(xn[:, k, :], x_tile(i * BT + k), ln_mv[:, k, 0:1], ln_rstd[:, k:k + 1],
                                      ALU.subtract, ALU.mult).then_inc(n.xn, 1)

            def vector_rest(dve, i):
                for c in range(DC):
                    dve.wait_ge(n.hi, (n.first + i) * DC + c + 1)
                    dve.tensor_tensor(flat(xlo[:, c:c + 1, ds(i * BLK, BLK)]), bank[c][:, :],
                                      flat(xhi[:, c:c + 1, ds(i * BLK, BLK)]).bitcast(F32),
                                      ALU.subtract).then_inc(n.lo, 1)

            def gpsimd(pool, i):
                g = n.first + i
                hold(pool, n.stat, g * 2 * BT + 2 * BT)
                pool.tensor_scalar(ln_ve[:, :], ln_mv[:, :, 1], LN_EPS, 1.0, ALU.add, ALU.mult).then_inc(n.rstd, 1)
                pool.wait_ge(n.rstd, g * 2 + 1)
                pool.tensor_tensor(ln_rstd[:, :], ln_ve[:, :], neg_half[:, :], ALU.pow).then_inc(n.rstd, 1)

            def tensor(pe, i):
                for c in range(DC):
                    for k in range(BT):
                        if c == 0:
                            pe.wait_ge(n.xn, (n.first + i) * BT + k + 1)
                        tp = pe.transpose(bank[c][:, k * P:(k + 1) * P], xn[:, k, c * P:(c + 1) * P], ident[:, :])
                    tp.then_inc(n.tp, 1)

            def scalar(act, i):
                for c in range(DC):
                    act.wait_ge(n.tp, (n.first + i) * DC + c + 1)
                    to = flat(xhi[:, c:c + 1, ds(i * BLK, BLK)]) if parts is None else parts[:, c, :]
                    act.activation(to, bank[c][:, :], ACT.Copy).then_inc(n.hi, 1)

            n.vector_norm, n.vector_rest, n.gpsimd, n.tensor, n.scalar = vector_norm, vector_rest, gpsimd, tensor, scalar
            return n

        ctx_sems = sems("ctx", "arrived in_free ready free tp turned")

        def make_context(use, dst):
            n = Names()
            n.arrived, n.in_free, n.ready, n.free, n.tp, n.turned = ctx_sems
            n.first = use * BLOCKS

            def sync(sp):
                with sp.Fori(0, BLOCKS) as i:
                    sp.wait_ge(n.in_free, n.first + i + 1)
                    sp.dma_start(ctx_in[:, :, :], block_of(io["ctx_2048"], i)).then_inc(n.arrived, 16)

            def gpsimd_first(pool):
                if use == 0:
                    pool.sem_inc(n.in_free, 1)

            def gpsimd(pool, i):
                g = n.first + i
                hold(pool, n.arrived, g * 16 + 16)
                hold(pool, n.free, g + 1)
                pool.tensor_copy(ctx_sb[:, :, :], ctx_in[:, :, :]).then_inc(n.ready, 1)
                pool.wait_ge(n.ready, g + 1)
                pool.sem_inc(n.in_free, 1)

            def tensor_first(pe):
                if use == 0:
                    pe.sem_inc(n.free, 1)

            def tensor(pe, i):
                pe.wait_ge(n.ready, n.first + i + 1)
                for c in range(DC):
                    for k in range(BT):
                        tp = pe.transpose(bank[2 + c][:, k * P:(k + 1) * P], ctx_sb[:, k, c * P:(c + 1) * P], ident[:, :])
                    tp.then_inc(n.tp, 1)

            def scalar(act, i):
                for c in range(DC):
                    act.wait_ge(n.tp, (n.first + i) * DC + c + 1)
                    act.activation(dst[:, c, :], bank[2 + c][:, :], ACT.Copy).then_inc(n.turned, 1)

            n.sync, n.gpsimd_first, n.gpsimd, n.tensor_first, n.tensor, n.scalar = sync, gpsimd_first, gpsimd, tensor_first, tensor, scalar
            return n

        def layer0_attention(before, done):
            lay = Layout()
            xT, cT = lay(DC, BLK), lay(DC, BLK)
            same_batch = lay(P)
            mask = lay(BT, P)
            mask_low = lay(BT, P)
            seen = lay(BT)
            score, prob, probT = lay(BT, P), lay(BT, P), lay(BT, P)
            neg_max, total, inv, scale = lay(BT), lay(BT), lay(BT), lay(BT)
            mask_in = sb("mask_in", [P, TILES, P], U8)
            norm = make_norm(0, xT)
            cx = make_context(0, cT)
            s = Names()
            s.mask_in, s.same, s.mask, s.score, s.soft, s.exp, s.probT_ps, s.probT, s.out, s.x = sems("a0", "mask_in same mask score soft exp probT_ps probT out x")
            SOFT = 5

            def sync(sp):
                sp.dma_start(mask_in[:, :, :].rearrange("p t k -> p (t k)"),
                             io["mask_BxS2_bk0"].rearrange("b s -> (b s)").partition_broadcast(P)).then_inc(s.mask_in, 16)
                cx.sync(sp)

            def gpsimd(pool):
                same3 = same_batch.rearrange("p (h j) -> p h j", h=2)
                pool.memset(same_batch, 1.0).then_inc(s.same, 1)
                pool.wait_ge(s.same, 1)
                pool.affine_select(out=same3, in_=same3, compare_op=ALU.is_ge, fill=0.0, base=0,
                                   pattern=[[-SEQ, 2], [0, SEQ]], channel_multiplier=1).then_inc(s.same, 1)
                pool.wait_ge(s.same, 2)
                pool.affine_select(out=same3, in_=same3, compare_op=ALU.is_ge, fill=0.0, base=SEQ - 1,
                                   pattern=[[SEQ, 2], [0, SEQ]], channel_multiplier=-1).then_inc(s.same, 1)
                cx.gpsimd_first(pool)
                with pool.Fori(0, BLOCKS) as i:
                    cx.gpsimd(pool, i)
                    norm.gpsimd(pool, i)

            def scalar(act):
                with act.Fori(0, BLOCKS) as i:
                    cx.scalar(act, i)
                    norm.scalar(act, i)
                    act.wait_ge(s.soft, i * SOFT + SOFT)
                    for k in range(BT):
                        act.activation(prob[:, k, :], score[:, k, :], ACT.Exp, bias=neg_max[:, k:k + 1],
                                       accum_out=total[:, k:k + 1]).then_inc(s.exp, 1)
                    act.wait_ge(s.probT_ps, i + 1)
                    act.activation(flat(probT), bank[5][:, :], ACT.Copy).then_inc(s.probT, 1)

            def vector(dve):
                dve.wait_ge(s.mask_in, 16)
                dve.wait_ge(s.same, 3)
                with dve.Fori(0, BLOCKS) as i:
                    norm.vector_norm(dve, i)
                    dve.tensor_tensor(mask, mask_in[:, ds(i * BT, BT), :], same_batch.unsqueeze(1).to_broadcast([P, BT, P]),
                                      ALU.mult).then_inc(s.soft, 1)
                    dve.wait_ge(s.soft, i * SOFT + 1)
                    dve.tensor_scalar(flat(mask_low), flat(mask), 1e30, -1e30, ALU.mult, ALU.add).then_inc(s.soft, 1)
                    dve.tensor_reduce(seen, mask, AX.X, ALU.max).then_inc(s.mask, 1)
                    dve.wait_ge(s.score, i + 1)
                    dve.scalar_tensor_tensor(flat(score), bank[4][:, :], D ** -0.5, flat(mask), ALU.mult, ALU.mult).then_inc(s.soft, 1)
                    dve.wait_ge(s.soft, i * SOFT + 3)
                    dve.tensor_tensor(flat(score), flat(score), flat(mask_low), ALU.add).then_inc(s.soft, 1)
                    dve.wait_ge(s.soft, i * SOFT + 4)
                    dve.tensor_reduce(neg_max, score, AX.X, ALU.max, negate=True).then_inc(s.soft, 1)
                    dve.wait_ge(s.exp, i * BT + BT)
                    dve.reciprocal(inv, total).then_inc(s.mask, 1)
                    dve.wait_ge(s.mask, i * 3 + 2)
                    dve.scalar_tensor_tensor(scale, inv, gates[:, 0:1], seen, ALU.mult, ALU.mult).then_inc(s.mask, 1)
                    dve.wait_ge(s.mask, i * 3 + 3)
                    for k in range(BT):
                        if k % 2 == 0:
                            dve.wait_ge(s.out, i * 2 + k // 2 + 1)
                        dve.scalar_tensor_tensor(x_tile(i * BT + k), bank[6 + k // 2][:, k % 2 * D:k % 2 * D + D],
                                                 scale[:, k:k + 1], x_tile(i * BT + k), ALU.mult, ALU.add).then_inc(done, 1)

            def tensor(pe):
                cx.tensor_first(pe)
                with pe.Fori(0, BLOCKS) as i:
                    cx.tensor(pe, i)
                    norm.tensor(pe, i)
                    pe.wait_ge(cx.turned, (cx.first + i) * DC + DC)
                    pe.wait_ge(norm.hi, (norm.first + i) * DC + DC)
                    for k in range(BT):
                        t = slice(k * P, (k + 1) * P)
                        for c in range(DC):
                            mm = pe.matmul(bank[4][:, t], xT[:, c, t], cT[:, c, t], start=c == 0, stop=c == DC - 1)
                    mm.then_inc(s.score, 1)
                    for k in range(BT):
                        pe.wait_ge(s.exp, i * BT + k + 1)
                        tp = pe.transpose(bank[5][:, k * P:(k + 1) * P], prob[:, k, :], ident[:, :])
                    tp.then_inc(s.probT_ps, 1)
                    pe.wait_ge(s.probT, i + 1)
                    for k in range(BT):
                        mm = pe.matmul(bank[6 + k // 2][:, k % 2 * D:k % 2 * D + D], probT[:, k, :], ctx_sb[:, k, :],
                                       start=True, stop=True)
                        if k % 2:
                            mm.then_inc(s.out, 1)
                    pe.wait_ge(s.out, i * 2 + 2)
                    pe.sem_inc(cx.free, 1)

            return sync, gpsimd, scalar, vector, tensor

        route_sems = sems("route", "loaded zeroed w_tp w logits_ps logitsT turned_ps kept chain soft exp")
        route_counts = [(0, 0)]

        def make_router(name, use, lay, scratch, experts, top, gate, w_rows, dram_w, dram_b=None, dram_bias=None):
            r = Names()
            r.loaded, r.zeroed, r.w_tp, r.w, r.logits_ps, r.logitsT, r.turned_ps, r.kept, r.chain, r.soft, r.exp = route_sems
            first_block = use * BLOCKS
            E = experts
            w_in = sb(f"{name}_win", [P, D] if w_rows else [P, DC, E])
            w_hi, w_lo = route_hi, route_lo
            logitsT = lay(BLK)
            r.logits, prob, key = lay(TILES, E), lay(TILES, E), lay(TILES, E)
            small, inv = lay(TILES), lay(TILES)
            pairs = TILES * E * E
            beats, ties = [scratch[:, j * pairs:(j + 1) * pairs].rearrange("p (t a b) -> p t a b", t=TILES, a=E) for j in range(2)]
            earlier = sb(f"{name}_earlier", [P, E, E])
            rank = lay(TILES, E)
            r.shares = lay(E + 1, TILES)
            bias_in = sb(f"{name}_bias", [P, 2, E])
            extra = (dram_b is not None) + (dram_bias is not None)
            loaded0, chain0 = route_counts[-1]
            loads = loaded0 + 16 * ((1 if w_rows else DC) + extra)
            route_counts.append((loads, chain0 + 17 + extra))

            def sync(sp):
                if w_rows:
                    sp.dma_start(w_in[0:E, :], dram_w).then_inc(r.loaded, 16)
                else:
                    for c in range(DC):
                        sp.dma_start(w_in[:, c, :], dram_w[c * P:(c + 1) * P, :]).then_inc(r.loaded, 16)
                if dram_b is not None:
                    sp.dma_start(bias_in[:, 0, :], dram_b.partition_broadcast(P)).then_inc(r.loaded, 16)
                if dram_bias is not None:
                    sp.dma_start(bias_in[:, 1, :], dram_bias.partition_broadcast(P)).then_inc(r.loaded, 16)

            def gpsimd(pool):
                pool.memset(earlier[:, :, :], 1.0).then_inc(r.zeroed, 1)
                pool.wait_ge(r.zeroed, use * 2 + 1)
                pool.affine_select(out=earlier[:, :, :], in_=earlier[:, :, :], compare_op=ALU.is_gt, fill=0.0, base=0,
                                   pattern=[[1, E], [-1, E]], channel_multiplier=0).then_inc(r.zeroed, 1)

            def vector_weights(dve):
                dve.memset(w_hi[:, :, :].bitcast(F32), 0.0).then_inc(r.w, 1)
                dve.memset(w_lo[:, :, :].bitcast(F32), 0.0).then_inc(r.w, 1)
                dve.wait_ge(r.loaded, loads)
                dve.wait_ge(r.w, use * 4 + 2)
                if w_rows:
                    dve.wait_ge(r.w_tp, use + 1)
                    src = bank[4][:, 0:DC * E].rearrange("p (c e) -> p c e", c=DC)
                else:
                    src = w_in[:, :, :]
                dve.tensor_copy(w_hi[:, :, 0:E], src).then_inc(r.w, 1)
                dve.wait_ge(r.w, use * 4 + 3)
                dve.tensor_tensor(w_lo[:, :, 0:E], src, w_hi[:, :, 0:E].bitcast(F32), ALU.subtract).then_inc(r.w, 1)

            def tensor_weights(pe):
                if w_rows:
                    pe.wait_ge(r.loaded, loads)
                    for c in range(DC):
                        tp = pe.transpose(bank[4][:, c * E:(c + 1) * E], w_in[0:E, c * P:(c + 1) * P], ident[0:E, 0:E])
                    tp.then_inc(r.w_tp, 1)
                pe.wait_ge(r.w, use * 4 + 4)

            def tensor(pe, norm, i):
                pe.wait_ge(norm.lo, (norm.first_lo + i) * DC + DC)
                n = 0
                for c in range(DC):
                    for w, x in ((w_hi, xhi), (w_hi, xlo), (w_lo, xhi)):
                        mm = pe.matmul(bank[4][:, :], w[:, c, :], flat(x[:, c:c + 1, ds(i * BLK, BLK)]), start=n == 0, stop=n == 5)
                        n += 1
                mm.then_inc(r.logits_ps, 1)
                hold(pe, r.logitsT, first_block + i + 1)
                for k in range(BT):
                    tp = pe.transpose(bank[5][:, k * E:(k + 1) * E], logitsT[0:E, k * P:(k + 1) * P], ident[0:E, 0:E])
                tp.then_inc(r.turned_ps, 1)

            def scalar(act, i):
                act.wait_ge(r.logits_ps, first_block + i + 1)
                act.activation(logitsT[0:E, :], bank[4][0:E, :], ACT.Copy).then_inc(r.logitsT, 1)
                act.wait_ge(r.turned_ps, first_block + i + 1)
                act.activation(r.logits[:, ds(i * BT, BT), :], bank[5][:, 0:BT * E].rearrange("p (k e) -> p k e", k=BT),
                               ACT.Copy).then_inc(r.kept, 1)
            r.all_kept = first_block + BLOCKS

            def scalar_last(act):
                act.wait_ge(r.soft, use + 1)
                act.activation(prob, r.logits, ACT.Exp).then_inc(r.exp, 1)

            def over(v):
                return v.unsqueeze(2).to_broadcast([P, TILES, E])

            def vector_last(dve):
                dve.wait_ge(r.kept, r.all_kept)
                dve.wait_ge(r.zeroed, use * 2 + 2)
                link = linker(dve, r.chain, chain0)
                if dram_b is not None:
                    link(dve.tensor_tensor(r.logits, r.logits, bias_in[:, 0:1, :].to_broadcast([P, TILES, E]), ALU.add))
                link(dve.tensor_reduce(small, r.logits, AX.X, ALU.max))
                dve.tensor_tensor(r.logits, r.logits, over(small), ALU.subtract).then_inc(r.soft, 1)
                dve.wait_ge(r.exp, use + 1)
                link(dve.tensor_reduce(small, prob, AX.X, ALU.add))
                link(dve.reciprocal(inv, small))
                link(dve.tensor_tensor(prob, prob, over(inv), ALU.mult))
                rated = prob
                if dram_bias is not None:
                    link(dve.tensor_tensor(key, prob, bias_in[:, 1:2, :].to_broadcast([P, TILES, E]), ALU.add))
                    rated = key
                other = rated.unsqueeze(2).to_broadcast([P, TILES, E, E])
                own = rated.unsqueeze(3).to_broadcast([P, TILES, E, E])
                link(dve.tensor_tensor(beats, other, own, ALU.is_gt))
                link(dve.tensor_tensor(ties, other, own, ALU.is_equal))
                link(dve.tensor_tensor(ties, ties, earlier[:, :, :].unsqueeze(1).to_broadcast([P, TILES, E, E]), ALU.mult))
                link(dve.tensor_tensor(beats, beats, ties, ALU.add))
                link(dve.tensor_reduce(rank, beats, AX.X, ALU.add))
                link(dve.tensor_scalar(rank, rank, float(top), None, ALU.is_lt))
                link(dve.tensor_tensor(prob, prob, rank, ALU.mult))
                link(dve.tensor_reduce(small, prob, AX.X, ALU.add))
                link(dve.reciprocal(inv, small))
                link(dve.tensor_tensor(prob, prob, over(inv), ALU.mult))
                link(dve.tensor_scalar(r.shares[:, 0:E, :].rearrange("p e t -> p t e"), prob, gate, None, ALU.mult))
                link(dve.memset(r.shares[:, E, :], 1.0))
                link(dve.tensor_scalar(r.shares[:, E, :], r.shares[:, E, :], gate, None, ALU.mult))

            r.sync, r.gpsimd, r.vector_weights, r.tensor_weights = sync, gpsimd, vector_weights, tensor_weights
            r.tensor, r.scalar, r.scalar_last, r.vector_last = tensor, scalar, scalar_last, vector_last
            return r

        gated_sems = sems("gated", "raw raw_free zeroed whi wlo w_free up1 up2 silu hid ahi alo down shares acc")
        gated_counts = [(0, 0, 0, 0, 0, 0)]

        def gated_experts(name, sublayer, split, gate, before, done, experts, top, router_args, chunks, outputs, groups, load, up_width, down_chunks):
            lay = Layout()
            hidden = lay(4, BLK)
            silu, act32 = hidden[:, 0:2, :], hidden[:, 2:4, :]
            router = make_router(name, split, lay, flat(hidden), experts, top, gate, *router_args)
            norm = make_norm(sublayer, split=split)
            per = 1 + max(e for pieces in outputs for e, _, _ in pieces)
            shares_now = lay(2 * per, TILES)
            s = Names()
            (
                s.raw, s.raw_free, s.zeroed, s.whi, s.wlo, s.w_free, s.up1, s.up2, s.silu, s.hid, s.ahi, s.alo,
                s.down, s.shares, s.acc
            ) = gated_sems
            NC = len(chunks)
            UNITS = BLOCKS * NC
            ACCS = BLOCKS * per
            NL = load.count
            width = up_width
            used = 2 * DC * width + down_chunks * D
            even = groups - 2 + groups % 2
            was = Names()
            was.raw, was.zeroed, was.groups, was.units, was.shares, was.accs = gated_counts[-1]
            gated_counts.append((was.raw + groups * 16 * NL, was.zeroed + 1, was.groups + groups, was.units + groups * UNITS,
                                 was.shares + even // 2 + (groups - even) * per, was.accs + groups * ACCS))

            def up_w(w, slot, mat, c, q):
                at = (mat * DC + c) * width + chunks[q][0]
                return w[:, slot, at:at + chunks[q][1]]

            def down_w(w, slot, q, p0, n):
                at = 2 * DC * width + q * D
                return w[p0:p0 + n, slot, at:at + D]

            raw_up = raw[:, 0:2 * DC * width].rearrange("p (m c w) -> p m c w", m=2, c=DC)
            raw_down = raw[:, 2 * DC * width:used].rearrange("p (q d) -> p q d", q=down_chunks)

            def sync(sp):
                router.sync(sp)
                sp.wait_ge(s.zeroed, was.zeroed + 1)
                with sp.Fori(0, even) as n:
                    sp.wait_ge(s.raw_free, was.groups + n + 1)
                    load(sp, n, raw_up, raw_down, s.raw)
                for n in range(even, groups):
                    sp.wait_ge(s.raw_free, was.groups + n + 1)
                    load(sp, n, raw_up, raw_down, s.raw)

            def gpsimd(pool):
                router.gpsimd(pool)
                with pool.Fori(0, BLOCKS) as i:
                    norm.gpsimd(pool, i)
                if was.groups == 0:
                    pool.sem_inc(s.raw_free, 1)

                def split_low(n, slot):
                    hold(pool, s.whi, was.groups + n + 1)
                    pool.tensor_tensor(wlo[:, slot, 0:used], raw[:, 0:used], whi[:, slot, 0:used].bitcast(F32),
                                       ALU.subtract).then_inc(s.wlo, 1)
                    hold(pool, s.wlo, was.groups + n + 1)
                    pool.sem_inc(s.raw_free, 1)

                with pool.Fori(0, groups // 2) as i:
                    for slot in range(2):
                        split_low(2 * i + slot, slot)
                if groups % 2:
                    split_low(groups - 1, 0)

            def split_high(act, n, slot):
                act.wait_ge(s.raw, was.raw + (n + 1) * 16 * NL)
                act.wait_ge(s.w_free, was.groups + n + 1)
                act.activation(whi[:, slot, 0:used], raw[:, 0:used], ACT.Copy).then_inc(s.whi, 1)

            def scalar_group(act, n, slot, more):
                for u in range(UNITS):
                    U = was.units + n * UNITS + u
                    m = chunks[u % NC][1]
                    act.wait_ge(s.up1, U + 1)
                    act.activation(silu[0:m, u % 2, :], bank[u % 2][0:m, :], ACT.Silu).then_inc(s.silu, 1)
                    act.wait_ge(s.hid, U + 3)
                    act.wait_ge(s.down, U + 1)
                    act.activation(ahi[0:m, u % 2, :], act32[0:m, u % 2, :], ACT.Copy).then_inc(s.ahi, 1)
                    if u == NC and more:
                        split_high(act, n + 1, 1 - slot)

            def scalar(act):
                with act.Fori(0, BLOCKS) as i:
                    norm.scalar(act, i)
                    router.scalar(act, i)
                router.scalar_last(act)
                split_high(act, 0, 0)
                with act.Fori(0, even // 2) as i:
                    for slot in range(2):
                        scalar_group(act, 2 * i + slot, slot, True)
                for n in range(even, groups):
                    scalar_group(act, n, n % 2, n + 1 < groups)

            def vector_group(dve, n, slot):
                for u in range(UNITS):
                    U = was.units + n * UNITS + u
                    b, q = divmod(u, NC)
                    m = chunks[q][1]
                    dve.wait_ge(s.silu, U + 1)
                    dve.wait_ge(s.up2, U + 1)
                    dve.tensor_tensor(act32[0:m, u % 2, :], silu[0:m, u % 2, :], bank[2 + u % 2][0:m, :], ALU.mult).then_inc(s.hid, 1)
                    dve.wait_ge(s.ahi, U + 1)
                    dve.tensor_tensor(alo[0:m, u % 2, :], act32[0:m, u % 2, :], ahi[0:m, u % 2, :].bitcast(F32),
                                      ALU.subtract).then_inc(s.alo, 1)
                    if u:
                        add_outputs(dve, n, slot, u - 1)
                add_outputs(dve, n, slot, UNITS - 1)

            last_chunk = {e: max(q for q in range(NC) for x, _, _ in outputs[q] if x == e) for e in range(per)}

            def add_outputs(dve, n, slot, u):
                b, q = divmod(u, NC)
                for e in range(per):
                    if last_chunk[e] == q:
                        add_output(dve, n, slot, b, e, was.units + n * UNITS + u)

            def add_output(dve, n, slot, b, e, U):
                Y = was.accs + (n * BLOCKS + b) * per + e
                y_slot = (b * per + e) % 2
                dve.wait_ge(s.acc, Y + 2)
                dve.wait_ge(s.down, U + 3)
                for k in range(BT):
                    t = b * BT + k
                    ins = dve.scalar_tensor_tensor(X[:, t, :], bank[4 + 2 * y_slot + k // 2][:, k % 2 * D:k % 2 * D + D],
                                                   shares_now[:, slot * per + e, t:t + 1], X[:, t, :], ALU.mult, ALU.add)
                ins.then_inc(s.acc, 1)

            def vector(dve):
                dve.wait_ge(*before)
                dve.memset(raw[:, 0:used], 0.0).then_inc(s.zeroed, 1)
                router.vector_weights(dve)
                with dve.Fori(0, BLOCKS) as i:
                    norm.vector_norm(dve, i)
                    norm.vector_rest(dve, i)
                router.vector_last(dve)
                if was.groups == 0:
                    dve.sem_inc(s.hid, 2)
                    dve.sem_inc(s.acc, 2)
                with dve.Fori(0, even // 2) as i:
                    dve.wait_ge(s.acc, was.accs + i * 2 * ACCS + 2)
                    dve.tensor_copy(shares_now, router.shares[:, ds(i * 2 * per, 2 * per), :]).then_inc(s.shares, 1)
                    hold(dve, s.shares, was.shares + i + 1)
                    for slot in range(2):
                        vector_group(dve, 2 * i + slot, slot)
                for j, n in enumerate(range(even, groups)):
                    dve.wait_ge(s.acc, was.accs + n * ACCS + 2)
                    for e in range(per):
                        dve.tensor_copy(shares_now[:, n % 2 * per + e, :], router.shares[:, min(n * per + e, experts), :]).then_inc(s.shares, 1)
                    dve.wait_ge(s.shares, was.shares + even // 2 + (j + 1) * per)
                    vector_group(dve, n, n % 2)
                dve.wait_ge(s.acc, was.accs + groups * ACCS + 2)
                dve.sem_inc(done, TILES)

            def tensor_group(pe, n, slot):
                hold(pe, s.wlo, was.groups + n + 1)

                def up(u):
                    U = was.units + n * UNITS + u
                    b, q = divmod(u, NC)
                    cols = slice(b * BLK, (b + 1) * BLK)
                    m = chunks[q][1]
                    hold(pe, s.hid, U + 1)
                    for mat, signal in ((0, s.up1), (1, s.up2)):
                        j = 0
                        for c in range(DC):
                            for w, x in ((whi, xhi), (whi, xlo), (wlo, xhi)):
                                mm = pe.matmul(bank[2 * mat + u % 2][0:m, :], up_w(w, slot, mat, c, q), x[:, c, cols],
                                               start=j == 0, stop=j == 3 * DC - 1)
                                j += 1
                        mm.then_inc(signal, 1)

                opened = set()

                def down(u):
                    U = was.units + n * UNITS + u
                    b, q = divmod(u, NC)
                    hold(pe, s.alo, U + 1)
                    for e, p0, np_ in outputs[q]:
                        Y = was.accs + (n * BLOCKS + b) * per + e
                        y_slot = (b * per + e) % 2
                        first = (b, e) not in opened
                        if first:
                            opened.add((b, e))
                            hold(pe, s.acc, Y + 1)
                        for k in range(BT):
                            j = 0
                            for a, w in ((ahi, whi), (ahi, wlo), (alo, whi)):
                                mm = pe.matmul(bank[4 + 2 * y_slot + k // 2][:, k % 2 * D:k % 2 * D + D],
                                               a[p0:p0 + np_, u % 2, k * P:(k + 1) * P], down_w(w, slot, q, p0, np_),
                                               start=first and k % 2 == 0 and j == 0, stop=last_chunk[e] == q and j == 2,
                                               skip_group_check=True)
                                j += 1
                    mm.then_inc(s.down, 1)

                for u in range(UNITS + 1):
                    if u < UNITS:
                        up(u)
                    if u:
                        down(u - 1)

            def tensor(pe):
                pe.wait_ge(*before)
                router.tensor_weights(pe)
                with pe.Fori(0, BLOCKS) as i:
                    norm.tensor(pe, i)
                    router.tensor(pe, norm, i)
                pe.wait_ge(router.kept, router.all_kept)
                pe.wait_ge(s.shares, was.shares + 1)
                if was.groups == 0:
                    pe.sem_inc(s.w_free, 2)
                    pe.sem_inc(s.down, 2)
                def group(n, slot):
                    tensor_group(pe, n, slot)
                    pe.wait_ge(s.down, was.units + (n + 1) * UNITS + 2)
                    pe.sem_inc(s.w_free, 1)

                with pe.Fori(0, even // 2) as i:
                    for slot in range(2):
                        group(2 * i + slot, slot)
                for n in range(even, groups):
                    group(n, n % 2)

            return sync, gpsimd, scalar, vector, tensor

        def layer0_experts(before, done):
            EXPERTS, HALF = 8, P // 2
            rest = L0_I - P

            def load(sp, n, raw_up, raw_down, signal):
                for mat, (routed, shared) in enumerate((("L0_ffn_w1", "L0_ffn_sw1"), ("L0_ffn_w3", "L0_ffn_sw3"))):
                    for c in range(DC):
                        for e in range(2):
                            if isinstance(n, int) and n == EXPERTS // 2:
                                src = io[shared][c * P:(c + 1) * P, e * L0_I:(e + 1) * L0_I]
                            else:
                                src = io[routed][ds(2 * n + e, 1), c * P:(c + 1) * P, :].rearrange("o p i -> p (o i)")
                            at = e * (P + HALF)
                            sp.dma_start(raw_up[:, mat, c, at:at + L0_I], src).then_inc(signal, 16)
                for e in range(2):
                    def rows(a, b):
                        if isinstance(n, int) and n == EXPERTS // 2:
                            return io["L0_ffn_sw2"][e * L0_I + a:e * L0_I + b, :]
                        return io["L0_ffn_w2"][ds(2 * n + e, 1), a:b, :].rearrange("o i d -> (o i) d")
                    if e == 0:
                        sp.dma_start(raw_down[:, 0, :], rows(0, P)).then_inc(signal, 16)
                        sp.dma_start(raw_down[0:rest, 1, :], rows(P, L0_I)).then_inc(signal, 16)
                    else:
                        sp.dma_start(raw_down[HALF:P, 1, :], rows(0, HALF)).then_inc(signal, 16)
                        sp.dma_start(raw_down[0:L0_I - HALF, 2, :], rows(HALF, L0_I)).then_inc(signal, 16)
            load.count = 12

            return gated_experts("f0", 1, 0, gates[:, 4:5], before, done, EXPERTS, 2, (True, io["L0_ffn_gate_w"]),
                                 chunks=[(0, P), (P, P), (2 * P, L0_I - HALF)],
                                 outputs=[[(0, 0, P)], [(0, 0, rest), (1, HALF, HALF)], [(1, 0, L0_I - HALF)]],
                                 groups=EXPERTS // 2 + 1, load=load, up_width=3 * P, down_chunks=3)

        def layer1_attention(before, done):
            HEADS = 16
            HD = D // HEADS
            HC = P // HD
            AUG = P + HC
            EPS = 1e-6
            lay = Layout()
            xT, cT = lay(DC, BLK), lay(DC, BLK)
            wq, wg, wo, wkv = lay(DC, D), lay(DC, D), lay(DC, D), lay(DC, 2 * D)
            head_mask = sb("a1_head_mask", [P, AUG])
            gate_bias = sb("a1_gate_bias", [P, D])
            q_neg, qf = lay(DC, BLK), lay(DC, BLK)
            k_neg, kf = lay(BT, D), lay(BT, D)
            values = lay(BT, DC, AUG)
            summary = lay(2, BT, DC, AUG)
            gate_z, gated, den = lay(BT, D), lay(BT, D), lay(BT, HEADS)
            attended, attendedT = lay(BT, D), lay(DC, BLK)
            norm = make_norm(2, xT)
            cx = make_context(1, cT)
            s = Names()
            (
                s.mask, s.ones, s.q, s.q_neg, s.q_exp, s.qf, s.g, s.gz, s.gexp, s.kv, s.k_neg, s.k_exp, s.kf, s.v,
                s.sum_ps, s.sum, s.num, s.den, s.att, s.attT_ps, s.attT, s.out
            ) = sems("a1",
                 "mask ones q q_neg q_exp qf g gz gexp kv k_neg k_exp kf v sum_ps sum num den att attT_ps "
                 "attT out")
            was = count_weights(loaded=16 * 5, turned=4, ready=DC * 4)
            RAW_W = 10 * D
            raw_w = raw[:, 0:RAW_W].rearrange("p (a k) -> p a k", k=D)
            weights = (("L1_xattn_Wq", wq, 0, 2), ("L1_xattn_Wg", wg, 2, 2), ("L1_xattn_Wo", wo, 4, 2),
                       ("L1_xattn_Wkv", wkv, 6, 4))

            def sum_bank(b, k, c):
                m = k * DC + c
                return bank[((4, 5, 6), (7, 0, 1))[b][m // 3]], m % 3 * AUG

            def sync(sp):
                sp.wait_ge(*before)
                for name, _, a, n in weights:
                    sp.dma_start(raw_w[:, a:a + n, :], io[name].rearrange("(a p) k -> p a k", p=P)).then_inc(weight.loaded, 16)
                sp.dma_start(gate_bias[:, :], io["L1_xattn_bg"].partition_broadcast(P)).then_inc(weight.loaded, 16)
                cx.sync(sp)

            def gpsimd(pool):
                v = head_mask[:, 0:P].rearrange("p (h j) -> p h j", h=HC)
                pool.memset(head_mask[:, :], 1.0).then_inc(s.mask, 1)
                pool.wait_ge(s.mask, 1)
                for half, (base, sign) in enumerate(((0, 1), (HD - 1, -1))):
                    if half:
                        pool.wait_ge(s.mask, 3)
                    pool.affine_select(out=v, in_=v, compare_op=ALU.is_ge, fill=0.0, base=base,
                                       pattern=[[-sign * HD, HC], [0, HD]], channel_multiplier=sign).then_inc(s.mask, 1)
                    pool.affine_select(out=head_mask[:, P:AUG], in_=head_mask[:, P:AUG], compare_op=ALU.is_ge, fill=0.0, base=base,
                                       pattern=[[-sign * HD, HC]], channel_multiplier=sign).then_inc(s.mask, 1)
                cx.gpsimd_first(pool)
                with pool.Fori(0, BLOCKS) as i:
                    cx.gpsimd(pool, i)
                    norm.gpsimd(pool, i)

            def scalar(act):
                for j, (_, w, _, n) in enumerate(weights):
                    act.wait_ge(weight.turned, was.turned + j + 1)
                    for c in range(DC):
                        at = c * n * P
                        act.activation(w[:, c, :], bank[j + at // 512][:, at % 512:at % 512 + n * P], ACT.Copy).then_inc(weight.ready, 1)
                with act.Fori(0, BLOCKS) as i:
                    cx.scalar(act, i)
                    norm.scalar(act, i)
                    for m in range(DC):
                        act.wait_ge(s.q_neg, i * DC + m + 1)
                        act.activation(q_neg[:, m, :], q_neg[:, m, :], ACT.Exp).then_inc(s.q_exp, 1)
                    for h in range(2):
                        act.wait_ge(s.gz, i * 2 + h + 1)
                        act.activation(flat(gate_z[:, 2 * h:2 * h + 2, :]), flat(gate_z[:, 2 * h:2 * h + 2, :]), ACT.Exp,
                                       scale=-1.0).then_inc(s.gexp, 1)
                    for k in range(BT):
                        act.wait_ge(s.k_neg, i * BT + k + 1)
                        act.activation(k_neg[:, k, :], k_neg[:, k, :], ACT.Exp).then_inc(s.k_exp, 1)
                        act.wait_ge(s.kf, i * BT + k + 1)
                        act.activation(values[:, k, :, 0:P], bank[k][:, D:2 * D].rearrange("p (c e) -> p c e", c=DC),
                                       ACT.Copy).then_inc(s.v, 1)
                    act.wait_ge(s.attT_ps, i + 1)
                    for c in range(DC):
                        act.activation(attendedT[:, c, :], bank[6 + c][:, :], ACT.Copy).then_inc(s.attT, 1)

            def vector(dve):
                dve.wait_ge(*before)
                dve.wait_ge(weight.loaded, was.loaded + 16 * 5)
                dve.wait_ge(s.mask, 5)
                dve.memset(values[:, :, :, P:AUG], 1.0).then_inc(s.ones, 1)
                bias2 = gate_bias[:, :].unsqueeze(1).to_broadcast([P, 2, D])
                with dve.Fori(0, BLOCKS) as i:
                    norm.vector_norm(dve, i)
                    for m in range(DC):
                        dve.wait_ge(s.q, i * DC + m + 1)
                        dve.tensor_scalar(q_neg[:, m, :], bank[4 + m][:, :], 0.0, None, ALU.min).then_inc(s.q_neg, 1)
                    for h in range(2):
                        dve.wait_ge(s.g, i * 2 + h + 1)
                        dve.tensor_tensor(gate_z[:, 2 * h:2 * h + 2, :], bank[6 + h][:, :].rearrange("p (k d) -> p k d", k=2),
                                          bias2, ALU.add).then_inc(s.gz, 1)
                    for m in range(DC):
                        dve.wait_ge(s.q_exp, i * DC + m + 1)
                        dve.scalar_tensor_tensor(qf[:, m, :], bank[4 + m][:, :], 0.0, q_neg[:, m, :], ALU.max, ALU.add).then_inc(s.qf, 1)
                    for k in range(BT):
                        dve.wait_ge(s.kv, i * BT + k + 1)
                        dve.tensor_scalar(k_neg[:, k, :], bank[k][:, 0:D], 0.0, None, ALU.min).then_inc(s.k_neg, 1)
                    for k in range(BT):
                        dve.wait_ge(s.k_exp, i * BT + k + 1)
                        dve.scalar_tensor_tensor(kf[:, k, :], bank[k][:, 0:D], 0.0, k_neg[:, k, :], ALU.max, ALU.add).then_inc(s.kf, 1)
                    dve.wait_ge(s.sum_ps, i + 1)
                    for b in range(2):
                        for k in range(BT):
                            for c in range(DC):
                                bk, at = sum_bank(b, k, c)
                                dve.tensor_tensor(summary[:, b, k, c, :], bk[:, at:at + AUG],
                                                  head_mask[:, :], ALU.mult).then_inc(s.sum, 1)
                    for k in range(BT):
                        dve.wait_ge(s.num, i * BT + k + 1)
                        got = bank[2 + k][:, 0:DC * AUG].rearrange("p (c a) -> p c a", c=DC)
                        dve.tensor_scalar(den[:, k, :].rearrange("p (c h) -> p c h", c=DC), got[:, :, P:AUG], EPS, None,
                                          ALU.add).then_inc(s.den, 1)
                        if k == 0:
                            dve.wait_ge(s.gexp, i * 2 + 2)
                        dve.wait_ge(s.den, (i * BT + k) * 3 + 1)
                        heads = gated[:, k, :].rearrange("p (h e) -> p h e", h=HEADS)
                        dve.scalar_tensor_tensor(heads, gate_z[:, k, :].rearrange("p (h e) -> p h e", h=HEADS), 1.0,
                                                 den[:, k, :].unsqueeze(2).to_broadcast([P, HEADS, HD]), ALU.add, ALU.mult).then_inc(s.den, 1)
                        dve.wait_ge(s.den, (i * BT + k) * 3 + 2)
                        dve.reciprocal(gated[:, k, :], gated[:, k, :]).then_inc(s.den, 1)
                        dve.wait_ge(s.den, (i * BT + k) * 3 + 3)
                        dve.tensor_tensor(attended[:, k, :].rearrange("p (c e) -> p c e", c=DC), got[:, :, 0:P],
                                          gated[:, k, :].rearrange("p (c e) -> p c e", c=DC), ALU.mult).then_inc(s.att, 1)
                    for k in range(BT):
                        if k % 2 == 0:
                            dve.wait_ge(s.out, i * 2 + k // 2 + 1)
                        dve.scalar_tensor_tensor(x_tile(i * BT + k), bank[k // 2][:, k % 2 * D:k % 2 * D + D], gates[:, 1:2],
                                                 x_tile(i * BT + k), ALU.mult, ALU.add).then_inc(done, 1)

            def tensor(pe):
                pe.wait_ge(*before)
                pe.wait_ge(weight.loaded, was.loaded + 16 * 5)
                for j, (_, _, a0, n) in enumerate(weights):
                    for c in range(DC):
                        for a in range(n):
                            at = (c * n + a) * P
                            tp = pe.transpose(bank[j + at // 512][:, at % 512:at % 512 + P], raw_w[:, a0 + a, c * P:(c + 1) * P], ident[:, :])
                    tp.then_inc(weight.turned, 1)
                pe.wait_ge(weight.ready, was.ready + DC * len(weights))
                pe.wait_ge(s.ones, 1)
                cx.tensor_first(pe)
                with pe.Fori(0, BLOCKS) as i:
                    cx.tensor(pe, i)
                    norm.tensor(pe, i)
                    hold(pe, norm.hi, (norm.first + i) * DC + DC)
                    for m in range(DC):
                        for c in range(DC):
                            mm = pe.matmul(bank[4 + m][:, :], wq[:, c, m * P:(m + 1) * P], xT[:, c, :], start=c == 0, stop=c == DC - 1)
                        mm.then_inc(s.q, 1)
                    for k in range(BT):
                        for c in range(DC):
                            mm = pe.matmul(bank[6 + k // 2][:, k % 2 * D:k % 2 * D + D], xT[:, c, k * P:(k + 1) * P], wg[:, c, :],
                                           start=c == 0, stop=c == DC - 1)
                        if k % 2:
                            mm.then_inc(s.g, 1)
                    hold(pe, cx.turned, (cx.first + i) * DC + DC)
                    for k in range(BT):
                        for c in range(DC):
                            mm = pe.matmul(bank[k][:, :], cT[:, c, k * P:(k + 1) * P], wkv[:, c, :], start=c == 0, stop=c == DC - 1)
                        mm.then_inc(s.kv, 1)
                    hold(pe, s.qf, i * DC + DC)
                    hold(pe, s.gz, i * 2 + 2)
                    hold(pe, s.v, i * BT + BT)
                    for b in range(2):
                        rows = slice(b * SEQ, (b + 1) * SEQ)
                        for k in range(BT):
                            for c in range(DC):
                                bk, at = sum_bank(b, k, c)
                                mm = pe.matmul(bk[:, at:at + AUG], kf[rows, k, c * P:(c + 1) * P], values[rows, k, c, :], start=True, stop=True)
                    mm.then_inc(s.sum_ps, 1)
                    hold(pe, s.sum, (i + 1) * 2 * BT * DC)
                    for k in range(BT):
                        for b in range(2):
                            rows = slice(b * SEQ, (b + 1) * SEQ)
                            for c in range(DC):
                                mm = pe.matmul(bank[2 + k][rows, c * AUG:(c + 1) * AUG],
                                               qf[:, c, k * P + b * SEQ:k * P + (b + 1) * SEQ], summary[:, b, k, c, :], start=True, stop=True)
                        mm.then_inc(s.num, 1)
                    hold(pe, s.att, i * BT + BT)
                    for c in range(DC):
                        for k in range(BT):
                            tp = pe.transpose(bank[6 + c][:, k * P:(k + 1) * P], attended[:, k, c * P:(c + 1) * P], ident[:, :])
                    tp.then_inc(s.attT_ps, 1)
                    hold(pe, s.attT, i * DC + DC)
                    for k in range(BT):
                        for c in range(DC):
                            mm = pe.matmul(bank[k // 2][:, k % 2 * D:k % 2 * D + D], attendedT[:, c, k * P:(k + 1) * P], wo[:, c, :],
                                           start=c == 0, stop=c == DC - 1)
                        if k % 2:
                            mm.then_inc(s.out, 1)
                    pe.sem_inc(cx.free, 1)

            return sync, gpsimd, scalar, vector, tensor

        quant_sems = sems("quant", "chain scale shifted whole tp turned")

        def make_quant(use, lay, dst):
            n = Names()
            n.chain, n.scale, n.shifted, n.whole, n.tp, n.turned = quant_sems
            n.first = use * BLOCKS
            peak, rate = lay(BT), lay(BT)
            n.step = lay(TILES)
            shifted, whole = lay(BT, D), lay(BT, D, dt=BF16)
            turn = bank[6][:, :].bitcast(BF16).rearrange("p (c t) -> p c t", c=DC)

            def vector(dve, norm, i):
                g = n.first + i
                dve.wait_ge(norm.xn, (norm.first + i) * BT + BT)
                dve.tensor_reduce(peak, xn[:, :, :], AX.X, ALU.max, apply_absolute_value=True).then_inc(n.chain, 1)
                dve.wait_ge(n.chain, g * 2 + 1)
                step = n.step[:, ds(i * BT, BT)]
                dve.tensor_scalar(step, peak, QUANT_EPS, 1.0 / 127, ALU.max, ALU.mult).then_inc(n.chain, 1)
                hold(dve, n.chain, g * 2 + 2)
                dve.reciprocal(rate, step).then_inc(n.scale, 1)

            def scalar(act, i):
                act.wait_ge(n.scale, n.first + i + 1)
                for k in range(BT):
                    act.activation(shifted[:, k, :], xn[:, k, :], ACT.Identity, scale=rate[:, k:k + 1],
                                   bias=magic[:, 0:1]).then_inc(n.shifted, 1)

            def gpsimd(pool, i):
                hold(pool, n.shifted, (n.first + i) * BT + BT)
                pool.tensor_scalar(flat(whole), flat(shifted), MAGIC, None, ALU.subtract).then_inc(n.whole, 1)

            def tensor(pe, i):
                hold(pe, n.whole, n.first + i + 1)
                for c in range(DC):
                    for k in range(BT):
                        tp = pe.transpose(turn[:, c, k * P:(k + 1) * P], whole[:, k, c * P:(c + 1) * P], identb[:, :])
                tp.then_inc(n.tp, 1)

            def scalar_last(act, i):
                act.wait_ge(n.tp, n.first + i + 1)
                act.activation(dst[:, :, ds(i * BLK, BLK)], turn, ACT.Copy).then_inc(n.turned, 1)

            n.vector, n.scalar, n.gpsimd, n.tensor, n.scalar_last = vector, scalar, gpsimd, tensor, scalar_last
            return n

        whole_sems = sems("whole", "raw size total chain ternary tern shifted w_tp w up relu once prod peak pair rate turned "
                            "wholeT down acc")
        whole_used = Names()
        weights_free = sem("weights_free")

        def layer1_experts(before, done):
            E, I = 8, 512
            IC = I // P
            AHEAD, PEAK_AHEAD, SHIFT_AHEAD = 6, 4, 1
            RING = 8
            RELUS = 4
            TURN_AT = (5, 7, 9)
            MAT = I * D // P
            GATE, UP, DOWN = 0, 1, 2
            lay = Layout()
            prod = lay(RING, I)
            router = make_router("f1", 1, lay, flat(prod), E, 2, gates[:, 5:6], True, io["L1_ffn_router_w"])
            norm = make_norm(3, split=1)
            xqT = lay(DC, TOK, dt=BF16)
            quant = make_quant(0, lay, xqT)
            step3 = lay(TILES)
            relu, once = lay(RELUS, I), lay(2, I)
            shifted, wholeT = lay(2, I), lay(2, I, dt=BF16)
            up_w = lay(2, 2, DC, I, dt=BF16)
            down_w = lay(2, IC, D, dt=BF16)
            tern = lay(3, MAT, dt=BF16)
            size_sum, mean, per_mean = lay(3), lay(3), lay(3)
            factor, inv = lay(TILES), lay(TILES)
            least, out_factor = lay(2, TILES), lay(2, TILES)
            peak, unit, rate, out_scale = lay(TILES), lay(TILES), lay(TILES), lay(TILES)
            s = Names()
            (
                s.raw, s.size, s.total, s.chain, s.ternary, s.tern, s.shifted, s.w_tp, s.w, s.up, s.relu, s.once,
                s.prod, s.peak, s.pair, s.rate, s.turned, s.wholeT, s.down, s.acc
            ) = whole_sems
            raw_m = raw[:, 0:3 * MAT].rearrange("p (m k) -> p m k", m=3)
            turn = bank[4][:, :]
            w_turn = bank[5][:, :].bitcast(BF16)
            CHAIN = 7
            units = E * TILES
            after = whole_used
            after.raw, after.size, after.total, after.chain, after.tern = E * 48, E * 3, E, 2 + E * CHAIN, E * 3 + 3
            after.w_tp, after.w = E * 3, E * 3 + 1
            after.up = after.relu = after.peak = after.pair = after.wholeT = after.down = units
            after.rate, after.shifted, after.turned, after.acc = units // 2, units + RING, units + 2, units + 2
            even = E - 2

            def sync(sp):
                sp.wait_ge(*before)
                router.sync(sp)
                with sp.Fori(0, E) as n:
                    sp.wait_ge(s.tern, n * 3 + 3)
                    for m, w in ((GATE, "L1_ffn_gate_w"), (UP, "L1_ffn_up_w"), (DOWN, "L1_ffn_down_w")):
                        width = I if m == DOWN else D
                        src = io[w][ds(n, 1)].rearrange("o (a p) k -> p (o a) k", p=P)
                        sp.dma_start(raw_m[:, m, :].rearrange("p (a k) -> p a k", k=width), src).then_inc(s.raw, 16)

            def scalar_size(act, n, m):
                act.wait_ge(s.raw, n * 48 + 48)
                act.activation(tern[:, m, :], raw_m[:, m, :], ACT.Abs, accum_out=size_sum[:, m:m + 1]).then_inc(s.size, 1)

            def tensor_total(pe, n):
                hold(pe, s.size, n * 3 + 3)
                pe.matmul(bank[5][:, 0:3], ones[:, :], size_sum, start=True, stop=True).then_inc(s.total, 1)

            def vector_scales(dve, n, slot):
                dve.wait_ge(s.total, n + 1)
                link = linker(dve, s.chain, n * CHAIN + 2)
                link(dve.tensor_scalar(mean, bank[5][:, 0:3], 1.0 / (I * D), QUANT_EPS, ALU.mult, ALU.max))
                link(dve.reciprocal(per_mean, mean))
                link(dve.tensor_scalar(factor, step3, mean[:, GATE:GATE + 1], mean[:, GATE:GATE + 1], ALU.mult, ALU.mult))
                link(dve.tensor_scalar(factor, factor, mean[:, UP:UP + 1], None, ALU.mult))
                link(dve.reciprocal(inv, factor))
                link(dve.tensor_scalar(least[:, slot, :], inv, QUANT_EPS / 127, None, ALU.mult))
                link(dve.scalar_tensor_tensor(out_factor[:, slot, :], factor, mean[:, DOWN:DOWN + 1],
                                              flat(router.shares[:, ds(n, 1), :]) if not isinstance(n, int) else router.shares[:, n, :],
                                              ALU.mult, ALU.mult))

            def vector_ternary(dve, n, m, part):
                w = raw_m[:, m, :]
                if part == 0:
                    dve.tensor_scalar(w, w, per_mean[:, m:m + 1], MAGIC, ALU.mult, ALU.add).then_inc(s.ternary, 1)
                elif part == 1:
                    dve.wait_ge(s.ternary, (n * 3 + m) * 2 + 1)
                    dve.tensor_scalar(tern[:, m, :], w, MAGIC, -1.0, ALU.subtract, ALU.max).then_inc(s.ternary, 1)
                else:
                    dve.wait_ge(s.ternary, (n * 3 + m) * 2 + 2)
                    dve.tensor_scalar(tern[:, m, :], tern[:, m, :], 1.0, None, ALU.min).then_inc(s.tern, 1)

            def tensor_turn(pe, n, m):
                hold(pe, s.tern, n * 3 + m + 4)
                hold(pe, s.w, n * 3 + m + 1)
                rows, cols = (DC, IC) if m == DOWN else (IC, DC)
                for c in range(cols):
                    for a in range(rows):
                        at = (c * rows + a) * P
                        tp = pe.transpose(w_turn[:, at:at + P], tern[:, m, (a * cols + c) * P:(a * cols + c + 1) * P], identb[:, :])
                tp.then_inc(s.w_tp, 1)

            def scalar_weights(act, n, slot, m):
                act.wait_ge(s.w_tp, n * 3 + m + 1)
                to = down_w[:, slot, :, :] if m == DOWN else up_w[:, slot, m, :, :]
                act.activation(flat(to), w_turn, ACT.Copy).then_inc(s.w, 1)

            def scalar_relu(act, n, t):
                act.wait_ge(s.up, n * TILES + t + 1)
                act.wait_ge(s.prod, n * TILES + t + 1)
                act.activation(relu[:, t % RELUS, :], bank[t % 2][:, :], ACT.Relu).then_inc(s.relu, 1)

            def scalar_shift(act, n, t):
                U = n * TILES + t
                act.wait_ge(s.rate, n * (TILES // 2) + t // 2 + 1)
                act.wait_ge(s.turned, U + 1)
                act.activation(shifted[:, t % 2, :], prod[:, t % RING, :], ACT.Copy, scale=rate[:, t:t + 1],
                               bias=MAGIC).then_inc(s.shifted, 1)

            def scalar_back(act, n, t):
                act.wait_ge(s.turned, n * TILES + t + 3)
                act.activation(wholeT[:, t % 2, :], turn, ACT.Copy, bias=-MAGIC).then_inc(s.wholeT, 1)

            def vector_once(dve, n, t):
                U = n * TILES + t
                dve.wait_ge(s.relu, U + 1)
                dve.wait_ge(s.prod, U + RELUS - 1)
                dve.tensor_tensor(once[:, t % 2, :], relu[:, t % RELUS, :], bank[2 + t % 2][:, :], ALU.mult).then_inc(s.once, 1)

            def gpsimd_prod(pool, n, t):
                U = n * TILES + t
                pool.wait_ge(s.once, U + 3)
                hold(pool, s.shifted, U + 1)
                pool.tensor_tensor(prod[:, t % RING, :], once[:, t % 2, :], relu[:, t % RELUS, :], ALU.mult).then_inc(s.prod, 1)

            def vector_peak(dve, n, t, slot):
                U = n * TILES + t
                dve.wait_ge(s.prod, U + RELUS + 1)
                dve.tensor_reduce(peak[:, t:t + 1], prod[:, t % RING, :], AX.X, ALU.max, apply_absolute_value=True).then_inc(s.peak, 1)
                if t % 2:
                    two = slice(t - 1, t + 1)
                    Q = n * (TILES // 2) + t // 2
                    dve.wait_ge(s.peak, U + 1)
                    dve.scalar_tensor_tensor(unit[:, two], peak[:, two], 1.0 / 127, least[:, slot, two], ALU.mult, ALU.max).then_inc(s.pair, 1)
                    hold(dve, s.pair, Q * 2 + 1)
                    dve.reciprocal(rate[:, two], unit[:, two]).then_inc(s.rate, 1)
                    dve.tensor_tensor(out_scale[:, two], unit[:, two], out_factor[:, slot, two], ALU.mult).then_inc(s.pair, 1)

            def vector_back(dve, n, t):
                U = n * TILES + t
                dve.wait_ge(s.down, U + 1)
                dve.wait_ge(s.pair, (n * (TILES // 2) + t // 2) * 2 + 2)
                dve.scalar_tensor_tensor(X[:, t, :], bank[6 + t % 2][:, 0:D], out_scale[:, t:t + 1], X[:, t, :],
                                         ALU.mult, ALU.add).then_inc(s.acc, 1)

            def tensor_up(pe, n, t, slot):
                hold(pe, s.once, n * TILES + t + 1)
                for m in (GATE, UP):
                    for c in range(DC):
                        mm = pe.matmul(bank[2 * m + t % 2][:, :], xqT[:, c, t * P:(t + 1) * P], up_w[:, slot, m, c, :],
                                       start=c == 0, stop=c == DC - 1)
                mm.then_inc(s.up, 1)

            def tensor_turn_tile(pe, n, t):
                hold(pe, s.shifted, n * TILES + t + RING + 1)
                for c in range(IC):
                    tp = pe.transpose(turn[:, c * P:(c + 1) * P], shifted[:, t % 2, c * P:(c + 1) * P], ident[:, :])
                tp.then_inc(s.turned, 1)

            def tensor_down(pe, n, t, slot):
                hold(pe, s.wholeT, n * TILES + t + 1)
                hold(pe, s.acc, n * TILES + t + 1)
                for c in range(IC):
                    mm = pe.matmul(bank[6 + t % 2][:, 0:D], wholeT[:, t % 2, c * P:(c + 1) * P], down_w[:, slot, c, :],
                                   start=c == 0, stop=c == IC - 1)
                mm.then_inc(s.down, 1)

            def over_experts(eng, step):
                with eng.Fori(0, even // 2) as i:
                    for slot in range(2):
                        step(2 * i + slot, slot, True)
                for n in range(even, E):
                    step(n, n % 2, n + 1 < E)

            def following(n, t, slot, lead):
                return (n, t + lead, slot) if t + lead < TILES else (n + 1, t + lead - TILES, 1 - slot)

            def gpsimd(pool):
                router.gpsimd(pool)
                with pool.Fori(0, BLOCKS) as i:
                    norm.gpsimd(pool, i)
                    quant.gpsimd(pool, i)
                pool.sem_inc(s.prod, RELUS)
                for t in range(AHEAD):
                    gpsimd_prod(pool, 0, t)

                def step(n, slot, more):
                    for t in range(TILES):
                        if t + AHEAD < TILES or more:
                            gpsimd_prod(pool, *following(n, t, slot, AHEAD)[0:2])
                over_experts(pool, step)

            def scalar(act):
                with act.Fori(0, BLOCKS) as i:
                    norm.scalar(act, i)
                    quant.scalar(act, i)
                    router.scalar(act, i)
                    quant.scalar_last(act, i)
                router.scalar_last(act)
                act.sem_inc(s.w, 1)
                for m in range(3):
                    scalar_size(act, 0, m)
                for m in range(3):
                    scalar_weights(act, 0, 0, m)
                act.sem_inc(s.shifted, RING)
                for t in range(AHEAD):
                    scalar_relu(act, 0, t)
                for t in range(SHIFT_AHEAD):
                    scalar_shift(act, 0, t)

                def step(n, slot, more):
                    for t in range(TILES):
                        if t < 3 and more:
                            scalar_size(act, n + 1, t)
                        if t + SHIFT_AHEAD < TILES or more:
                            scalar_shift(act, *following(n, t, slot, SHIFT_AHEAD)[0:2])
                        scalar_back(act, n, t)
                        if t + AHEAD < TILES or more:
                            scalar_relu(act, *following(n, t, slot, AHEAD)[0:2])
                        if t in TURN_AT and more:
                            scalar_weights(act, n + 1, 1 - slot, TURN_AT.index(t))
                over_experts(act, step)

            def vector(dve):
                dve.wait_ge(*before)
                dve.sem_inc(s.tern, 3)
                router.vector_weights(dve)
                with dve.Fori(0, BLOCKS) as i:
                    norm.vector_norm(dve, i)
                    quant.vector(dve, norm, i)
                    norm.vector_rest(dve, i)
                router.vector_last(dve)
                dve.wait_ge(quant.chain, 2 * BLOCKS)
                dve.tensor_tensor(step3, quant.step, quant.step, ALU.mult).then_inc(s.chain, 1)
                dve.wait_ge(s.chain, 1)
                dve.tensor_tensor(step3, step3, quant.step, ALU.mult).then_inc(s.chain, 1)
                dve.wait_ge(s.chain, 2)
                vector_scales(dve, 0, 0)
                for m in range(3):
                    for part in range(3):
                        vector_ternary(dve, 0, m, part)
                dve.sem_inc(s.once, 2)
                dve.sem_inc(s.acc, 2)
                for t in range(AHEAD):
                    vector_once(dve, 0, t)
                    if t >= AHEAD - PEAK_AHEAD:
                        vector_peak(dve, 0, t - (AHEAD - PEAK_AHEAD), 0)

                def step(n, slot, more):
                    for t in range(TILES):
                        if t == 3 and more:
                            vector_scales(dve, n + 1, 1 - slot)
                        if t + AHEAD < TILES or more:
                            vector_once(dve, *following(n, t, slot, AHEAD)[0:2])
                        if t + PEAK_AHEAD < TILES or more:
                            vector_peak(dve, *following(n, t, slot, PEAK_AHEAD))
                        vector_back(dve, n, t)
                        for third in range(9):
                            if t == TURN_AT[0] - 2 + 2 * third // 3 and more:
                                vector_ternary(dve, n + 1, *divmod(third, 3))
                over_experts(dve, step)
                dve.wait_ge(s.acc, E * TILES + 2)
                dve.sem_inc(done, TILES)

            def tensor(pe):
                pe.wait_ge(*before)
                router.tensor_weights(pe)
                with pe.Fori(0, BLOCKS) as i:
                    norm.tensor(pe, i)
                    quant.tensor(pe, i)
                    router.tensor(pe, norm, i)
                pe.wait_ge(quant.turned, BLOCKS)
                pe.wait_ge(router.kept, router.all_kept)
                tensor_total(pe, 0)
                for m in range(3):
                    tensor_turn(pe, 0, m)
                pe.wait_ge(s.w, 4)
                pe.sem_inc(s.turned, 2)
                for t in range(AHEAD):
                    tensor_up(pe, 0, t, 0)

                def step(n, slot, more):
                    for t in range(TILES):
                        if t == 2 and more:
                            tensor_total(pe, n + 1)
                        tensor_turn_tile(pe, n, t)
                        if t + AHEAD < TILES or more:
                            if t + AHEAD == TILES:
                                hold(pe, s.w, (n + 1) * 3 + 4)
                            tensor_up(pe, *following(n, t, slot, AHEAD))
                        tensor_down(pe, n, t, slot)
                        if t in TURN_AT and more:
                            tensor_turn(pe, n + 1, TURN_AT.index(t))
                over_experts(pe, step)

            return sync, gpsimd, scalar, vector, tensor

        def layer2_attention(before, done):
            HEADS, GROUPS, HD = 32, 8, 8
            GD = GROUPS * HD
            SETS = HEADS // GROUPS
            PAIRS = SETS // 2
            NB = BLK // SEQ
            UNITS = NB * PAIRS
            SC = GROUPS * SEQ // P
            AUG = HD + 1
            lay = Layout()
            xT, cT = lay(DC, BLK), lay(DC, BLK)
            wqT, wkT, wvT, wfT = lay(DC, SETS, GD), lay(DC, GD), lay(DC, GD), lay(2, D)
            qT = lay(NB, PAIRS, 2 * SEQ)
            kT = lay(NB, SEQ)
            kblk = lay(NB, GROUPS, SEQ)
            vblk = lay(NB, SC, 2 * AUG)
            score, prob, probT = lay(2, GROUPS * SEQ), lay(2, GROUPS * SEQ), lay(2, GROUPS * SEQ)
            top, inv = lay(2, GROUPS), lay(2, PAIRS, GROUPS)
            attended, attendedT = lay(2, PAIRS, GD), lay(2, 2, SEQ)
            in_group = sb("a2_in_group", [P, GROUPS])
            bias_row = sb("a2_bias_row", [1, D])
            norm = make_norm(4, xT)
            cx = make_context(2, cT)
            s = Names()
            (
                s.fold, s.group, s.ones, s.q, s.qT, s.k, s.kT, s.kblk, s.kblk_pool, s.v, s.vblk, s.score, s.top,
                s.shifted, s.exp, s.probT_ps, s.probT, s.read, s.inv, s.att, s.attT_ps, s.attT, s.out
            ) = sems("a2",
                 "fold group ones q qT k kT kblk kblk_pool v vblk score top shifted exp probT_ps probT read "
                 "inv att attT_ps attT out")
            was = count_weights(loaded=16 * 5, turned=1, ready=DC + 3)
            raw_q, raw_f = raw[:, 0:2 * D].rearrange("p (a k) -> p a k", a=2), raw[:, 2 * D:4 * D].rearrange("p (a k) -> p a k", a=2)
            raw_k, raw_v = raw[:, 4 * D:5 * D], raw[:, 5 * D:6 * D]
            fold_f = raw[:, 6 * D:8 * D].rearrange("p (a m k) -> p a m k", a=DC, m=2)
            SOFT_BANK, TURN_BANK, READ_BANK, OUT_BANK = (0, 1, 2), (3, 4), (5, 6), 7

            def sync(sp):
                sp.wait_ge(*before)
                sp.dma_start(raw_q, io["L2_xattn_Wq"].rearrange("(a p) k -> p a k", p=P)).then_inc(weight.loaded, 16)
                sp.dma_start(raw_f, io["L2_xattn_Wfc"].rearrange("(a p) k -> p a k", p=P)).then_inc(weight.loaded, 16)
                sp.dma_start(raw_k[0:GD, :], io["L2_xattn_Wk"]).then_inc(weight.loaded, 16)
                sp.dma_start(raw_v[0:GD, :], io["L2_xattn_Wv"]).then_inc(weight.loaded, 16)
                sp.dma_start(bias_row[:, :], io["L2_xattn_bfc"].partition_broadcast(1)).then_inc(weight.loaded, 16)
                cx.sync(sp)

            def gpsimd(pool):
                pool.memset(in_group[:, :], 1.0).then_inc(s.group, 1)
                pool.wait_ge(s.group, 1)
                pool.affine_select(out=in_group[:, :], in_=in_group[:, :], compare_op=ALU.is_ge, fill=0.0, base=0,
                                   pattern=[[-HD, GROUPS]], channel_multiplier=1).then_inc(s.group, 1)
                pool.wait_ge(s.group, 2)
                pool.affine_select(out=in_group[:, :], in_=in_group[:, :], compare_op=ALU.is_ge, fill=0.0, base=HD - 1,
                                   pattern=[[HD, GROUPS]], channel_multiplier=-1).then_inc(s.group, 1)
                cx.gpsimd_first(pool)
                pool.wait_ge(s.group, 3)
                with pool.Fori(0, BLOCKS) as i:
                    cx.gpsimd(pool, i)
                    norm.gpsimd(pool, i)
                    pool.wait_ge(s.kT, i + 1)
                    block_keys(pool, NB // 2, NB).then_inc(s.kblk_pool, 1)

            def block_keys(eng, b0, b1):
                n = [GD, b1 - b0, GROUPS, SEQ]
                return eng.tensor_tensor(kblk[0:GD, b0:b1], kT[0:GD, b0:b1, :].unsqueeze(2).to_broadcast(n),
                                         in_group[0:GD, :].unsqueeze(1).unsqueeze(3).to_broadcast(n), ALU.mult)

            def scalar(act):
                act.wait_ge(weight.loaded, was.loaded + 16 * 5)
                for a in range(DC):
                    cols = raw_f[:, a, :].rearrange("p (g q m d) -> p m q g d", g=GROUPS, q=PAIRS, m=2)
                    for m in range(2):
                        act.activation(fold_f[:, a, m, :].rearrange("p (q g d) -> p q g d", q=PAIRS, g=GROUPS), cols[:, m], ACT.Copy).then_inc(s.fold, 1)
                act.wait_ge(weight.turned, was.turned + 1)
                for c in range(DC):
                    act.activation(wqT[:, c].rearrange("p j (g d) -> p j g d", g=GROUPS),
                                   bank[0][:, c * D:(c + 1) * D].rearrange("p (g j d) -> p j g d", g=GROUPS, j=SETS), ACT.Copy).then_inc(weight.ready, 1)
                act.activation(flat(wfT), bank[1][:, :], ACT.Copy).then_inc(weight.ready, 1)
                act.activation(flat(wkT), bank[2][:, 0:DC * GD], ACT.Copy).then_inc(weight.ready, 1)
                act.activation(flat(wvT), bank[2][:, DC * GD:2 * DC * GD], ACT.Copy).then_inc(weight.ready, 1)
                with act.Fori(0, BLOCKS) as i:
                    cx.scalar(act, i)
                    norm.scalar(act, i)
                    act.wait_ge(s.k, i + 1)
                    act.activation(flat(kT[0:GD]), bank[0][0:GD, :], ACT.Copy).then_inc(s.kT, 1)
                    act.wait_ge(s.v, i + 1)
                    for half in range(2):
                        rows = slice(half * SEQ, (half + 1) * SEQ)
                        got = bank[1][rows, :].rearrange("p (b c g d) -> p b c g d", b=NB, c=SC, g=2)
                        for b in range(0, NB, NB // 2):
                            bs = slice(b, b + NB // 2)
                            act.activation(vblk[rows, bs, :, half * AUG:half * AUG + HD], got[:, bs, :, half, :], ACT.Copy).then_inc(s.vblk, 1)
                    for j in range(SETS):
                        act.wait_ge(s.q, i * SETS + j + 1)
                        pair, member = divmod(j, 2)
                        act.activation(qT[0:GD, :, pair, member * SEQ:(member + 1) * SEQ],
                                       bank[4 + j][0:GD, :].rearrange("p (b t) -> p b t", b=NB), ACT.Copy).then_inc(s.qT, 1)
                    for u in range(UNITS + 4):
                        if u < UNITS:
                            act.wait_ge(s.shifted, i * UNITS + u + 1)
                            act.activation(prob[:, u % 2, :], score[:, u % 2, :], ACT.Exp, scale=HD ** -0.5).then_inc(s.exp, 1)
                        if 1 <= u <= UNITS:
                            act.wait_ge(s.probT_ps, i * UNITS + u)
                            act.activation(probT[:, (u - 1) % 2, :], bank[TURN_BANK[(u - 1) % 2]][:, :], ACT.Copy).then_inc(s.probT, 1)
                        if u >= 4 and u % 4 == 3:
                            tile = (u - 4) // 4
                            act.wait_ge(s.attT_ps, i * BT + tile + 1)
                            act.activation(attendedT,
                                           bank[OUT_BANK][:, 0:2 * P].rearrange("p (b m t) -> p m b t", b=2, m=2),
                                           ACT.Copy).then_inc(s.attT, 1)

            def vector(dve):
                dve.wait_ge(*before)
                dve.memset(vblk.rearrange("p b c a -> p (b c a)"), 0.0).then_inc(s.ones, 1)
                dve.wait_ge(s.ones, 1)
                for half in range(2):
                    rows = slice(half * SEQ, (half + 1) * SEQ)
                    dve.memset(vblk[rows, :, :, half * AUG + HD], 1.0).then_inc(s.ones, 1)
                dve.wait_ge(s.group, 3)
                with dve.Fori(0, BLOCKS) as i:
                    norm.vector_norm(dve, i)
                    dve.wait_ge(s.kT, i + 1)
                    block_keys(dve, 0, NB // 2).then_inc(s.kblk, 1)
                    for u in range(UNITS + 6):
                        if u < UNITS:
                            U = i * UNITS + u
                            got = bank[SOFT_BANK[u % 3]][:, :].rearrange("p (g k) -> p g k", g=GROUPS)
                            dve.wait_ge(s.score, U + 1)
                            dve.tensor_reduce(top[:, u % 2, :], got, AX.X, ALU.max).then_inc(s.top, 1)
                            dve.wait_ge(s.top, U + 1)
                            if u >= 2:
                                dve.wait_ge(s.exp, U - 1)
                            dve.tensor_tensor(score[:, u % 2, :].rearrange("p (g k) -> p g k", g=GROUPS), got,
                                              top[:, u % 2, :].unsqueeze(2).to_broadcast([P, GROUPS, SEQ]), ALU.subtract).then_inc(s.shifted, 1)
                        if u >= 4 and u % 2 == 0 and u < UNITS + 4:
                            b = (u - 4) // 2
                            B = i * NB + b
                            got = bank[READ_BANK[b % 2]][:, 0:UNITS // NB * SC * 2 * AUG].rearrange("p (m g a) -> p m g a", m=PAIRS, g=GROUPS)
                            dve.wait_ge(s.read, B + 1)
                            dve.reciprocal(inv[:, b % 2], got[:, :, :, HD]).then_inc(s.inv, 1)
                            dve.wait_ge(s.inv, B + 1)
                            dve.tensor_tensor(attended[:, b % 2].rearrange("p m (g d) -> p m g d", g=GROUPS), got[:, :, :, 0:HD],
                                              inv[:, b % 2].unsqueeze(3).to_broadcast([P, PAIRS, GROUPS, HD]), ALU.mult).then_inc(s.att, 1)
                        if u >= 9 and (u - 9) % 4 == 0:
                            add_tile(dve, i, (u - 9) // 4)

            def add_tile(dve, i, tile):
                dve.wait_ge(s.out, i * BT + tile + 1)
                dve.scalar_tensor_tensor(x_tile(i * BT + tile), bank[OUT_BANK][:, 2 * P:2 * P + D], gates[:, 2:3],
                                         x_tile(i * BT + tile), ALU.mult, ALU.add).then_inc(done, 1)

            def tensor(pe):
                pe.wait_ge(*before)
                pe.wait_ge(s.fold, 2 * DC)
                for c in range(DC):
                    for a in range(DC):
                        pe.transpose(bank[0][:, c * D + a * P:c * D + (a + 1) * P], raw_q[:, a, c * P:(c + 1) * P], ident[:, :])
                for m in range(2):
                    for a in range(DC):
                        pe.transpose(bank[1][:, m * D + a * P:m * D + (a + 1) * P], fold_f[:, a, m, :], ident[:, :])
                for j, w in enumerate((raw_k, raw_v)):
                    for c in range(DC):
                        at = (j * DC + c) * GD
                        tp = pe.transpose(bank[2][:, at:at + GD], w[0:GD, c * P:(c + 1) * P], ident[0:GD, 0:GD])
                tp.then_inc(weight.turned, 1)
                pe.wait_ge(weight.ready, was.ready + DC + 3)
                pe.wait_ge(s.ones, 3)
                cx.tensor_first(pe)
                with pe.Fori(0, BLOCKS) as i:
                    cx.tensor(pe, i)
                    norm.tensor(pe, i)
                    hold(pe, cx.turned, (cx.first + i) * DC + DC)
                    hold(pe, norm.hi, (norm.first + i) * DC + DC)
                    for c in range(DC):
                        mm = pe.matmul(bank[0][0:GD, :], wkT[:, c, :], cT[:, c, :], start=c == 0, stop=c == DC - 1)
                    mm.then_inc(s.k, 1)
                    for b in range(NB):
                        for half in range(2):
                            for c in range(DC):
                                mm = pe.matmul(bank[1][half * SEQ:(half + 1) * SEQ, b * GD:(b + 1) * GD], cT[:, c, b * SEQ:(b + 1) * SEQ], wvT[:, c, :],
                                               start=c == 0, stop=c == DC - 1)
                    mm.then_inc(s.v, 1)
                    for j in range(SETS):
                        for c in range(DC):
                            mm = pe.matmul(bank[4 + j][0:GD, :], wqT[:, c, j, :], xT[:, c, :], start=c == 0, stop=c == DC - 1)
                        mm.then_inc(s.q, 1)
                    hold(pe, s.kblk, i + 1)
                    hold(pe, s.kblk_pool, i + 1)
                    hold(pe, s.vblk, i * 4 + 4)
                    hold(pe, s.qT, i * SETS + SETS)

                    def scores(u):
                        b, pair = divmod(u, PAIRS)
                        if u >= 3:
                            hold(pe, s.shifted, i * UNITS + u - 2)
                        pe.matmul(bank[SOFT_BANK[u % 3]][:, :], qT[0:GD, b, pair, :], kblk[0:GD, b].rearrange("p g k -> p (g k)"),
                                  start=True, stop=True).then_inc(s.score, 1)

                    scores(0)
                    scores(1)
                    for u in range(UNITS + 6):
                        if u + 2 < UNITS:
                            scores(u + 2)
                        if u < UNITS:
                            hold(pe, s.exp, i * UNITS + u + 1)
                            for c in range(SC):
                                tp = pe.transpose(bank[TURN_BANK[u % 2]][:, c * P:(c + 1) * P], prob[:, u % 2, c * P:(c + 1) * P], ident[:, :])
                            tp.then_inc(s.probT_ps, 1)
                        if 1 <= u <= UNITS:
                            b, pair = divmod(u - 1, PAIRS)
                            hold(pe, s.probT, i * UNITS + u)
                            if pair == 0 and b >= 2:
                                hold(pe, s.att, i * NB + b - 1)
                            for c in range(SC):
                                at = (pair * SC + c) * 2 * AUG
                                mm = pe.matmul(bank[READ_BANK[b % 2]][:, at:at + 2 * AUG], probT[:, (u - 1) % 2, c * P:(c + 1) * P],
                                               vblk[:, b, c, :], start=True, stop=True)
                            if pair == PAIRS - 1:
                                mm.then_inc(s.read, 1)
                        if u >= 5 and (u - 5) % 2 == 0 and u < UNITS + 5:
                            b = (u - 5) // 2
                            hold(pe, s.att, i * NB + b + 1)
                            if b >= 2 and b % 2 == 0:
                                hold(pe, done, before[1] + i * BT + b // 2)
                            tp = pe.transpose(bank[OUT_BANK][:, b % 2 * P:(b % 2 + 1) * P], attended[:, b % 2].rearrange("p m k -> p (m k)"), ident[:, :])
                            if b % 2:
                                tp.then_inc(s.attT_ps, 1)
                        if u >= 8 and (u - 8) % 4 == 0:
                            tile = (u - 8) // 4
                            hold(pe, s.attT, i * BT + tile + 1)
                            for m in range(2):
                                pe.matmul(bank[OUT_BANK][:, 2 * P:2 * P + D], attendedT[:, m].rearrange("p b t -> p (b t)"), wfT[:, m, :],
                                          start=m == 0, stop=False)
                            pe.matmul(bank[OUT_BANK][:, 2 * P:2 * P + D], ones[0:1, :], bias_row[0:1, :], start=False, stop=True).then_inc(s.out, 1)
                    pe.sem_inc(cx.free, 1)

            return sync, gpsimd, scalar, vector, tensor

        def layer2_experts(before, done):
            EXPERTS = 7

            def load(sp, n, raw_up, raw_down, signal):
                for mat, (routed, shared) in enumerate((("L2_ffn_W1", "L2_ffn_Ws1"), ("L2_ffn_Wg", "L2_ffn_Wsg"), ("L2_ffn_W2", "L2_ffn_Ws2"))):
                    w = io[shared] if isinstance(n, int) and n == EXPERTS else io[routed][ds(n, 1)].rearrange("o a b -> (o a) b")
                    sp.dma_start(raw_down if mat == 2 else raw_up[:, mat], w.rearrange("(c p) h -> p c h", p=P)).then_inc(signal, 16)
            load.count = 3

            return gated_experts("f2", 5, 2, gates[:, 6:7], before, done, EXPERTS, 3,
                                 (False, io["L2_ffn_gate_w"], io["L2_ffn_gate_b"], io["L2_ffn_biases"]),
                                 chunks=[(0, P), (P, P)], outputs=[[(0, 0, P)], [(0, 0, P)]], groups=EXPERTS + 1,
                                 load=load, up_width=2 * P, down_chunks=2)

        def layer3_attention(before, done):
            NB = BLK // SEQ
            STEPS = int(np.log2(SEQ))
            lay = Layout()
            w_in, w_out = lay(DC, D), lay(DC, D)
            power, series = lay(STEPS), lay(SEQ)
            weigh = lay(SEQ)
            row_weight, weight_sum, weights = lay(1), lay(1), lay(2)
            pooled, state, summary = lay(DC, BATCH), lay(DC, BATCH), lay(BLOCKS, D)
            weight_sums = lay(BATCH)
            gain, offset = lay(D), lay(D)
            shifted, normed = lay(BT, D), lay(BT, D)
            stat, mean_var, rstd = lay(BT, 6), lay(BT, 2), lay(BT)
            var_eps = lay(BT)
            decay = lay(1)
            of_row = lay(SEQ)
            of_half = lay(2)
            spread = lay(BT, P)[0:NB]
            bias_in = lay(D)[0:1]
            bias_out = lay(D)[0:1]
            affine = lay(2, D)
            assert lay.at <= L3_ATTENTION, lay.at
            norm = make_norm(6)
            s = Names()
            (
                s.masks, s.keep, s.chain, s.pooled_ps, s.pooled, s.state_ps, s.state, s.summary_ps, s.summary,
                s.spread, s.y, s.stat, s.rstd, s.normed, s.scaled, s.affine, s.acc
            ) = sems("a3",
                 "masks keep chain pooled_ps pooled state_ps state summary_ps summary spread y stat rstd "
                 "normed scaled affine acc")
            was = count_weights(loaded=16 * 7, turned=1, ready=2)
            raw_in, raw_out = raw[:, 0:DC * D].rearrange("p (a k) -> p a k", a=DC), raw[:, DC * D:2 * DC * D].rearrange("p (a k) -> p a k", a=DC)
            ctx_buf = (ctx_in, ctx_sb)
            s.ctx = [sem(f"a3_ctx{j}") for j in range(2)]

            def sync(sp):
                sp.wait_ge(*before)
                for i in range(2):
                    sp.dma_start(ctx_buf[i][:, :, :], io["ctx_2048"].rearrange("b s d -> (b s) d").rearrange("(i k p) d -> i p k d", k=BT, p=P)[i]).then_inc(s.ctx[i % 2], 16)
                sp.dma_start(decay[:, :], io["L3_xattn_decay"].partition_broadcast(P)).then_inc(weight.loaded, 16)
                sp.dma_start(raw_in, io["L3_xattn_W_in"].rearrange("(a p) k -> p a k", p=P)).then_inc(weight.loaded, 16)
                sp.dma_start(raw_out, io["L3_xattn_W_out"].rearrange("(a p) k -> p a k", p=P)).then_inc(weight.loaded, 16)
                sp.dma_start(bias_in[:, :], io["L3_xattn_b_in"].partition_broadcast(1)).then_inc(weight.loaded, 16)
                sp.dma_start(bias_out[:, :], io["L3_xattn_b_out"].partition_broadcast(1)).then_inc(weight.loaded, 16)
                sp.dma_start(affine[:, 0, :], io["L3_xattn_gamma"].partition_broadcast(P)).then_inc(weight.loaded, 16)
                sp.dma_start(affine[:, 1, :], io["L3_xattn_beta"].partition_broadcast(P)).then_inc(weight.loaded, 16)
                for i in range(2, BLOCKS):
                    sp.wait_ge(s.pooled_ps, i - 1)
                    sp.dma_start(ctx_buf[i % 2][:, :, :], io["ctx_2048"].rearrange("b s d -> (b s) d").rearrange("(i k p) d -> i p k d", k=BT, p=P)[i]).then_inc(s.ctx[i % 2], 16)

            def gpsimd(pool):
                pool.wait_ge(*before)
                pool.memset(of_row[:, :], 0.0).then_inc(s.masks, 1)
                pool.memset(spread[:, :, :], 0.0).then_inc(s.masks, 1)
                pool.wait_ge(s.masks, 2)
                at = spread[:, :, :].rearrange("r k (h t) -> r k h t", h=2)
                pool.affine_select(out=at, in_=at, compare_op=ALU.not_equal, fill=1.0, base=0,
                                   pattern=[[2, BT], [1, 2], [0, SEQ]], channel_multiplier=-1).then_inc(s.masks, 1)
                for h in range(2):
                    pool.wait_ge(s.masks, 3 + h)
                    pool.affine_select(out=of_row[:, :], in_=of_row[:, :], compare_op=ALU.not_equal, fill=1.0,
                                       base=1 - SEQ * (h + 1), pattern=[[1, SEQ]], channel_multiplier=1).then_inc(s.masks, 1)
                pool.wait_ge(s.affine, 2)
                with pool.Fori(0, BLOCKS) as i:
                    norm.gpsimd(pool, i)
                    hold(pool, s.stat, i * 2 * BT + 2 * BT)
                    pool.tensor_scalar(var_eps, mean_var[:, :, 1], LN_EPS, 1.0, ALU.add, ALU.mult).then_inc(s.rstd, 1)
                    pool.wait_ge(s.rstd, i * 2 + 1)
                    pool.tensor_tensor(rstd, var_eps, neg_half[:, :], ALU.pow).then_inc(s.rstd, 1)
                    pool.wait_ge(s.normed, i * BT + BT)
                    pool.tensor_tensor(normed, normed, gain.unsqueeze(1).to_broadcast([P, BT, D]), ALU.mult).then_inc(s.scaled, 1)
                    pool.wait_ge(s.scaled, i * 2 + 1)
                    pool.tensor_tensor(normed, normed, offset.unsqueeze(1).to_broadcast([P, BT, D]), ALU.add).then_inc(s.scaled, 1)

            def scalar(act):
                act.wait_ge(weight.loaded, was.loaded + 16 * 7)
                act.activation(decay[:, :], decay[:, :], ACT.Sigmoid).then_inc(s.keep, 1)
                act.wait_ge(weight.turned, was.turned + 1)
                act.activation(flat(w_in), bank[0][:, :], ACT.Copy).then_inc(weight.ready, 1)
                act.activation(flat(w_out), bank[1][:, :], ACT.Copy).then_inc(weight.ready, 1)
                act.wait_ge(s.pooled_ps, BLOCKS)
                act.activation(flat(pooled), bank[2][:, 0:DC * BATCH], ACT.Copy).then_inc(s.pooled, 1)
                act.wait_ge(s.summary_ps, 1)
                for h in range(2):
                    act.activation(flat(summary[0:NB, 2 * h:2 * h + 2, :]), bank[4 + h][0:NB, :], ACT.Copy).then_inc(s.summary, 1)

            def vector(dve):
                dve.wait_ge(*before)
                dve.wait_ge(s.keep, 1)
                dve.wait_ge(s.masks, 5)
                link = linker(dve, s.chain)
                link(dve.memset(of_half[:, :], 0.0))
                link(dve.memset(of_half[0:SEQ, 0:1], 1.0))
                link(dve.memset(of_half[SEQ:P, 1:2], 1.0))
                link(dve.tensor_copy(power[:, 0:1], decay[:, :]))
                for n in range(1, STEPS):
                    link(dve.tensor_tensor(power[:, n:n + 1], power[:, n - 1:n], power[:, n - 1:n], ALU.mult))
                link(dve.memset(series[:, 0:1], 1.0))
                for n in range(STEPS):
                    m = 1 << n
                    link(dve.tensor_scalar(series[:, m:2 * m], series[:, 0:m], power[:, n:n + 1], series[:, m - 1:m], ALU.mult, ALU.add))
                link(dve.tensor_reduce(weight_sum, series, AX.X, ALU.add))
                link(dve.tensor_tensor(weigh, series, of_row[:, :], ALU.mult))
                link(dve.tensor_reduce(row_weight, weigh, AX.X, ALU.add))
                link(dve.tensor_scalar(weights, of_half[:, :], row_weight, 1.0 / SEQ, ALU.mult, ALU.mult))
                link(dve.tensor_scalar(weight_sums, ones[:, 0:BATCH], weight_sum, 1.0 / SEQ, ALU.mult, ALU.mult))
                dve.tensor_scalar(gain, affine[:, 0, :], gates[:, 3:4], None, ALU.mult).then_inc(s.affine, 1)
                dve.tensor_scalar(offset, affine[:, 1, :], gates[:, 3:4], None, ALU.mult).then_inc(s.affine, 1)
                dve.wait_ge(s.state_ps, 1)
                for c in range(DC):
                    dve.tensor_copy(state[:, c, :], bank[3][:, c * BATCH:(c + 1) * BATCH]).then_inc(s.state, 1)
                dve.sem_inc(s.y, 1)
                with dve.Fori(0, BLOCKS) as i:
                    norm.vector_norm(dve, i)
                    for k in range(BT):
                        if k % 2 == 0:
                            dve.wait_ge(s.spread, i * 2 + k // 2 + 1)
                        if k == 0:
                            dve.wait_ge(norm.xn, (norm.first + i) * BT + BT)
                        dve.tensor_tensor(shifted[:, k, :], xn[:, k, :], bank[6 + k // 2][:, k % 2 * D:k % 2 * D + D], ALU.add).then_inc(s.y, 1)
                    dve.wait_ge(s.y, i * BT + BT + 1)
                    for k in range(BT):
                        dve.bn_stats(stat[:, k, :], shifted[:, k, :]).then_inc(s.stat, 1)
                    hold(dve, s.stat, i * 2 * BT + BT)
                    for k in range(BT):
                        dve.bn_aggr(mean_var[:, k, :], stat[:, k, :]).then_inc(s.stat, 1)
                    dve.wait_ge(s.rstd, i * 2 + 2)
                    for k in range(BT):
                        dve.tensor_scalar(normed[:, k, :], shifted[:, k, :], mean_var[:, k, 0:1], rstd[:, k:k + 1],
                                          ALU.subtract, ALU.mult).then_inc(s.normed, 1)
                    dve.wait_ge(s.scaled, i * 2 + 2)
                    tiles = X[:, ds(i * BT, BT), :]
                    dve.tensor_tensor(tiles, tiles, normed, ALU.add).then_inc(s.acc, 1)
                dve.wait_ge(s.acc, BLOCKS)
                dve.sem_inc(done, TILES)

            def tensor(pe):
                pe.wait_ge(*before)
                pe.wait_ge(weight.loaded, was.loaded + 16 * 7)
                for j, w in enumerate((raw_in, raw_out)):
                    for c in range(DC):
                        for a in range(DC):
                            tp = pe.transpose(bank[j][:, c * D + a * P:c * D + (a + 1) * P], w[:, a, c * P:(c + 1) * P], ident[:, :])
                tp.then_inc(weight.turned, 1)
                pe.wait_ge(weight.turned, was.turned + 1)
                pe.sem_inc(weights_free, 1)
                pe.wait_ge(s.chain, 2 * STEPS + 9)
                for i in range(BLOCKS):
                    pe.wait_ge(s.ctx[i % 2], 16 * (i // 2 + 1))
                    for k in range(BT):
                        for c in range(DC):
                            at = c * BATCH + (i * BT + k) * 2
                            mm = pe.matmul(bank[2][:, at:at + 2], ctx_buf[i % 2][:, k, c * P:(c + 1) * P], weights, start=True, stop=True)
                    mm.then_inc(s.pooled_ps, 1)
                pe.wait_ge(s.pooled, 1)
                pe.wait_ge(weight.ready, was.ready + 2)
                for m in range(DC):
                    for c in range(DC):
                        pe.matmul(bank[3][:, m * BATCH:(m + 1) * BATCH], w_in[:, c, m * P:(m + 1) * P], pooled[:, c, :],
                                  start=c == 0, stop=False)
                    mm = pe.matmul(bank[3][:, m * BATCH:(m + 1) * BATCH], bias_in[0:1, m * P:(m + 1) * P], weight_sums[0:1, :],
                                   start=False, stop=True)
                mm.then_inc(s.state_ps, 1)
                pe.wait_ge(s.state, DC)
                for i in range(BLOCKS):
                    out = bank[4 + i // 2][0:NB, i % 2 * D:i % 2 * D + D]
                    for c in range(DC):
                        pe.matmul(out, state[:, c, i * NB:(i + 1) * NB], w_out[:, c, :], start=c == 0, stop=False)
                    mm = pe.matmul(out, ones[0:1, 0:NB], bias_out[0:1, :], start=False, stop=True)
                mm.then_inc(s.summary_ps, 1)
                pe.wait_ge(s.summary, 2)
                with pe.Fori(0, BLOCKS) as i:
                    hold(pe, s.y, i * BT + 1)
                    for k in range(BT):
                        mm = pe.matmul(bank[6 + k // 2][:, k % 2 * D:k % 2 * D + D], spread[:, k, :], flat(summary[0:NB, ds(i, 1), :]),
                                       start=True, stop=True)
                        if k % 2:
                            mm.then_inc(s.spread, 1)

            return sync, gpsimd, scalar, vector, tensor

        def layer3_experts(before, done):
            I = 1024
            IC = I // P
            MAT = I * D // P
            UP, DOWN = 0, 1
            HALF = I // 2
            lay = Layout()
            lay.at = L3_ATTENTION
            xqT = lay(DC, TOK, dt=BF16)
            quant = make_quant(1, lay, xqT)
            norm = make_norm(7)
            up_w, down_w = lay(DC, I, dt=BF16), lay(IC, D, dt=BF16)
            tern = lay(2, MAT, dt=BF16)
            size_sum, mean, per_mean, out_factor = lay(2), lay(2), lay(2), lay(1)
            gelu_scale = lay(TILES)
            hidden, shifted, wholeT = lay(2, I), lay(2, I), lay(2, I, dt=BF16)
            peak, unit, rate, out_scale = lay(2), lay(2), lay(2), lay(2)
            s = Names()
            (
                s.raw, s.size, s.total, s.chain, s.ternary, s.tern, s.shifted, s.w_tp, s.w, s.up, s.relu, s.once,
                s.prod, s.peak, s.pair, s.rate, s.turned, s.wholeT, s.down, s.acc
            ) = whole_sems
            was = whole_used
            raw_m = raw[:, 0:2 * MAT].rearrange("p (m k) -> p m k", m=2)
            stored = sem("stored")

            def sync(sp):
                sp.wait_ge(weights_free, 1)
                for m, w in ((UP, "L3_ffn_w1"), (DOWN, "L3_ffn_w2")):
                    sp.dma_start(raw_m[:, m, :].rearrange("p (a k) -> p a k", k=I if m == DOWN else D),
                                 io[w].rearrange("(a p) k -> p a k", p=P)).then_inc(s.raw, 16)
                with sp.Fori(0, BLOCKS) as i:
                    sp.wait_ge(s.acc, was.acc + i * BT + BT)
                    sp.dma_start(block_of(io["out"], i), X[:, ds(i * BT, BT), :]).then_inc(stored, 16)
                sp.wait_ge(stored, 16 * BLOCKS)

            def gpsimd(pool):
                with pool.Fori(0, BLOCKS) as i:
                    norm.gpsimd(pool, i)
                    quant.gpsimd(pool, i)

            def scalar_gelu(act, T, k):
                act.wait_ge(s.up, was.up + T + 1)
                act.wait_ge(s.shifted, was.shifted + T - 1)
                for h in range(2):
                    act.activation(hidden[:, k % 2, h * HALF:(h + 1) * HALF], bank[2 * (k % 2) + h][:, :], ACT.Gelu,
                                   scale=gelu_scale[:, ds(T, 1)]).then_inc(s.relu, 1)

            def scalar_back(act, T, k):
                act.wait_ge(s.turned, was.turned + T + 1)
                for h in range(2):
                    act.activation(wholeT[:, k % 2, h * HALF:(h + 1) * HALF], bank[4 + h][:, :], ACT.Copy, bias=-MAGIC).then_inc(s.wholeT, 1)

            def vector_front(dve, T, k):
                j = slice(k % 2, k % 2 + 1)
                dve.wait_ge(s.relu, was.relu + T * 2 + 2)
                dve.tensor_reduce(peak[:, j], hidden[:, k % 2, :], AX.X, ALU.max, apply_absolute_value=True).then_inc(s.peak, 1)
                dve.wait_ge(s.peak, was.peak + T + 1)
                dve.tensor_scalar(unit[:, j], peak[:, j], QUANT_EPS, 1.0 / 127, ALU.max, ALU.mult).then_inc(s.pair, 1)
                hold(dve, s.pair, was.pair + T * 2 + 1)
                dve.reciprocal(rate[:, j], unit[:, j]).then_inc(s.rate, 1)
                dve.tensor_scalar(out_scale[:, j], unit[:, j], out_factor, None, ALU.mult).then_inc(s.pair, 1)
                dve.wait_ge(s.rate, was.rate + T + 1)
                dve.tensor_scalar(shifted[:, k % 2, :], hidden[:, k % 2, :], rate[:, j], MAGIC, ALU.mult, ALU.add).then_inc(s.shifted, 1)

            def vector_back(dve, T, k):
                dve.wait_ge(s.down, was.down + T + 1)
                dve.wait_ge(s.pair, was.pair + T * 2 + 2)
                dve.scalar_tensor_tensor(x_tile(T), bank[6 + k % 2][:, 0:D], out_scale[:, k % 2:k % 2 + 1], x_tile(T),
                                         ALU.mult, ALU.add).then_inc(s.acc, 1)

            def tensor_up(pe, T, k):
                hold(pe, s.relu, was.relu + T * 2 - 2)
                for h in range(2):
                    for c in range(DC):
                        mm = pe.matmul(bank[2 * (k % 2) + h][:, :], flat(xqT[:, c:c + 1, ds(T * P, P)]), up_w[:, c, h * HALF:(h + 1) * HALF],
                                       start=c == 0, stop=c == DC - 1)
                mm.then_inc(s.up, 1)

            def tensor_turn(pe, T, k):
                hold(pe, s.shifted, was.shifted + T + 1)
                for c in range(IC):
                    tp = pe.transpose(bank[4 + c // 4][:, c % 4 * P:(c % 4 + 1) * P], shifted[:, k % 2, c * P:(c + 1) * P], ident[:, :])
                tp.then_inc(s.turned, 1)

            def tensor_down(pe, T, k):
                hold(pe, s.wholeT, was.wholeT + T * 2 + 2)
                hold(pe, s.acc, was.acc + T - 1)
                for c in range(IC):
                    mm = pe.matmul(bank[6 + k % 2][:, 0:D], wholeT[:, k % 2, c * P:(c + 1) * P], down_w[:, c, :],
                                   start=c == 0, stop=c == IC - 1)
                mm.then_inc(s.down, 1)

            def over_blocks(eng, step):
                with eng.Fori(0, BLOCKS - 1) as i:
                    step(i, True)
                step(BLOCKS - 1, False)

            def scalar(act):
                act.wait_ge(s.raw, was.raw + 32)
                for m in range(2):
                    act.activation(tern[:, m, :], raw_m[:, m, :], ACT.Abs, accum_out=size_sum[:, m:m + 1]).then_inc(s.size, 1)
                with act.Fori(0, BLOCKS) as i:
                    quant.scalar(act, i)
                    quant.scalar_last(act, i)
                for q in range(4):
                    act.wait_ge(s.w_tp, was.w_tp + q + 1)
                    to = up_w[:, q, :] if q < 2 else flat(down_w[:, q % 2 * IC // 2:(q % 2 + 1) * IC // 2, :])
                    act.activation(to, bank[4 + q][:, :].bitcast(BF16), ACT.Copy).then_inc(s.w, 1)
                for T in range(2):
                    scalar_gelu(act, T, T)

                def step(i, more):
                    for k in range(BT):
                        T = i * BT + k
                        scalar_back(act, T, k)
                        if k + 2 < BT or more:
                            scalar_gelu(act, T + 2, k)
                over_blocks(act, step)

            def vector(dve):
                dve.wait_ge(*before)
                dve.wait_ge(s.total, was.total + 1)
                link = linker(dve, s.chain, was.chain)
                link(dve.tensor_scalar(mean, bank[0][:, 0:2], 1.0 / (I * D), QUANT_EPS, ALU.mult, ALU.max))
                link(dve.reciprocal(per_mean, mean))
                link(dve.tensor_scalar(out_factor, mean[:, DOWN:DOWN + 1], gates[:, 7:8], None, ALU.mult))
                for m in range(2):
                    w = raw_m[:, m, :]
                    link(dve.tensor_scalar(w, w, per_mean[:, m:m + 1], MAGIC, ALU.mult, ALU.add))
                    link(dve.tensor_scalar(tern[:, m, :], w, MAGIC, -1.0, ALU.subtract, ALU.max))
                    dve.tensor_scalar(tern[:, m, :], tern[:, m, :], 1.0, None, ALU.min).then_inc(s.tern, 1)
                with dve.Fori(0, BLOCKS) as i:
                    norm.vector_norm(dve, i)
                    quant.vector(dve, norm, i)
                dve.wait_ge(quant.chain, 2 * 2 * BLOCKS)
                link(dve.tensor_scalar(gelu_scale, quant.step, mean[:, UP:UP + 1], None, ALU.mult))
                vector_front(dve, 0, 0)

                def step(i, more):
                    for k in range(BT):
                        T = i * BT + k
                        if k + 1 < BT or more:
                            vector_front(dve, T + 1, k + 1)
                        vector_back(dve, T, k)
                over_blocks(dve, step)
                dve.wait_ge(s.acc, was.acc + TILES)
                dve.sem_inc(done, TILES)

            def tensor(pe):
                hold(pe, s.size, was.size + 2)
                pe.matmul(bank[0][:, 0:2], ones[:, :], size_sum, start=True, stop=True).then_inc(s.total, 1)
                with pe.Fori(0, BLOCKS) as i:
                    quant.tensor(pe, i)
                pe.wait_ge(quant.turned, quant.first + BLOCKS)
                for q in range(4):
                    m, half = divmod(q, 2)
                    pe.wait_ge(s.tern, was.tern + m + 1)
                    for j in range(IC):
                        at = j * D + half * P if m == UP else (j % 2) * I + (half * IC // 2 + j // 2) * P
                        tp = pe.transpose(bank[4 + q][:, :].bitcast(BF16)[:, j * P:(j + 1) * P], tern[:, m, at:at + P], identb[:, :])
                    tp.then_inc(s.w_tp, 1)
                pe.wait_ge(s.w, was.w + 4)
                pe.wait_ge(s.chain, was.chain + 8)
                for T in range(2):
                    tensor_up(pe, T, T)

                def step(i, more):
                    for k in range(BT):
                        T = i * BT + k
                        tensor_turn(pe, T, k)
                        if k + 2 < BT or more:
                            tensor_up(pe, T + 2, k)
                        tensor_down(pe, T, k)
                over_blocks(pe, step)

            return sync, gpsimd, scalar, vector, tensor

        done = sem("done")
        makers = [layer0_attention, layer0_experts, layer1_attention, layer1_experts,
                  layer2_attention, layer2_experts, layer3_attention, layer3_experts]
        sublayers = [make((done, j * TILES), done) for j, make in enumerate(makers)]

        block = ctx.enter_context(nc.Block())

        @block.sync
        def _(sp):
            setup_sync(sp)
            for sublayer in sublayers:
                sublayer[SYNC](sp)

        @block.gpsimd
        def _(pool):
            setup_gpsimd(pool)
            for sublayer in sublayers:
                sublayer[GPSIMD](pool)

        @block.scalar
        def _(act):
            setup_scalar(act)
            for sublayer in sublayers:
                sublayer[SCALAR](act)

        @block.vector
        def _(dve):
            setup_vector(dve)
            for sublayer in sublayers:
                sublayer[VECTOR](dve)

        @block.tensor
        def _(pe):
            setup_tensor(pe)
            for sublayer in sublayers:
                sublayer[TENSOR](pe)


INPUTS = ("x", "ctx_2048", "mask_BxS2_bk0", "g_xattn", "g_ffn",
          "L0_ffn_gate_w", "L0_ffn_w1", "L0_ffn_w3", "L0_ffn_w2", "L0_ffn_sw1", "L0_ffn_sw3", "L0_ffn_sw2",
          "L1_xattn_Wq", "L1_xattn_Wg", "L1_xattn_bg", "L1_xattn_Wkv", "L1_xattn_Wo",
          "L1_ffn_router_w", "L1_ffn_gate_w", "L1_ffn_up_w", "L1_ffn_down_w",
          "L2_xattn_Wq", "L2_xattn_Wk", "L2_xattn_Wv", "L2_xattn_Wfc", "L2_xattn_bfc",
          "L2_ffn_W1", "L2_ffn_Wg", "L2_ffn_W2", "L2_ffn_Ws1", "L2_ffn_Wsg", "L2_ffn_Ws2",
          "L2_ffn_gate_w", "L2_ffn_gate_b", "L2_ffn_biases",
          "L3_xattn_decay", "L3_xattn_W_in", "L3_xattn_b_in", "L3_xattn_W_out", "L3_xattn_b_out",
          "L3_xattn_gamma", "L3_xattn_beta", "L3_ffn_w1", "L3_ffn_w2")


def kernel(**inputs):
    import concourse.bacc as bacc
    from concourse.bass_utils import run_bass_kernel_spmd

    nc = bacc.Bacc("TRN2", target_bir_lowering=False, num_devices=1)
    arrays, io = {}, {}
    for name in INPUTS:
        a = np.ascontiguousarray(inputs[name])
        if a.ndim == 0:
            a = a.reshape(1)
        arrays["in_" + name] = a
        io[name] = nc.dram_tensor("in_" + name, a.shape, mybir.dt.from_np(a.dtype), kind="ExternalInput").ap()
    io["out"] = nc.dram_tensor("out", (BATCH, SEQ, D), F32, kind="ExternalOutput").ap()
    build_program(nc, io)
    return run_bass_kernel_spmd(nc, [arrays], core_ids=[0]).results[0]["out"]
```

```python
from contextlib import ExitStack

import numpy as np

import concourse.bass as bass
from concourse import mybir

ACT = mybir.ActivationFunctionType
ALU = mybir.AluOpType
AX = mybir.AxisListType
F32 = mybir.dt.float32
F32R = mybir.dt.float32r
BF16 = mybir.dt.bfloat16
U8 = mybir.dt.uint8
ds = bass.ds

P = 128
D = 256
DC = D // P
BATCH, SEQ = 32, 64
TOK = BATCH * SEQ
TILES = TOK // P
BT = 4
BLK = BT * P
BLOCKS = TILES // BT
LN_EPS = 1e-5
QUANT_EPS = 1e-5
MAGIC = 1.5 * 2.0 ** 23
L0_I = 176
PAIR = 2 * L0_I + 16
RAW = 4096
SPLIT = 2 * DC * 3 * P + 3 * D
SYNC, GPSIMD, SCALAR, VECTOR, TENSOR = range(5)
WORK = 19600
L1_RAW = 14000
L3_ATTENTION = 6600


class Names:
    pass


def build_program(nc, io):
    ctx = ExitStack()
    with ctx:
        def sb(name, shape, dt=F32):
            return ctx.enter_context(nc.sbuf_tensor(name, shape, dt))

        def sem(name):
            return ctx.enter_context(nc.semaphore(name))

        def sems(prefix, names):
            return [sem(prefix + "_" + name) for name in names.split()]

        X = sb("resid", [P, TILES, D])
        ident = sb("ident", [P, P])
        identb = sb("identb", [P, P], BF16)
        ones = sb("ones", [P, P])
        neg_half = sb("neg_half", [P, TILES])
        magic = sb("magic", [P, 1])
        gates = sb("gates", [P, 8])
        xn = sb("xn", [P, BT, D])
        ln_stat = sb("ln_stat", [P, TILES, 6])
        ln_mv = sb("ln_mv", [P, TILES, 2])
        ln_ve = sb("ln_ve", [P, TILES])
        ln_rstd = sb("ln_rstd", [P, TILES])
        xhi = sb("xhi", [P, DC, TOK], F32R)
        xlo = sb("xlo", [P, DC, TOK], F32R)
        ctx_in = sb("ctx_in", [P, BT, D])
        ctx_sb = sb("ctx_sb", [P, BT, D])
        work = sb("work", [P, WORK])
        raw = sb("raw", [P, RAW])
        whi = sb("whi", [P, 2, SPLIT], F32R)
        wlo = sb("wlo", [P, 2, SPLIT], F32R)
        ahi = sb("ahi", [P, 2, BLK], F32R)
        alo = sb("alo", [P, 2, BLK], F32R)
        route_hi = sb("route_hi", [P, DC, P], F32R)
        route_lo = sb("route_lo", [P, DC, P], F32R)
        bank = [ctx.enter_context(nc.psum_tensor(f"bank{i}", [P, 512], F32)) for i in range(8)]

        class Layout:

            def __init__(self):
                self.at = 0

            def __call__(self, *shape, dt=F32):
                n = int(np.prod(shape))
                n32 = n if dt == F32 else (n + 1) // 2
                v = work[:, self.at:self.at + n32]
                self.at += n32
                assert self.at <= WORK, self.at
                if dt != F32:
                    v = v.bitcast(dt)
                if len(shape) == 2:
                    v = v.rearrange("p (a b) -> p a b", a=shape[0])
                if len(shape) == 3:
                    v = v.rearrange("p (a b c) -> p a b c", a=shape[0], b=shape[1])
                if len(shape) == 4:
                    v = v.rearrange("p (a b c d) -> p a b c d", a=shape[0], b=shape[1], c=shape[2])
                return v

        def flat(ap):
            return ap.rearrange("p a b -> p (a b)")

        def x_tile(t):
            return flat(X[:, ds(t, 1), :])

        def block_of(dram, i):
            v = dram.rearrange("b s d -> (b s) d").rearrange("(i k p) d -> i p k d", k=BT, p=P)
            return v[ds(i, 1)].rearrange("o p k d -> p (o k) d")

        passed = sem("passed")

        def hold(eng, s, value):
            eng.wait_ge(s, value)
            eng.sem_inc(passed, 1)

        def linker(eng, s, base=0):
            count = [0]

            def link(ins):
                ins.then_inc(s, 1)
                count[0] += 1
                eng.wait_ge(s, base + count[0])
            link.count = count
            return link

        weight = Names()
        weight.loaded, weight.turned, weight.ready = sems("weight", "loaded turned ready")
        weight_counts = [(0, 0, 0)]

        def count_weights(loaded, turned, ready):
            was = Names()
            was.loaded, was.turned, was.ready = weight_counts[-1]
            weight_counts.append((was.loaded + loaded, was.turned + turned, was.ready + ready))
            return was

        x_loaded, g_loaded = sem("x_loaded"), sem("g_loaded")
        const_set, gates_set, ident_set = sem("const_set"), sem("gates_set"), sem("ident_set")

        def setup_sync(sp):
            for i in range(BLOCKS):
                sp.dma_start(X[:, BT * i:BT * i + BT, :], block_of(io["x"], i)).then_inc(x_loaded, 16)
            sp.dma_start(gates[:, 0:4], io["g_xattn"].partition_broadcast(P)).then_inc(g_loaded, 16)
            sp.dma_start(gates[:, 4:8], io["g_ffn"].partition_broadcast(P)).then_inc(g_loaded, 16)

        def setup_gpsimd(pool):
            pool.memset(ident[:, :], 0.0).then_inc(const_set, 1)
            pool.memset(ones[:, :], 1.0).then_inc(const_set, 1)
            pool.memset(neg_half[:, :], -0.5).then_inc(const_set, 1)
            pool.memset(magic[:, :], MAGIC).then_inc(const_set, 1)
            pool.wait_ge(const_set, 4)
            pool.affine_select(out=ident[:, :], in_=ident[:, :], compare_op=ALU.not_equal, fill=1.0, base=0,
                               pattern=[[-1, P]], channel_multiplier=1).then_inc(ident_set, 1)
            pool.wait_ge(ident_set, 1)
            pool.tensor_copy(identb[:, :], ident[:, :]).then_inc(ident_set, 1)

        def setup_scalar(act):
            act.wait_ge(g_loaded, 32)
            act.activation(gates[:, :], gates[:, :], ACT.Tanh).then_inc(gates_set, 1)

        def setup_vector(dve):
            dve.wait_ge(x_loaded, 16 * BLOCKS)
            dve.wait_ge(gates_set, 1)

        def setup_tensor(pe):
            pe.wait_ge(ident_set, 2)

        norm_sems = sems("norm", "stat rstd xn tp hi lo")

        def make_norm(sublayer, parts=None, split=None, turn=0):
            n = Names()
            n.stat, n.rstd, n.xn, n.tp, n.hi, n.lo = norm_sems
            n.first = sublayer * BLOCKS
            n.first_tp = turn * BLOCKS
            n.first_lo = (split or 0) * BLOCKS
            n.rstd_there = sublayer * 2 + 2

            def vector_stats(dve):
                for t in range(TILES):
                    dve.bn_stats(ln_stat[:, t, :], X[:, t, :]).then_inc(n.stat, 1)
                dve.wait_ge(n.stat, sublayer * 2 * TILES + TILES)
                for t in range(TILES):
                    dve.bn_aggr(ln_mv[:, t, :], ln_stat[:, t, :]).then_inc(n.stat, 1)

            def gpsimd_stats(pool):
                pool.wait_ge(n.stat, (sublayer + 1) * 2 * TILES)
                pool.tensor_scalar(ln_ve[:, :], ln_mv[:, :, 1], LN_EPS, 1.0, ALU.add, ALU.mult).then_inc(n.rstd, 1)
                pool.wait_ge(n.rstd, sublayer * 2 + 1)
                pool.tensor_tensor(ln_rstd[:, :], ln_ve[:, :], neg_half[:, :], ALU.pow).then_inc(n.rstd, 1)

            def vector_norm(dve, i, into=xn):
                dve.wait_ge(n.rstd, n.rstd_there)
                for k in range(BT):
                    t = i * BT + k
                    dve.tensor_scalar(into[:, k, :], x_tile(t), flat(ln_mv[:, ds(t, 1), 0:1]), ln_rstd[:, ds(t, 1)],
                                      ALU.subtract, ALU.mult).then_inc(n.xn, 1)

            def vector_rest(dve, i, at=0):
                for c in range(DC):
                    dve.wait_ge(n.hi, (n.first_tp + i) * DC + c + 1)
                    dve.tensor_tensor(flat(xlo[:, c:c + 1, ds(i * BLK, BLK)]), bank[at + c][:, :],
                                      flat(xhi[:, c:c + 1, ds(i * BLK, BLK)]).bitcast(F32),
                                      ALU.subtract).then_inc(n.lo, 1)

            def tensor(pe, i, tiles=xn, at=0):
                for c in range(DC):
                    for k in range(BT):
                        if c == 0:
                            pe.wait_ge(n.xn, (n.first + i) * BT + k + 1)
                        tp = pe.transpose(bank[at + c][:, k * P:(k + 1) * P], tiles[:, k, c * P:(c + 1) * P], ident[:, :])
                    tp.then_inc(n.tp, 1)

            def scalar(act, i, at=0):
                for c in range(DC):
                    act.wait_ge(n.tp, (n.first_tp + i) * DC + c + 1)
                    to = flat(xhi[:, c:c + 1, ds(i * BLK, BLK)]) if parts is None else parts[:, c, :]
                    act.activation(to, bank[at + c][:, :], ACT.Copy).then_inc(n.hi, 1)

            n.vector_stats, n.gpsimd_stats = vector_stats, gpsimd_stats
            n.vector_norm, n.vector_rest, n.tensor, n.scalar = vector_norm, vector_rest, tensor, scalar
            return n

        ctx_sems = sems("ctx", "arrived in_free ready free tp turned")

        def make_context(use, dst):
            n = Names()
            n.arrived, n.in_free, n.ready, n.free, n.tp, n.turned = ctx_sems
            n.first = use * BLOCKS

            def sync(sp):
                with sp.Fori(0, BLOCKS) as i:
                    sp.wait_ge(n.in_free, n.first + i + 1)
                    sp.dma_start(ctx_in[:, :, :], block_of(io["ctx_2048"], i)).then_inc(n.arrived, 16)

            def gpsimd_first(pool):
                if use == 0:
                    pool.sem_inc(n.in_free, 1)

            def gpsimd(pool, i):
                g = n.first + i
                hold(pool, n.arrived, g * 16 + 16)
                hold(pool, n.free, g + 1)
                pool.tensor_copy(ctx_sb[:, :, :], ctx_in[:, :, :]).then_inc(n.ready, 1)
                pool.wait_ge(n.ready, g + 1)
                pool.sem_inc(n.in_free, 1)

            def tensor_first(pe):
                if use == 0:
                    pe.sem_inc(n.free, 1)

            def tensor(pe, i):
                pe.wait_ge(n.ready, n.first + i + 1)
                for c in range(DC):
                    for k in range(BT):
                        tp = pe.transpose(bank[2 + c][:, k * P:(k + 1) * P], ctx_sb[:, k, c * P:(c + 1) * P], ident[:, :])
                    tp.then_inc(n.tp, 1)

            def scalar(act, i):
                for c in range(DC):
                    act.wait_ge(n.tp, (n.first + i) * DC + c + 1)
                    act.activation(dst[:, c, :], bank[2 + c][:, :], ACT.Copy).then_inc(n.turned, 1)

            n.sync, n.gpsimd_first, n.gpsimd, n.tensor_first, n.tensor, n.scalar = sync, gpsimd_first, gpsimd, tensor_first, tensor, scalar
            return n

        ctx_here = sems("ctx_here", "0 1 2 3")
        RING_LOADS = 16 * TILES // 4

        def layer0_attention(before, done):
            lay = Layout()
            xT, cT = lay(DC, BLK), lay(DC, BLK)
            same_batch = lay(P)
            mask = lay(BT, P)
            mask_low = lay(BT, P)
            seen = lay(BT)
            score, prob, probT = lay(BT, P), lay(BT, P), lay(BT, P)
            neg_max, total, inv, scale = lay(BT), lay(BT), lay(BT), lay(BT)
            mask_in = sb("mask_in", [P, TILES, P], U8)
            norm = make_norm(0, xT, turn=0)
            cx = make_context(0, cT)
            s = Names()
            s.mask_in, s.same, s.mask, s.score, s.soft, s.exp, s.probT_ps, s.probT, s.out, s.x = sems("a0", "mask_in same mask score soft exp probT_ps probT out x")
            SOFT = 5

            def sync(sp):
                sp.dma_start(mask_in[:, :, :].rearrange("p t k -> p (t k)"),
                             io["mask_BxS2_bk0"].rearrange("b s -> (b s)").partition_broadcast(P)).then_inc(s.mask_in, 16)
                cx.sync(sp)

            def gpsimd(pool):
                same3 = same_batch.rearrange("p (h j) -> p h j", h=2)
                pool.memset(same_batch, 1.0).then_inc(s.same, 1)
                pool.wait_ge(s.same, 1)
                pool.affine_select(out=same3, in_=same3, compare_op=ALU.is_ge, fill=0.0, base=0,
                                   pattern=[[-SEQ, 2], [0, SEQ]], channel_multiplier=1).then_inc(s.same, 1)
                pool.wait_ge(s.same, 2)
                pool.affine_select(out=same3, in_=same3, compare_op=ALU.is_ge, fill=0.0, base=SEQ - 1,
                                   pattern=[[SEQ, 2], [0, SEQ]], channel_multiplier=-1).then_inc(s.same, 1)
                cx.gpsimd_first(pool)
                norm.gpsimd_stats(pool)
                with pool.Fori(0, BLOCKS) as i:
                    cx.gpsimd(pool, i)

            def scalar(act):
                with act.Fori(0, BLOCKS) as i:
                    cx.scalar(act, i)
                    norm.scalar(act, i)
                    act.wait_ge(s.soft, i * SOFT + SOFT)
                    for k in range(BT):
                        act.activation(prob[:, k, :], score[:, k, :], ACT.Exp, bias=neg_max[:, k:k + 1],
                                       accum_out=total[:, k:k + 1]).then_inc(s.exp, 1)
                    act.wait_ge(s.probT_ps, i + 1)
                    act.activation(flat(probT), bank[5][:, :], ACT.Copy).then_inc(s.probT, 1)

            def vector(dve):
                norm.vector_stats(dve)
                dve.wait_ge(s.mask_in, 16)
                dve.wait_ge(s.same, 3)
                with dve.Fori(0, BLOCKS) as i:
                    norm.vector_norm(dve, i)
                    dve.tensor_tensor(mask, mask_in[:, ds(i * BT, BT), :], same_batch.unsqueeze(1).to_broadcast([P, BT, P]),
                                      ALU.mult).then_inc(s.soft, 1)
                    dve.wait_ge(s.soft, i * SOFT + 1)
                    dve.tensor_scalar(flat(mask_low), flat(mask), 1e30, -1e30, ALU.mult, ALU.add).then_inc(s.soft, 1)
                    dve.tensor_reduce(seen, mask, AX.X, ALU.max).then_inc(s.mask, 1)
                    dve.wait_ge(s.score, i + 1)
                    dve.scalar_tensor_tensor(flat(score), bank[4][:, :], D ** -0.5, flat(mask), ALU.mult, ALU.mult).then_inc(s.soft, 1)
                    dve.wait_ge(s.soft, i * SOFT + 3)
                    dve.tensor_tensor(flat(score), flat(score), flat(mask_low), ALU.add).then_inc(s.soft, 1)
                    dve.wait_ge(s.soft, i * SOFT + 4)
                    dve.tensor_reduce(neg_max, score, AX.X, ALU.max, negate=True).then_inc(s.soft, 1)
                    dve.wait_ge(s.exp, i * BT + BT)
                    dve.reciprocal(inv, total).then_inc(s.mask, 1)
                    dve.wait_ge(s.mask, i * 3 + 2)
                    dve.scalar_tensor_tensor(scale, inv, gates[:, 0:1], seen, ALU.mult, ALU.mult).then_inc(s.mask, 1)
                    dve.wait_ge(s.mask, i * 3 + 3)
                    for k in range(BT):
                        if k % 2 == 0:
                            dve.wait_ge(s.out, i * 2 + k // 2 + 1)
                        dve.scalar_tensor_tensor(x_tile(i * BT + k), bank[6 + k // 2][:, k % 2 * D:k % 2 * D + D],
                                                 scale[:, k:k + 1], x_tile(i * BT + k), ALU.mult, ALU.add).then_inc(done, 1)

            def tensor(pe):
                cx.tensor_first(pe)
                with pe.Fori(0, BLOCKS) as i:
                    cx.tensor(pe, i)
                    norm.tensor(pe, i)
                    pe.wait_ge(cx.turned, (cx.first + i) * DC + DC)
                    pe.wait_ge(norm.hi, (norm.first_tp + i) * DC + DC)
                    for k in range(BT):
                        t = slice(k * P, (k + 1) * P)
                        for c in range(DC):
                            mm = pe.matmul(bank[4][:, t], xT[:, c, t], cT[:, c, t], start=c == 0, stop=c == DC - 1)
                    mm.then_inc(s.score, 1)
                    for k in range(BT):
                        pe.wait_ge(s.exp, i * BT + k + 1)
                        tp = pe.transpose(bank[5][:, k * P:(k + 1) * P], prob[:, k, :], ident[:, :])
                    tp.then_inc(s.probT_ps, 1)
                    pe.wait_ge(s.probT, i + 1)
                    for k in range(BT):
                        mm = pe.matmul(bank[6 + k // 2][:, k % 2 * D:k % 2 * D + D], probT[:, k, :], ctx_sb[:, k, :],
                                       start=True, stop=True)
                        if k % 2:
                            mm.then_inc(s.out, 1)
                    pe.wait_ge(s.out, i * 2 + 2)
                    pe.sem_inc(cx.free, 1)

            return sync, gpsimd, scalar, vector, tensor

        route_sems = sems("route", "loaded zeroed w_tp w logits_ps logitsT turned_ps kept chain soft exp")
        route_counts = [(0, 0)]

        def make_router(name, use, lay, scratch, experts, top, gate, w_rows, dram_w, dram_b=None, dram_bias=None):
            r = Names()
            r.loaded, r.zeroed, r.w_tp, r.w, r.logits_ps, r.logitsT, r.turned_ps, r.kept, r.chain, r.soft, r.exp = route_sems
            first_block = use * BLOCKS
            E = experts
            w_in = sb(f"{name}_win", [P, D] if w_rows else [P, DC, E])
            w_hi, w_lo = route_hi, route_lo
            logitsT = lay(BLK)
            r.logits, prob, key = lay(TILES, E), lay(TILES, E), lay(TILES, E)
            small, inv = lay(TILES), lay(TILES)
            pairs = TILES * E * E
            beats, ties = [scratch[:, j * pairs:(j + 1) * pairs].rearrange("p (t a b) -> p t a b", t=TILES, a=E) for j in range(2)]
            earlier = lay(E, E)
            rank = lay(TILES, E)
            r.shares = lay(E + 1, TILES)
            bias_in = sb(f"{name}_bias", [P, 2, E])
            extra = (dram_b is not None) + (dram_bias is not None)
            loaded0, chain0 = route_counts[-1]
            loads = loaded0 + 16 * ((1 if w_rows else DC) + extra)
            route_counts.append((loads, chain0 + 17 + extra))

            def sync(sp):
                if w_rows:
                    sp.dma_start(w_in[0:E, :], dram_w).then_inc(r.loaded, 16)
                else:
                    for c in range(DC):
                        sp.dma_start(w_in[:, c, :], dram_w[c * P:(c + 1) * P, :]).then_inc(r.loaded, 16)
                if dram_b is not None:
                    sp.dma_start(bias_in[:, 0, :], dram_b.partition_broadcast(P)).then_inc(r.loaded, 16)
                if dram_bias is not None:
                    sp.dma_start(bias_in[:, 1, :], dram_bias.partition_broadcast(P)).then_inc(r.loaded, 16)

            def gpsimd(pool):
                pool.memset(earlier, 1.0).then_inc(r.zeroed, 1)
                pool.wait_ge(r.zeroed, use * 2 + 1)
                pool.affine_select(out=earlier, in_=earlier, compare_op=ALU.is_gt, fill=0.0, base=0,
                                   pattern=[[1, E], [-1, E]], channel_multiplier=0).then_inc(r.zeroed, 1)

            def vector_weights(dve):
                dve.memset(w_hi[:, :, :].bitcast(F32), 0.0).then_inc(r.w, 1)
                dve.memset(w_lo[:, :, :].bitcast(F32), 0.0).then_inc(r.w, 1)
                dve.wait_ge(r.loaded, loads)
                dve.wait_ge(r.w, use * 4 + 2)
                if w_rows:
                    dve.wait_ge(r.w_tp, use + 1)
                    src = bank[4][:, 0:DC * E].rearrange("p (c e) -> p c e", c=DC)
                else:
                    src = w_in[:, :, :]
                dve.tensor_copy(w_hi[:, :, 0:E], src).then_inc(r.w, 1)
                dve.wait_ge(r.w, use * 4 + 3)
                dve.tensor_tensor(w_lo[:, :, 0:E], src, w_hi[:, :, 0:E].bitcast(F32), ALU.subtract).then_inc(r.w, 1)

            def tensor_weights(pe):
                if w_rows:
                    pe.wait_ge(r.loaded, loads)
                    for c in range(DC):
                        tp = pe.transpose(bank[4][:, c * E:(c + 1) * E], w_in[0:E, c * P:(c + 1) * P], ident[0:E, 0:E])
                    tp.then_inc(r.w_tp, 1)
                pe.wait_ge(r.w, use * 4 + 4)

            def tensor_logits(pe, norm, i):
                pe.wait_ge(norm.lo, (norm.first_lo + i) * DC + DC)
                n = 0
                for c in range(DC):
                    for w, x in ((w_hi, xhi), (w_hi, xlo), (w_lo, xhi)):
                        mm = pe.matmul(bank[4][:, :], w[:, c, :], flat(x[:, c:c + 1, ds(i * BLK, BLK)]), start=n == 0, stop=n == 5)
                        n += 1
                mm.then_inc(r.logits_ps, 1)

            def tensor_turn(pe, i):
                hold(pe, r.logitsT, first_block + i + 1)
                for k in range(BT):
                    tp = pe.transpose(bank[5][:, k * E:(k + 1) * E], logitsT[0:E, k * P:(k + 1) * P], ident[0:E, 0:E])
                tp.then_inc(r.turned_ps, 1)

            def scalar_logits(act, i):
                act.wait_ge(r.logits_ps, first_block + i + 1)
                act.activation(logitsT[0:E, :], bank[4][0:E, :], ACT.Copy).then_inc(r.logitsT, 1)

            def scalar_keep(act, i):
                act.wait_ge(r.turned_ps, first_block + i + 1)
                act.activation(r.logits[:, ds(i * BT, BT), :], bank[5][:, 0:BT * E].rearrange("p (k e) -> p k e", k=BT),
                               ACT.Copy).then_inc(r.kept, 1)
            r.all_kept = first_block + BLOCKS

            def scalar_last(act):
                act.wait_ge(r.soft, use + 1)
                act.activation(prob, r.logits, ACT.Exp).then_inc(r.exp, 1)

            def over(v):
                return v.unsqueeze(2).to_broadcast([P, TILES, E])

            def vector_last(dve):
                dve.wait_ge(r.kept, r.all_kept)
                dve.wait_ge(r.zeroed, use * 2 + 2)
                link = linker(dve, r.chain, chain0)
                if dram_b is not None:
                    link(dve.tensor_tensor(r.logits, r.logits, bias_in[:, 0:1, :].to_broadcast([P, TILES, E]), ALU.add))
                link(dve.tensor_reduce(small, r.logits, AX.X, ALU.max))
                dve.tensor_tensor(r.logits, r.logits, over(small), ALU.subtract).then_inc(r.soft, 1)
                dve.wait_ge(r.exp, use + 1)
                link(dve.tensor_reduce(small, prob, AX.X, ALU.add))
                link(dve.reciprocal(inv, small))
                link(dve.tensor_tensor(prob, prob, over(inv), ALU.mult))
                rated = prob
                if dram_bias is not None:
                    link(dve.tensor_tensor(key, prob, bias_in[:, 1:2, :].to_broadcast([P, TILES, E]), ALU.add))
                    rated = key
                other = rated.unsqueeze(2).to_broadcast([P, TILES, E, E])
                own = rated.unsqueeze(3).to_broadcast([P, TILES, E, E])
                link(dve.tensor_tensor(beats, other, own, ALU.is_gt))
                link(dve.tensor_tensor(ties, other, own, ALU.is_equal))
                link(dve.tensor_tensor(ties, ties, earlier.unsqueeze(1).to_broadcast([P, TILES, E, E]), ALU.mult))
                link(dve.tensor_tensor(beats, beats, ties, ALU.add))
                link(dve.tensor_reduce(rank, beats, AX.X, ALU.add))
                link(dve.tensor_scalar(rank, rank, float(top), None, ALU.is_lt))
                link(dve.tensor_tensor(prob, prob, rank, ALU.mult))
                link(dve.tensor_reduce(small, prob, AX.X, ALU.add))
                link(dve.reciprocal(inv, small))
                link(dve.tensor_tensor(prob, prob, over(inv), ALU.mult))
                link(dve.tensor_scalar(r.shares[:, 0:E, :].rearrange("p e t -> p t e"), prob, gate, None, ALU.mult))
                link(dve.memset(r.shares[:, E, :], 1.0))
                link(dve.tensor_scalar(r.shares[:, E, :], r.shares[:, E, :], gate, None, ALU.mult))

            r.sync, r.gpsimd, r.vector_weights, r.tensor_weights = sync, gpsimd, vector_weights, tensor_weights
            r.tensor_logits, r.tensor_turn, r.scalar_logits, r.scalar_keep = tensor_logits, tensor_turn, scalar_logits, scalar_keep
            r.scalar_last, r.vector_last = scalar_last, vector_last
            return r

        def make_entry(norm, router, quant=None):
            n = Names()
            through = (xn, ctx_sb)

            def vector(dve):
                norm.vector_stats(dve)
                for i in range(BLOCKS + 1):
                    if i < BLOCKS:
                        norm.vector_norm(dve, i, through[i % 2])
                        if quant:
                            quant.vector(dve, norm, i, through[i % 2])
                    if i:
                        norm.vector_rest(dve, i - 1, (i - 1) % 2 * DC)

            def gpsimd(pool):
                norm.gpsimd_stats(pool)

            def scalar(act):
                for i in range(BLOCKS + 2):
                    if i < BLOCKS:
                        norm.scalar(act, i, i % 2 * DC)
                        if quant:
                            quant.scalar(act, i)
                    if i >= 2:
                        router.scalar_keep(act, i - 2)
                    if 1 <= i <= BLOCKS:
                        router.scalar_logits(act, i - 1)

            def tensor(pe):
                for i in range(BLOCKS + 2):
                    if i < BLOCKS:
                        norm.tensor(pe, i, through[i % 2], i % 2 * DC)
                        if quant:
                            quant.tensor(pe, i)
                    if i >= 2:
                        router.tensor_turn(pe, i - 2)
                    if 1 <= i <= BLOCKS:
                        router.tensor_logits(pe, norm, i - 1)

            n.vector, n.gpsimd, n.scalar, n.tensor = vector, gpsimd, scalar, tensor
            return n

        gated_sems = sems("gated", "raw raw_free zeroed whi wlo w_free up1 up2 silu hid ahi alo down shares acc")
        gated_counts = [(0, 0, 0, 0, 0, 0)]

        def gated_experts(name, sublayer, split, turn, gate, before, done, experts, top, router_args, chunks, outputs, groups, load, up_width, down_chunks):
            lay = Layout()
            hidden = lay(4, BLK)
            silu, act32 = hidden[:, 0:2, :], hidden[:, 2:4, :]
            router = make_router(name, split, lay, flat(hidden), experts, top, gate, *router_args)
            norm = make_norm(sublayer, split=split, turn=turn)
            entry = make_entry(norm, router)
            per = 1 + max(e for pieces in outputs for e, _, _ in pieces)
            shares_now = lay(2 * per, TILES)
            s = Names()
            (
                s.raw, s.raw_free, s.zeroed, s.whi, s.wlo, s.w_free, s.up1, s.up2, s.silu, s.hid, s.ahi, s.alo,
                s.down, s.shares, s.acc
            ) = gated_sems
            NC = len(chunks)
            UNITS = BLOCKS * NC
            ACCS = BLOCKS * per
            NL = load.count
            width = up_width
            used = 2 * DC * width + down_chunks * D
            even = groups - 2 + groups % 2
            was = Names()
            was.raw, was.zeroed, was.groups, was.units, was.shares, was.accs = gated_counts[-1]
            gated_counts.append((was.raw + groups * 16 * NL, was.zeroed + 1, was.groups + groups, was.units + groups * UNITS,
                                 was.shares + even // 2 + (groups - even) * per, was.accs + groups * ACCS))

            def up_w(w, slot, mat, c, q):
                at = (mat * DC + c) * width + chunks[q][0]
                return w[:, slot, at:at + chunks[q][1]]

            def down_w(w, slot, q, p0, n):
                at = 2 * DC * width + q * D
                return w[p0:p0 + n, slot, at:at + D]

            raw_up = raw[:, 0:2 * DC * width].rearrange("p (m c w) -> p m c w", m=2, c=DC)
            raw_down = raw[:, 2 * DC * width:used].rearrange("p (q d) -> p q d", q=down_chunks)

            def sync(sp):
                router.sync(sp)
                sp.wait_ge(s.zeroed, was.zeroed + 1)
                with sp.Fori(0, even) as n:
                    sp.wait_ge(s.raw_free, was.groups + n + 1)
                    load(sp, n, raw_up, raw_down, s.raw)
                for n in range(even, groups):
                    sp.wait_ge(s.raw_free, was.groups + n + 1)
                    load(sp, n, raw_up, raw_down, s.raw)

            def gpsimd(pool):
                pool.wait_ge(*before)
                router.gpsimd(pool)
                entry.gpsimd(pool)
                if was.groups == 0:
                    pool.sem_inc(s.raw_free, 1)

                def split_low(n, slot):
                    hold(pool, s.whi, was.groups + n + 1)
                    pool.tensor_tensor(wlo[:, slot, 0:used], raw[:, 0:used], whi[:, slot, 0:used].bitcast(F32),
                                       ALU.subtract).then_inc(s.wlo, 1)
                    hold(pool, s.wlo, was.groups + n + 1)
                    pool.sem_inc(s.raw_free, 1)

                with pool.Fori(0, groups // 2) as i:
                    for slot in range(2):
                        split_low(2 * i + slot, slot)
                if groups % 2:
                    split_low(groups - 1, 0)

            def split_high(act, n, slot):
                act.wait_ge(s.raw, was.raw + (n + 1) * 16 * NL)
                act.wait_ge(s.w_free, was.groups + n + 1)
                act.activation(whi[:, slot, 0:used], raw[:, 0:used], ACT.Copy).then_inc(s.whi, 1)

            def scalar_group(act, n, slot, more):
                for u in range(UNITS):
                    U = was.units + n * UNITS + u
                    m = chunks[u % NC][1]
                    act.wait_ge(s.up1, U + 1)
                    act.activation(silu[0:m, u % 2, :], bank[u % 2][0:m, :], ACT.Silu).then_inc(s.silu, 1)
                    act.wait_ge(s.hid, U + 3)
                    act.wait_ge(s.down, U + 1)
                    act.activation(ahi[0:m, u % 2, :], act32[0:m, u % 2, :], ACT.Copy).then_inc(s.ahi, 1)
                    if u == NC and more:
                        split_high(act, n + 1, 1 - slot)

            def scalar(act):
                entry.scalar(act)
                split_high(act, 0, 0)
                router.scalar_last(act)
                with act.Fori(0, even // 2) as i:
                    for slot in range(2):
                        scalar_group(act, 2 * i + slot, slot, True)
                for n in range(even, groups):
                    scalar_group(act, n, n % 2, n + 1 < groups)

            def vector_group(dve, n, slot):
                for u in range(UNITS):
                    U = was.units + n * UNITS + u
                    b, q = divmod(u, NC)
                    m = chunks[q][1]
                    dve.wait_ge(s.silu, U + 1)
                    dve.wait_ge(s.up2, U + 1)
                    dve.tensor_tensor(act32[0:m, u % 2, :], silu[0:m, u % 2, :], bank[2 + u % 2][0:m, :], ALU.mult).then_inc(s.hid, 1)
                    dve.wait_ge(s.ahi, U + 1)
                    dve.tensor_tensor(alo[0:m, u % 2, :], act32[0:m, u % 2, :], ahi[0:m, u % 2, :].bitcast(F32),
                                      ALU.subtract).then_inc(s.alo, 1)
                    if u:
                        add_outputs(dve, n, slot, u - 1)
                add_outputs(dve, n, slot, UNITS - 1)

            last_chunk = {e: max(q for q in range(NC) for x, _, _ in outputs[q] if x == e) for e in range(per)}

            def add_outputs(dve, n, slot, u):
                b, q = divmod(u, NC)
                for e in range(per):
                    if last_chunk[e] == q:
                        add_output(dve, n, slot, b, e, was.units + n * UNITS + u)

            def add_output(dve, n, slot, b, e, U):
                Y = was.accs + (n * BLOCKS + b) * per + e
                y_slot = (b * per + e) % 2
                dve.wait_ge(s.acc, Y + 2)
                dve.wait_ge(s.down, U + 3)
                for k in range(BT):
                    t = b * BT + k
                    ins = dve.scalar_tensor_tensor(X[:, t, :], bank[4 + 2 * y_slot + k // 2][:, k % 2 * D:k % 2 * D + D],
                                                   shares_now[:, slot * per + e, t:t + 1], X[:, t, :], ALU.mult, ALU.add)
                ins.then_inc(s.acc, 1)

            def vector(dve):
                dve.wait_ge(*before)
                dve.memset(raw[:, 0:used], 0.0).then_inc(s.zeroed, 1)
                router.vector_weights(dve)
                entry.vector(dve)
                router.vector_last(dve)
                if was.groups == 0:
                    dve.sem_inc(s.hid, 2)
                    dve.sem_inc(s.acc, 2)
                with dve.Fori(0, even // 2) as i:
                    dve.wait_ge(s.acc, was.accs + i * 2 * ACCS + 2)
                    dve.tensor_copy(shares_now, router.shares[:, ds(i * 2 * per, 2 * per), :]).then_inc(s.shares, 1)
                    hold(dve, s.shares, was.shares + i + 1)
                    for slot in range(2):
                        vector_group(dve, 2 * i + slot, slot)
                for j, n in enumerate(range(even, groups)):
                    dve.wait_ge(s.acc, was.accs + n * ACCS + 2)
                    for e in range(per):
                        dve.tensor_copy(shares_now[:, n % 2 * per + e, :], router.shares[:, min(n * per + e, experts), :]).then_inc(s.shares, 1)
                    dve.wait_ge(s.shares, was.shares + even // 2 + (j + 1) * per)
                    vector_group(dve, n, n % 2)
                dve.wait_ge(s.acc, was.accs + groups * ACCS + 2)
                dve.sem_inc(done, TILES)

            def tensor_group(pe, n, slot):
                hold(pe, s.wlo, was.groups + n + 1)

                def up(u):
                    U = was.units + n * UNITS + u
                    b, q = divmod(u, NC)
                    cols = slice(b * BLK, (b + 1) * BLK)
                    m = chunks[q][1]
                    hold(pe, s.hid, U + 1)
                    for mat, signal in ((0, s.up1), (1, s.up2)):
                        j = 0
                        for c in range(DC):
                            for w, x in ((whi, xhi), (whi, xlo), (wlo, xhi)):
                                mm = pe.matmul(bank[2 * mat + u % 2][0:m, :], up_w(w, slot, mat, c, q), x[:, c, cols],
                                               start=j == 0, stop=j == 3 * DC - 1)
                                j += 1
                        mm.then_inc(signal, 1)

                opened = set()

                def down(u):
                    U = was.units + n * UNITS + u
                    b, q = divmod(u, NC)
                    hold(pe, s.alo, U + 1)
                    for e, p0, np_ in outputs[q]:
                        Y = was.accs + (n * BLOCKS + b) * per + e
                        y_slot = (b * per + e) % 2
                        first = (b, e) not in opened
                        if first:
                            opened.add((b, e))
                            hold(pe, s.acc, Y + 1)
                        for k in range(BT):
                            j = 0
                            for a, w in ((ahi, whi), (ahi, wlo), (alo, whi)):
                                mm = pe.matmul(bank[4 + 2 * y_slot + k // 2][:, k % 2 * D:k % 2 * D + D],
                                               a[p0:p0 + np_, u % 2, k * P:(k + 1) * P], down_w(w, slot, q, p0, np_),
                                               start=first and k % 2 == 0 and j == 0, stop=last_chunk[e] == q and j == 2,
                                               skip_group_check=True)
                                j += 1
                    mm.then_inc(s.down, 1)

                for u in range(UNITS + 1):
                    if u < UNITS:
                        up(u)
                    if u:
                        down(u - 1)

            def tensor(pe):
                pe.wait_ge(*before)
                if was.groups == 0:
                    pe.sem_inc(s.w_free, 2)
                    pe.sem_inc(s.down, 2)
                router.tensor_weights(pe)
                entry.tensor(pe)
                pe.wait_ge(router.kept, router.all_kept)
                pe.wait_ge(s.shares, was.shares + 1)
                def group(n, slot):
                    tensor_group(pe, n, slot)
                    pe.wait_ge(s.down, was.units + (n + 1) * UNITS + 2)
                    pe.sem_inc(s.w_free, 1)

                with pe.Fori(0, even // 2) as i:
                    for slot in range(2):
                        group(2 * i + slot, slot)
                for n in range(even, groups):
                    group(n, n % 2)

            return sync, gpsimd, scalar, vector, tensor

        def layer0_experts(before, done):
            EXPERTS, HALF = 8, P // 2
            rest = L0_I - P

            def load(sp, n, raw_up, raw_down, signal):
                for mat, (routed, shared) in enumerate((("L0_ffn_w1", "L0_ffn_sw1"), ("L0_ffn_w3", "L0_ffn_sw3"))):
                    for c in range(DC):
                        for e in range(2):
                            if isinstance(n, int) and n == EXPERTS // 2:
                                src = io[shared][c * P:(c + 1) * P, e * L0_I:(e + 1) * L0_I]
                            else:
                                src = io[routed][ds(2 * n + e, 1), c * P:(c + 1) * P, :].rearrange("o p i -> p (o i)")
                            at = e * (P + HALF)
                            sp.dma_start(raw_up[:, mat, c, at:at + L0_I], src).then_inc(signal, 16)
                for e in range(2):
                    def rows(a, b):
                        if isinstance(n, int) and n == EXPERTS // 2:
                            return io["L0_ffn_sw2"][e * L0_I + a:e * L0_I + b, :]
                        return io["L0_ffn_w2"][ds(2 * n + e, 1), a:b, :].rearrange("o i d -> (o i) d")
                    if e == 0:
                        sp.dma_start(raw_down[:, 0, :], rows(0, P)).then_inc(signal, 16)
                        sp.dma_start(raw_down[0:rest, 1, :], rows(P, L0_I)).then_inc(signal, 16)
                    else:
                        sp.dma_start(raw_down[HALF:P, 1, :], rows(0, HALF)).then_inc(signal, 16)
                        sp.dma_start(raw_down[0:L0_I - HALF, 2, :], rows(HALF, L0_I)).then_inc(signal, 16)
            load.count = 12

            return gated_experts("f0", 1, 0, 1, gates[:, 4:5], before, done, EXPERTS, 2, (True, io["L0_ffn_gate_w"]),
                                 chunks=[(0, P), (P, P), (2 * P, L0_I - HALF)],
                                 outputs=[[(0, 0, P)], [(0, 0, rest), (1, HALF, HALF)], [(1, 0, L0_I - HALF)]],
                                 groups=EXPERTS // 2 + 1, load=load, up_width=3 * P, down_chunks=3)

        def layer1_attention(before, done):
            HEADS = 16
            HD = D // HEADS
            HC = P // HD
            AUG = P + HC
            EPS = 1e-6
            RING = 4
            lay = Layout()
            wq, wg, wo, wkv = lay(DC, D), lay(DC, D), lay(DC, D), lay(DC, 2 * D)
            inT = lay(2, 2 * DC, P)
            neg, grown, keyq = lay(2, 2 * D), lay(2, 2 * D), lay(2, 2 * D)
            values = lay(2, DC, AUG)
            summary = lay(2, 2, DC, AUG)
            gate, scaled = lay(2, D), lay(2, D)
            den, per_den = lay(2, HEADS), lay(2, HEADS)
            attended, attendedT = lay(2, D), lay(2, D)
            lay.at = L1_RAW
            raw_w = lay(10, D)
            bias_row = lay(D)[0:1]
            head_mask = sb("a1_head_mask", [P, AUG])
            norm = make_norm(2)
            s = Names()
            (
                s.mask, s.ones, s.in_ps, s.inT, s.keyq_ps, s.val_ps, s.neg, s.grown, s.keyq, s.values,
                s.gate, s.sum_ps, s.sum, s.num, s.den, s.att, s.attT_ps, s.attT, s.out
            ) = sems("a1", "mask ones in_ps inT keyq_ps val_ps neg grown keyq values gate sum_ps sum num den att "
                     "attT_ps attT out")
            was = count_weights(loaded=16 * 5, turned=4, ready=DC * 4)
            weights = (("L1_xattn_Wq", wq, 0, 2), ("L1_xattn_Wg", wg, 2, 2), ("L1_xattn_Wo", wo, 4, 2),
                       ("L1_xattn_Wkv", wkv, 6, 4))
            IN, KEYQ, VAL, SUM, NUM, OUT = bank[0], bank[1], bank[2], (bank[3], bank[4]), bank[5], bank[6]

            def inside(t):
                return not isinstance(t, int) or 0 <= t < TILES

            def over_tiles(eng, step):
                for t in range(2):
                    step(t, t)
                with eng.Fori(0, TILES // RING - 1) as i:
                    for k in range(RING):
                        step(i * RING + 2 + k, (2 + k) % RING)
                for t in range(TILES - 2, TILES + 2):
                    step(t, t % RING)

            def sync(sp):
                for name, _, a, n in weights:
                    sp.dma_start(raw_w[:, a:a + n, :], io[name].rearrange("(a p) k -> p a k", p=P)).then_inc(weight.loaded, 16)
                sp.dma_start(bias_row, io["L1_xattn_bg"].partition_broadcast(1)).then_inc(weight.loaded, 16)
                sp.wait_ge(*before)
                tiles = io["ctx_2048"].rearrange("b s d -> (b s) d").rearrange("(t p) d -> t p d", p=P)
                for k in range(RING):
                    sp.dma_start(ctx_in[:, k, :], tiles[k]).then_inc(ctx_here[k], 16)
                with sp.Fori(1, TILES // RING) as i:
                    for k in range(RING):
                        t = i * RING + k
                        sp.wait_ge(s.in_ps, t - RING + 1)
                        sp.dma_start(ctx_in[:, k, :], tiles[ds(t, 1)].rearrange("o p d -> p (o d)")).then_inc(ctx_here[k], 16)

            def gpsimd(pool):
                v = head_mask[:, 0:P].rearrange("p (h j) -> p h j", h=HC)
                pool.memset(head_mask[:, :], 1.0).then_inc(s.mask, 1)
                pool.wait_ge(s.mask, 1)
                for half, (base, sign) in enumerate(((0, 1), (HD - 1, -1))):
                    if half:
                        pool.wait_ge(s.mask, 3)
                    pool.affine_select(out=v, in_=v, compare_op=ALU.is_ge, fill=0.0, base=base,
                                       pattern=[[-sign * HD, HC], [0, HD]], channel_multiplier=sign).then_inc(s.mask, 1)
                    pool.affine_select(out=head_mask[:, P:AUG], in_=head_mask[:, P:AUG], compare_op=ALU.is_ge, fill=0.0, base=base,
                                       pattern=[[-sign * HD, HC]], channel_multiplier=sign).then_inc(s.mask, 1)
                norm.gpsimd_stats(pool)

            def scalar_in(act, t, k):
                act.wait_ge(s.in_ps, t + 1)
                act.activation(flat(inT[:, k % 2]), IN[:, :], ACT.Copy).then_inc(s.inT, 1)

            def scalar(act):
                for j, (_, w, _, n) in enumerate(weights):
                    act.wait_ge(weight.turned, was.turned + j + 1)
                    for c in range(DC):
                        at = c * n * P
                        act.activation(w[:, c, :], bank[j + at // 512][:, at % 512:at % 512 + n * P], ACT.Copy).then_inc(weight.ready, 1)
                scalar_in(act, 0, 0)

                def step(t, k):
                    j = k % 2
                    if inside(t - 2):
                        act.wait_ge(s.attT_ps, t - 1)
                        act.activation(attendedT[:, j, :], OUT[:, 0:D], ACT.Copy).then_inc(s.attT, 1)
                    if inside(t + 1):
                        scalar_in(act, t + 1, k + 1)
                    if inside(t):
                        act.wait_ge(s.keyq_ps, t + 1)
                        act.activation(neg[:, j, :], KEYQ[:, :], ACT.Relu, scale=-1.0).then_inc(s.neg, 1)
                        act.wait_ge(s.neg, t + 1)
                        act.activation(grown[:, j, :], neg[:, j, :], ACT.Exp, scale=-1.0).then_inc(s.grown, 1)
                        act.wait_ge(s.val_ps, t + 1)
                        act.activation(values[:, j, :, 0:P], VAL[:, 0:D].rearrange("p (c e) -> p c e", c=DC), ACT.Copy).then_inc(s.values, 1)
                        act.activation(gate[:, j, :], VAL[:, D:2 * D], ACT.Tanh, scale=0.5).then_inc(s.gate, 1)
                over_tiles(act, step)

            def vector_norm(dve, t, k):
                dve.tensor_scalar(xn[:, k, :], x_tile(t), flat(ln_mv[:, ds(t, 1), 0:1]), ln_rstd[:, ds(t, 1)],
                                  ALU.subtract, ALU.mult).then_inc(norm.xn, 1)

            def vector(dve):
                dve.wait_ge(*before)
                norm.vector_stats(dve)
                dve.memset(values[:, :, :, P:AUG].rearrange("p j c h -> p (j c) h"), 1.0).then_inc(s.ones, 1)
                dve.wait_ge(s.mask, 5)
                dve.wait_ge(norm.rstd, norm.rstd_there)
                for t in range(2):
                    vector_norm(dve, t, t)

                def step(t, k):
                    j = k % 2
                    if inside(t + 2):
                        if not isinstance(t, int) or t >= 2:
                            dve.wait_ge(s.in_ps, t - 1)
                        vector_norm(dve, t + 2, (k + 2) % RING)
                    if inside(t - 1):
                        dve.wait_ge(s.sum_ps, t)
                        for b in range(2):
                            dve.tensor_tensor(summary[:, 1 - j, b], SUM[b][:, 0:DC * AUG].rearrange("p (c a) -> p c a", c=DC),
                                              head_mask[:, :].unsqueeze(1).to_broadcast([P, DC, AUG]), ALU.mult).then_inc(s.sum, 1)
                    if inside(t - 2):
                        dve.wait_ge(s.out, t - 1)
                        dve.scalar_tensor_tensor(x_tile(t - 2), OUT[:, D:2 * D], gates[:, 1:2], x_tile(t - 2), ALU.mult, ALU.add).then_inc(done, 1)
                    if inside(t - 1):
                        dve.wait_ge(s.num, t)
                        got = NUM[:, 0:DC * AUG].rearrange("p (c a) -> p c a", c=DC)
                        dve.tensor_scalar(den[:, 1 - j, :].rearrange("p (c h) -> p c h", c=DC), got[:, :, P:AUG], EPS, 2.0, ALU.add, ALU.mult).then_inc(s.den, 1)
                        dve.wait_ge(s.gate, t)
                        dve.scalar_tensor_tensor(scaled[:, 1 - j, :].rearrange("p (c e) -> p c e", c=DC), gate[:, 1 - j, :].rearrange("p (c e) -> p c e", c=DC),
                                                 1.0, got[:, :, 0:P], ALU.add, ALU.mult).then_inc(s.den, 1)
                        hold(dve, s.den, t * 3 - 1)
                        dve.reciprocal(per_den[:, 1 - j, :], den[:, 1 - j, :]).then_inc(s.den, 1)
                        dve.wait_ge(s.den, t * 3)
                        dve.tensor_tensor(attended[:, 1 - j, :].rearrange("p (h e) -> p h e", h=HEADS), scaled[:, 1 - j, :].rearrange("p (h e) -> p h e", h=HEADS),
                                          per_den[:, 1 - j, :].unsqueeze(2).to_broadcast([P, HEADS, HD]), ALU.mult).then_inc(s.att, 1)
                    if inside(t):
                        dve.wait_ge(s.grown, t + 1)
                        dve.scalar_tensor_tensor(keyq[:, j, :], KEYQ[:, :], 0.0, grown[:, j, :], ALU.max, ALU.add).then_inc(s.keyq, 1)
                over_tiles(dve, step)

            def tensor_in(pe, t, k):
                hold(pe, ctx_here[k], t // RING * 16 + 16 if isinstance(t, int) else (t - k) * (16 // RING) + 16)
                hold(pe, norm.xn, norm.first * BT + t + 1)
                for c in range(DC):
                    pe.transpose(IN[:, c * P:(c + 1) * P], xn[:, k, c * P:(c + 1) * P], ident[:, :])
                for c in range(DC):
                    tp = pe.transpose(IN[:, D + c * P:D + (c + 1) * P], ctx_in[:, k, c * P:(c + 1) * P], ident[:, :])
                tp.then_inc(s.in_ps, 1)

            def tensor(pe):
                pe.wait_ge(*before)
                pe.wait_ge(weight.loaded, was.loaded + 16 * 5)
                for j, (_, _, a0, n) in enumerate(weights):
                    for c in range(DC):
                        for a in range(n):
                            at = (c * n + a) * P
                            tp = pe.transpose(bank[j + at // 512][:, at % 512:at % 512 + P], raw_w[:, a0 + a, c * P:(c + 1) * P], ident[:, :])
                    tp.then_inc(weight.turned, 1)
                pe.wait_ge(weight.ready, was.ready + DC * len(weights))
                pe.wait_ge(s.ones, 1)
                tensor_in(pe, 0, 0)

                def step(t, k):
                    j = k % 2
                    if inside(t - 1):
                        hold(pe, s.keyq, t)
                        hold(pe, s.values, t)
                        hold(pe, s.gate, t)
                        for b in range(2):
                            rows = slice(b * SEQ, (b + 1) * SEQ)
                            for c in range(DC):
                                mm = pe.matmul(SUM[b][:, c * AUG:(c + 1) * AUG], keyq[rows, 1 - j, c * P:(c + 1) * P], values[rows, 1 - j, c, :],
                                               start=True, stop=True)
                        mm.then_inc(s.sum_ps, 1)
                    if inside(t - 2):
                        hold(pe, s.attT, t - 1)
                        for c in range(DC):
                            mm = pe.matmul(OUT[:, D:2 * D], attendedT[:, j, c * P:(c + 1) * P], wo[:, c, :], start=c == 0, stop=c == DC - 1)
                        mm.then_inc(s.out, 1)
                    if inside(t):
                        hold(pe, s.inT, t + 1)
                    if inside(t + 1):
                        tensor_in(pe, t + 1, (k + 1) % RING)
                    if inside(t):
                        for c in range(DC):
                            pe.matmul(KEYQ[:, 0:D], inT[:, j, DC + c, :], wkv[:, c, 0:D], start=c == 0, stop=c == DC - 1)
                        for m in range(DC):
                            for c in range(DC):
                                mm = pe.matmul(KEYQ[:, D + m * P:D + (m + 1) * P], wq[:, c, m * P:(m + 1) * P], inT[:, j, c, :],
                                               start=c == 0, stop=c == DC - 1)
                        mm.then_inc(s.keyq_ps, 1)
                    if inside(t - 1):
                        hold(pe, s.sum, t * 2)
                        for b in range(2):
                            rows = slice(b * SEQ, (b + 1) * SEQ)
                            for c in range(DC):
                                at = D + c * P + b * SEQ
                                mm = pe.matmul(NUM[rows, c * AUG:(c + 1) * AUG], keyq[:, 1 - j, at:at + SEQ], summary[:, 1 - j, b, c, :],
                                               start=True, stop=True)
                        mm.then_inc(s.num, 1)
                    if inside(t):
                        for c in range(DC):
                            pe.matmul(VAL[:, 0:D], inT[:, j, DC + c, :], wkv[:, c, D:2 * D], start=c == 0, stop=c == DC - 1)
                        for c in range(DC):
                            pe.matmul(VAL[:, D:2 * D], inT[:, j, c, :], wg[:, c, :], start=c == 0, stop=False)
                        pe.matmul(VAL[:, D:2 * D], ones[0:1, :], bias_row, start=False, stop=True).then_inc(s.val_ps, 1)
                    if inside(t - 1):
                        hold(pe, s.att, t)
                        if not isinstance(t, int) or t >= 2:
                            hold(pe, done, before[1] + t - 1)
                        for c in range(DC):
                            tp = pe.transpose(OUT[:, c * P:(c + 1) * P], attended[:, 1 - j, c * P:(c + 1) * P], ident[:, :])
                        tp.then_inc(s.attT_ps, 1)
                over_tiles(pe, step)

            return sync, gpsimd, scalar, vector, tensor

        quant_sems = sems("quant", "chain scale shifted tp turned")

        def make_quant(use, lay, scratch, dst):
            n = Names()
            n.chain, n.scale, n.shifted, n.tp, n.turned = quant_sems
            n.first = use * BLOCKS
            peak, rate = lay(BT), lay(TILES)
            n.step = lay(TILES)
            shifted = scratch.rearrange("p (j k d) -> p j k d", j=2, k=BT)

            def vector(dve, norm, i, tiles):
                g = n.first + i
                block = slice(i * BT, (i + 1) * BT)
                dve.wait_ge(norm.xn, (norm.first + i) * BT + BT)
                dve.tensor_reduce(peak, tiles[:, :, :], AX.X, ALU.max, apply_absolute_value=True).then_inc(n.chain, 1)
                dve.wait_ge(n.chain, g * 2 + 1)
                dve.tensor_scalar(n.step[:, block], peak, QUANT_EPS, 1.0 / 127, ALU.max, ALU.mult).then_inc(n.chain, 1)
                dve.wait_ge(n.chain, g * 2 + 2)
                dve.reciprocal(rate[:, block], n.step[:, block]).then_inc(n.scale, 1)
                dve.wait_ge(n.scale, g + 1)
                if i >= 2:
                    dve.wait_ge(n.tp, g - 1)
                for k in range(BT):
                    dve.tensor_scalar(shifted[:, i % 2, k, :], tiles[:, k, :], rate[:, i * BT + k:i * BT + k + 1], MAGIC,
                                      ALU.mult, ALU.add).then_inc(n.shifted, 1)

            def tensor(pe, i):
                pe.wait_ge(n.shifted, (n.first + i) * BT + BT)
                if i:
                    pe.wait_ge(n.turned, (n.first + i) * DC)
                for c in range(DC):
                    for k in range(BT):
                        tp = pe.transpose(bank[6 + c][:, k * P:(k + 1) * P], shifted[:, i % 2, k, c * P:(c + 1) * P], ident[:, :])
                tp.then_inc(n.tp, 1)

            def scalar(act, i):
                act.wait_ge(n.tp, n.first + i + 1)
                for c in range(DC):
                    act.activation(dst[:, c, i * BLK:(i + 1) * BLK], bank[6 + c][:, :], ACT.Copy, bias=-MAGIC).then_inc(n.turned, 1)

            n.vector, n.scalar, n.tensor = vector, scalar, tensor
            return n

        whole_sems = sems("whole", "raw size total chain ternary tern shifted w_tp w up relu once prod peak pair rate turned "
                            "wholeT down acc")
        whole_used = Names()
        weights_free = sem("weights_free")

        def layer1_experts(before, done):
            E, I = 8, 512
            IC = I // P
            AHEAD, PEAK_AHEAD, SHIFT_AHEAD = 6, 4, 1
            RING = 8
            RELUS = 4
            TURN_AT = (5, 7, 9)
            MAT = I * D // P
            GATE, UP, DOWN = 0, 1, 2
            lay = Layout()
            prod = lay(RING, I)
            router = make_router("f1", 1, lay, flat(prod), E, 2, gates[:, 5:6], True, io["L1_ffn_router_w"])
            norm = make_norm(3, split=1, turn=2)
            xqT = lay(DC, TOK, dt=BF16)
            quant = make_quant(0, lay, flat(prod[:, RING // 2:, :]), xqT)
            entry = make_entry(norm, router, quant)
            step3 = lay(TILES)
            relu, once = lay(RELUS, I), lay(2, I)
            shifted, wholeT = lay(2, I), lay(2, I, dt=BF16)
            up_w = lay(2, 2, DC, I, dt=BF16)
            down_w = lay(2, IC, D, dt=BF16)
            tern = lay(3, MAT, dt=BF16)
            size_sum, mean, per_mean = lay(3), lay(3), lay(3)
            factor, inv = lay(TILES), lay(TILES)
            least, out_factor = lay(2, TILES), lay(2, TILES)
            peak, unit, rate, out_scale = lay(TILES), lay(TILES), lay(TILES), lay(TILES)
            s = Names()
            (
                s.raw, s.size, s.total, s.chain, s.ternary, s.tern, s.shifted, s.w_tp, s.w, s.up, s.relu, s.once,
                s.prod, s.peak, s.pair, s.rate, s.turned, s.wholeT, s.down, s.acc
            ) = whole_sems
            raw_m = raw[:, 0:3 * MAT].rearrange("p (m k) -> p m k", m=3)
            turn = bank[4][:, :]
            w_turn = bank[5][:, :].bitcast(BF16)
            CHAIN = 7
            units = E * TILES
            after = whole_used
            after.tern_signal = s.tern
            after.raw, after.size, after.total, after.chain, after.tern = E * 48, E * 3, E, 2 + E * CHAIN, E * 3 + 3
            after.w_tp, after.w = E * 3, E * 3 + 1
            after.up = after.relu = after.peak = after.pair = after.wholeT = after.down = units
            after.rate, after.shifted, after.turned, after.acc = units // 2, units + RING, units + 2, units + 2
            even = E - 2

            def sync(sp):
                sp.wait_ge(*before)
                router.sync(sp)
                with sp.Fori(0, E) as n:
                    sp.wait_ge(s.tern, n * 3 + 3)
                    for m, w in ((GATE, "L1_ffn_gate_w"), (UP, "L1_ffn_up_w"), (DOWN, "L1_ffn_down_w")):
                        width = I if m == DOWN else D
                        src = io[w][ds(n, 1)].rearrange("o (a p) k -> p (o a) k", p=P)
                        sp.dma_start(raw_m[:, m, :].rearrange("p (a k) -> p a k", k=width), src).then_inc(s.raw, 16)

            def scalar_size(act, n, m):
                act.wait_ge(s.raw, n * 48 + 48)
                act.activation(tern[:, m, :], raw_m[:, m, :], ACT.Abs, accum_out=size_sum[:, m:m + 1]).then_inc(s.size, 1)

            def tensor_total(pe, n):
                hold(pe, s.size, n * 3 + 3)
                pe.matmul(bank[5][:, 0:3], ones[:, :], size_sum, start=True, stop=True).then_inc(s.total, 1)

            def vector_scales(dve, n, slot):
                dve.wait_ge(s.total, n + 1)
                link = linker(dve, s.chain, n * CHAIN + 2)
                link(dve.tensor_scalar(mean, bank[5][:, 0:3], 1.0 / (I * D), QUANT_EPS, ALU.mult, ALU.max))
                link(dve.reciprocal(per_mean, mean))
                link(dve.tensor_scalar(factor, step3, mean[:, GATE:GATE + 1], mean[:, GATE:GATE + 1], ALU.mult, ALU.mult))
                link(dve.tensor_scalar(factor, factor, mean[:, UP:UP + 1], None, ALU.mult))
                link(dve.reciprocal(inv, factor))
                link(dve.tensor_scalar(least[:, slot, :], inv, QUANT_EPS / 127, None, ALU.mult))
                link(dve.scalar_tensor_tensor(out_factor[:, slot, :], factor, mean[:, DOWN:DOWN + 1],
                                              flat(router.shares[:, ds(n, 1), :]) if not isinstance(n, int) else router.shares[:, n, :],
                                              ALU.mult, ALU.mult))

            def vector_ternary(dve, n, m, part):
                w = raw_m[:, m, :]
                if part == 0:
                    dve.tensor_scalar(w, w, per_mean[:, m:m + 1], MAGIC, ALU.mult, ALU.add).then_inc(s.ternary, 1)
                elif part == 1:
                    dve.wait_ge(s.ternary, (n * 3 + m) * 2 + 1)
                    dve.tensor_scalar(tern[:, m, :], w, MAGIC, -1.0, ALU.subtract, ALU.max).then_inc(s.ternary, 1)
                else:
                    dve.wait_ge(s.ternary, (n * 3 + m) * 2 + 2)
                    dve.tensor_scalar(tern[:, m, :], tern[:, m, :], 1.0, None, ALU.min).then_inc(s.tern, 1)

            def tensor_turn(pe, n, m):
                hold(pe, s.tern, n * 3 + m + 4)
                hold(pe, s.w, n * 3 + m + 1)
                rows, cols = (DC, IC) if m == DOWN else (IC, DC)
                for c in range(cols):
                    for a in range(rows):
                        at = (c * rows + a) * P
                        tp = pe.transpose(w_turn[:, at:at + P], tern[:, m, (a * cols + c) * P:(a * cols + c + 1) * P], identb[:, :])
                tp.then_inc(s.w_tp, 1)

            def scalar_weights(act, n, slot, m):
                act.wait_ge(s.w_tp, n * 3 + m + 1)
                to = down_w[:, slot, :, :] if m == DOWN else up_w[:, slot, m, :, :]
                act.activation(flat(to), w_turn, ACT.Copy).then_inc(s.w, 1)

            def scalar_relu(act, n, t):
                act.wait_ge(s.up, n * TILES + t + 1)
                act.wait_ge(s.prod, n * TILES + t + 1)
                act.activation(relu[:, t % RELUS, :], bank[t % 2][:, :], ACT.Relu).then_inc(s.relu, 1)

            def scalar_shift(act, n, t):
                U = n * TILES + t
                act.wait_ge(s.rate, n * (TILES // 2) + t // 2 + 1)
                act.wait_ge(s.turned, U + 1)
                act.activation(shifted[:, t % 2, :], prod[:, t % RING, :], ACT.Copy, scale=rate[:, t:t + 1],
                               bias=MAGIC).then_inc(s.shifted, 1)

            def scalar_back(act, n, t):
                act.wait_ge(s.turned, n * TILES + t + 3)
                act.activation(wholeT[:, t % 2, :], turn, ACT.Copy, bias=-MAGIC).then_inc(s.wholeT, 1)

            def vector_once(dve, n, t):
                U = n * TILES + t
                dve.wait_ge(s.relu, U + 1)
                dve.wait_ge(s.prod, U + RELUS - 1)
                dve.tensor_tensor(once[:, t % 2, :], relu[:, t % RELUS, :], bank[2 + t % 2][:, :], ALU.mult).then_inc(s.once, 1)

            def gpsimd_prod(pool, n, t):
                U = n * TILES + t
                pool.wait_ge(s.once, U + 3)
                hold(pool, s.shifted, U + 1)
                pool.tensor_tensor(prod[:, t % RING, :], once[:, t % 2, :], relu[:, t % RELUS, :], ALU.mult).then_inc(s.prod, 1)

            def vector_peak(dve, n, t, slot):
                U = n * TILES + t
                dve.wait_ge(s.prod, U + RELUS + 1)
                dve.tensor_reduce(peak[:, t:t + 1], prod[:, t % RING, :], AX.X, ALU.max, apply_absolute_value=True).then_inc(s.peak, 1)
                if t % 2:
                    two = slice(t - 1, t + 1)
                    Q = n * (TILES // 2) + t // 2
                    dve.wait_ge(s.peak, U + 1)
                    dve.scalar_tensor_tensor(unit[:, two], peak[:, two], 1.0 / 127, least[:, slot, two], ALU.mult, ALU.max).then_inc(s.pair, 1)
                    hold(dve, s.pair, Q * 2 + 1)
                    dve.reciprocal(rate[:, two], unit[:, two]).then_inc(s.rate, 1)
                    dve.tensor_tensor(out_scale[:, two], unit[:, two], out_factor[:, slot, two], ALU.mult).then_inc(s.pair, 1)

            def vector_back(dve, n, t):
                U = n * TILES + t
                dve.wait_ge(s.down, U + 1)
                dve.wait_ge(s.pair, (n * (TILES // 2) + t // 2) * 2 + 2)
                dve.scalar_tensor_tensor(X[:, t, :], bank[6 + t % 2][:, 0:D], out_scale[:, t:t + 1], X[:, t, :],
                                         ALU.mult, ALU.add).then_inc(s.acc, 1)

            def tensor_up(pe, n, t, slot):
                hold(pe, s.once, n * TILES + t + 1)
                for m in (GATE, UP):
                    for c in range(DC):
                        mm = pe.matmul(bank[2 * m + t % 2][:, :], xqT[:, c, t * P:(t + 1) * P], up_w[:, slot, m, c, :],
                                       start=c == 0, stop=c == DC - 1)
                mm.then_inc(s.up, 1)

            def tensor_turn_tile(pe, n, t):
                hold(pe, s.shifted, n * TILES + t + RING + 1)
                for c in range(IC):
                    tp = pe.transpose(turn[:, c * P:(c + 1) * P], shifted[:, t % 2, c * P:(c + 1) * P], ident[:, :])
                tp.then_inc(s.turned, 1)

            def tensor_down(pe, n, t, slot):
                hold(pe, s.wholeT, n * TILES + t + 1)
                hold(pe, s.acc, n * TILES + t + 1)
                for c in range(IC):
                    mm = pe.matmul(bank[6 + t % 2][:, 0:D], wholeT[:, t % 2, c * P:(c + 1) * P], down_w[:, slot, c, :],
                                   start=c == 0, stop=c == IC - 1)
                mm.then_inc(s.down, 1)

            def over_experts(eng, step):
                with eng.Fori(0, even // 2) as i:
                    for slot in range(2):
                        step(2 * i + slot, slot, True)
                for n in range(even, E):
                    step(n, n % 2, n + 1 < E)

            def following(n, t, slot, lead):
                return (n, t + lead, slot) if t + lead < TILES else (n + 1, t + lead - TILES, 1 - slot)

            def gpsimd(pool):
                pool.wait_ge(*before)
                router.gpsimd(pool)
                entry.gpsimd(pool)
                pool.sem_inc(s.prod, RELUS)
                for t in range(AHEAD):
                    gpsimd_prod(pool, 0, t)

                def step(n, slot, more):
                    for t in range(TILES):
                        if t + AHEAD < TILES or more:
                            gpsimd_prod(pool, *following(n, t, slot, AHEAD)[0:2])
                over_experts(pool, step)

            def scalar(act):
                entry.scalar(act)
                router.scalar_last(act)
                act.sem_inc(s.w, 1)
                for m in range(3):
                    scalar_size(act, 0, m)
                for m in range(3):
                    scalar_weights(act, 0, 0, m)
                act.sem_inc(s.shifted, RING)
                for t in range(AHEAD):
                    scalar_relu(act, 0, t)
                for t in range(SHIFT_AHEAD):
                    scalar_shift(act, 0, t)

                def step(n, slot, more):
                    for t in range(TILES):
                        if t < 3 and more:
                            scalar_size(act, n + 1, t)
                        if t + SHIFT_AHEAD < TILES or more:
                            scalar_shift(act, *following(n, t, slot, SHIFT_AHEAD)[0:2])
                        scalar_back(act, n, t)
                        if t + AHEAD < TILES or more:
                            scalar_relu(act, *following(n, t, slot, AHEAD)[0:2])
                        if t in TURN_AT and more:
                            scalar_weights(act, n + 1, 1 - slot, TURN_AT.index(t))
                over_experts(act, step)

            def vector(dve):
                dve.wait_ge(*before)
                dve.sem_inc(s.tern, 3)
                router.vector_weights(dve)
                entry.vector(dve)
                router.vector_last(dve)
                dve.wait_ge(quant.chain, 2 * BLOCKS)
                dve.tensor_tensor(step3, quant.step, quant.step, ALU.mult).then_inc(s.chain, 1)
                dve.wait_ge(s.chain, 1)
                dve.tensor_tensor(step3, step3, quant.step, ALU.mult).then_inc(s.chain, 1)
                dve.wait_ge(s.chain, 2)
                vector_scales(dve, 0, 0)
                for m in range(3):
                    for part in range(3):
                        vector_ternary(dve, 0, m, part)
                dve.sem_inc(s.once, 2)
                dve.sem_inc(s.acc, 2)
                for t in range(AHEAD):
                    vector_once(dve, 0, t)
                    if t >= AHEAD - PEAK_AHEAD:
                        vector_peak(dve, 0, t - (AHEAD - PEAK_AHEAD), 0)

                def step(n, slot, more):
                    for t in range(TILES):
                        if t == 3 and more:
                            vector_scales(dve, n + 1, 1 - slot)
                        if t + AHEAD < TILES or more:
                            vector_once(dve, *following(n, t, slot, AHEAD)[0:2])
                        if t + PEAK_AHEAD < TILES or more:
                            vector_peak(dve, *following(n, t, slot, PEAK_AHEAD))
                        vector_back(dve, n, t)
                        for third in range(9):
                            if t == TURN_AT[0] - 2 + 2 * third // 3 and more:
                                vector_ternary(dve, n + 1, *divmod(third, 3))
                over_experts(dve, step)
                dve.wait_ge(s.acc, E * TILES + 2)
                dve.sem_inc(done, TILES)

            def tensor(pe):
                pe.wait_ge(*before)
                router.tensor_weights(pe)
                entry.tensor(pe)
                pe.wait_ge(quant.turned, DC * BLOCKS)
                pe.wait_ge(router.kept, router.all_kept)
                tensor_total(pe, 0)
                for m in range(3):
                    tensor_turn(pe, 0, m)
                pe.wait_ge(s.w, 4)
                pe.sem_inc(s.turned, 2)
                for t in range(AHEAD):
                    tensor_up(pe, 0, t, 0)

                def step(n, slot, more):
                    for t in range(TILES):
                        if t == 2 and more:
                            tensor_total(pe, n + 1)
                        tensor_turn_tile(pe, n, t)
                        if t + AHEAD < TILES or more:
                            if t + AHEAD == TILES:
                                hold(pe, s.w, (n + 1) * 3 + 4)
                            tensor_up(pe, *following(n, t, slot, AHEAD))
                        tensor_down(pe, n, t, slot)
                        if t in TURN_AT and more:
                            tensor_turn(pe, n + 1, TURN_AT.index(t))
                over_experts(pe, step)

            return sync, gpsimd, scalar, vector, tensor

        def layer2_attention(before, done):
            HEADS, GROUPS, HD = 32, 8, 8
            GD = GROUPS * HD
            PAIRS = HEADS // GROUPS // 2
            UNITS = BATCH * PAIRS
            QB = 4
            PARTS = BATCH // QB
            PT = QB * SEQ // P
            SLOTS = 2 * QB
            ROUND = SLOTS * PAIRS
            RING = 4
            SC = GROUPS * SEQ // P
            AUG = HD + 1
            lay = Layout()
            wqT, wkT, wvT, wfT = lay(DC, 2, P), lay(DC, P), lay(DC, GD), lay(2, D)
            xT, cT = lay(DC, QB * SEQ), lay(DC, QB, 2, SEQ)
            qT = lay(SLOTS, 2 * SEQ)
            kT = lay(QB, SEQ)
            kblk = lay(QB, GROUPS, SEQ)
            vblk = lay(SLOTS, SC, 2 * AUG)
            score, prob, probT = lay(2, GROUPS * SEQ), lay(2, GROUPS * SEQ), lay(2, GROUPS * SEQ)
            top, inv = lay(2, GROUPS), lay(2, PAIRS, GROUPS)
            attended, attendedT = lay(2, PAIRS, GD), lay(2, 2, SEQ)
            band, in_group = lay(2, GROUPS), lay(GROUPS)
            bias = lay(D)
            norm = make_norm(4)
            s = Names()
            (
                s.fold, s.group, s.ones, s.bias, s.biased, s.ctx_ps, s.cT, s.x_ps, s.xT, s.kv_ps, s.kT,
                s.vblk, s.q_ps, s.qT, s.kblk, s.score, s.top, s.shifted, s.exp, s.probT_ps, s.probT, s.read, s.inv, s.att, s.attT_ps,
                s.attT, s.out
            ) = sems("a2", "fold group ones bias biased ctx_ps cT x_ps xT kv_ps kT vblk q_ps qT kblk score top "
                     "shifted exp probT_ps probT read inv att attT_ps attT out")
            was = count_weights(loaded=16 * 5, turned=1, ready=2 * DC + 4)
            raw_q, raw_f = raw[:, 0:2 * D].rearrange("p (a k) -> p a k", a=2), raw[:, 2 * D:4 * D].rearrange("p (a k) -> p a k", a=2)
            raw_k, raw_v = raw[:, 4 * D:5 * D], raw[:, 5 * D:6 * D]
            fold_f = raw[:, 6 * D:8 * D].rearrange("p (a m k) -> p a m k", a=DC, m=2)
            raw_b = raw[:, 8 * D:9 * D]
            SOFT, IN, TURN, READ, OUT = (bank[0], bank[1]), bank[2], (bank[3], bank[4]), (bank[5], bank[6]), bank[7]

            def inside(i, x, units):
                return not isinstance(i, int) or 0 <= x < units

            def over_units(eng, step, last):
                for x in range(ROUND // 2):
                    step(0, x)
                with eng.Fori(0, UNITS // ROUND - 1) as i:
                    for x in range(ROUND // 2, ROUND + ROUND // 2):
                        step(i, x)
                for x in range(UNITS - ROUND // 2, UNITS + last):
                    step(0, x)

            def nth(i, x, per):
                return i * (ROUND // per) + x // per

            PART = QB * PAIRS
            BATCH_U, TILE_U = PAIRS, 2 * PAIRS

            def sync(sp):
                sp.wait_ge(whole_used.tern_signal, whole_used.tern)
                sp.dma_start(raw_q, io["L2_xattn_Wq"].rearrange("(a p) k -> p a k", p=P)).then_inc(weight.loaded, 16)
                sp.dma_start(raw_f, io["L2_xattn_Wfc"].rearrange("(a p) k -> p a k", p=P)).then_inc(weight.loaded, 16)
                sp.dma_start(raw_k[0:GD, :], io["L2_xattn_Wk"]).then_inc(weight.loaded, 16)
                sp.dma_start(raw_v[0:GD, :], io["L2_xattn_Wv"]).then_inc(weight.loaded, 16)
                sp.dma_start(raw_b, io["L2_xattn_bfc"].partition_broadcast(P)).then_inc(weight.loaded, 16)
                tiles = io["ctx_2048"].rearrange("b s d -> (b s) d").rearrange("(t p) d -> t p d", p=P)
                for k in range(RING):
                    sp.dma_start(ctx_in[:, k, :], tiles[k]).then_inc(ctx_here[k], 16)
                with sp.Fori(1, TILES // RING) as i:
                    for k in range(RING):
                        sp.wait_ge(s.ctx_ps, (i - 1) * (RING // PT) + k // PT + 1)
                        sp.dma_start(ctx_in[:, k, :], tiles[ds(i * RING + k, 1)].rearrange("o p d -> p (o d)")).then_inc(ctx_here[k], 16)

            def gpsimd(pool):
                pool.wait_ge(*before)
                flat_band = band.rearrange("p h g -> p (h g)")
                pool.memset(flat_band, 1.0).then_inc(s.group, 1)
                pool.wait_ge(s.group, 1)
                pool.affine_select(out=flat_band, in_=flat_band, compare_op=ALU.is_ge, fill=0.0, base=0,
                                   pattern=[[-HD, 2 * GROUPS]], channel_multiplier=1).then_inc(s.group, 1)
                pool.wait_ge(s.group, 2)
                pool.affine_select(out=flat_band, in_=flat_band, compare_op=ALU.is_ge, fill=0.0, base=HD - 1,
                                   pattern=[[HD, 2 * GROUPS]], channel_multiplier=-1).then_inc(s.group, 1)
                pool.wait_ge(s.group, 3)
                pool.tensor_tensor(in_group, band[:, 0, :], band[:, 1, :], ALU.add).then_inc(s.group, 1)
                norm.gpsimd_stats(pool)
                pool.wait_ge(s.group, 4)
                pool.wait_ge(s.bias, 1)

                def part(h):
                    for e in range(PT):
                        t = h * PT + e
                        pool.wait_ge(norm.xn, norm.first * BT + t + 1)
                        pool.tensor_tensor(x_tile(t), x_tile(t), bias, ALU.add).then_inc(s.biased, 1)
                    n = [P, GROUPS, SEQ]
                    for b in range(QB):
                        pool.wait_ge(s.kT, h + 1)
                        if not isinstance(h, int) or h:
                            pool.wait_ge(s.score, (h * QB + b - QB + 1) * PAIRS)
                        pool.tensor_tensor(kblk[:, b], kT[:, b, :].unsqueeze(1).to_broadcast(n), in_group.unsqueeze(2).to_broadcast(n),
                                           ALU.mult).then_inc(s.kblk, 1)
                part(0)
                with pool.Fori(1, PARTS) as h:
                    part(h)

            def scalar_context(act, h, at):
                act.wait_ge(s.ctx_ps, h + 1)
                for c in range(DC):
                    got = IN[:, c * QB * SEQ:(c + 1) * QB * SEQ].rearrange("p (b t) -> p b t", b=QB)
                    act.activation(cT[:, c], got.unsqueeze(2).to_broadcast([P, QB, 2, SEQ]), ACT.Copy).then_inc(s.cT, 1)

            def scalar_tokens(act, h, at):
                act.wait_ge(s.x_ps, h + 1)
                act.activation(flat(xT), IN[:, :], ACT.Copy).then_inc(s.xT, 1)

            def scalar_keys(act, h, at):
                act.wait_ge(s.kv_ps, h + 1)
                if not isinstance(h, int) or h:
                    act.wait_ge(s.kblk, h * QB)
                act.activation(flat(kT), IN[:, 0:QB * SEQ], ACT.Copy).then_inc(s.kT, 1)
                got = IN[:, QB * SEQ:].rearrange("p (b c g d) -> p b c g d", b=QB, c=SC, g=2)
                for half in range(2):
                    rows = slice(half * SEQ, (half + 1) * SEQ)
                    act.activation(vblk[rows, at * QB:(at + 1) * QB, :, half * AUG:half * AUG + HD], got[rows, :, :, half, :], ACT.Copy).then_inc(s.vblk, 1)

            def scalar_queries(act, h, at):
                act.wait_ge(s.q_ps, h + 1)
                act.activation(qT[:, at * QB:(at + 1) * QB, :].rearrange("p b (m t) -> p m b t", m=2),
                               IN[:, :].rearrange("p (m b t) -> p m b t", m=2, b=QB), ACT.Copy).then_inc(s.qT, 1)

            scalar_stages = (scalar_context, scalar_tokens, scalar_keys, scalar_queries)

            def scalar(act):
                act.wait_ge(weight.loaded, was.loaded + 16 * 5)
                for a in range(DC):
                    cols = raw_f[:, a, :].rearrange("p (g q m d) -> p m q g d", g=GROUPS, q=PAIRS, m=2)
                    for m in range(2):
                        act.activation(fold_f[:, a, m, :].rearrange("p (q g d) -> p q g d", q=PAIRS, g=GROUPS), cols[:, m], ACT.Copy).then_inc(s.fold, 1)
                act.wait_ge(weight.turned, was.turned + 1)
                for c in range(DC):
                    cols = bank[0][:, c * D:(c + 1) * D].rearrange("p (g q m d) -> p m q g d", g=GROUPS, q=PAIRS, m=2)
                    for m in range(2):
                        act.activation(wqT[:, c, m, :].rearrange("p (q g d) -> p q g d", q=PAIRS, g=GROUPS), cols[:, m], ACT.Copy).then_inc(weight.ready, 1)
                act.activation(flat(wfT), bank[1][:, :], ACT.Copy).then_inc(weight.ready, 1)
                for half in range(2):
                    act.activation(wkT[:, :, half * GD:(half + 1) * GD], bank[2][:, 0:DC * GD].rearrange("p (c k) -> p c k", c=DC), ACT.Copy).then_inc(weight.ready, 1)
                act.activation(flat(wvT), bank[2][:, DC * GD:2 * DC * GD], ACT.Copy).then_inc(weight.ready, 1)
                act.wait_ge(s.ones, 3)
                for stage in scalar_stages:
                    stage(act, 0, 0)

                def step(i, x):
                    if inside(i, x, UNITS):
                        act.wait_ge(s.shifted, i * ROUND + x + 1)
                        act.activation(prob[:, x % 2, :], score[:, x % 2, :], ACT.Exp, scale=HD ** -0.5).then_inc(s.exp, 1)
                    if inside(i, x - 1, UNITS):
                        act.wait_ge(s.probT_ps, i * ROUND + x)
                        act.activation(probT[:, (x - 1) % 2, :], TURN[(x - 1) % 2][:, :], ACT.Copy).then_inc(s.probT, 1)
                    if x % 4 == 3 and inside(i, x - 7, UNITS):
                        act.wait_ge(s.attT_ps, nth(i, x - 7, TILE_U) + 1)
                        act.activation(attendedT, OUT[:, 0:2 * P].rearrange("p (b m t) -> p m b t", b=2, m=2), ACT.Copy).then_inc(s.attT, 1)
                    if 1 <= x % PART <= 4 and inside(i, x + PART, UNITS):
                        scalar_stages[x % PART - 1](act, nth(i, x, PART) + 1, (x // PART + 1) % 2)
                over_units(act, step, 9)

            def vector_norm(dve, t, k):
                dve.tensor_scalar(xn[:, k, :], x_tile(t), flat(ln_mv[:, ds(t, 1), 0:1]), ln_rstd[:, ds(t, 1)],
                                  ALU.subtract, ALU.mult).then_inc(norm.xn, 1)

            def vector(dve):
                dve.wait_ge(*before)
                norm.vector_stats(dve)
                dve.memset(vblk.rearrange("p b c a -> p (b c a)"), 0.0).then_inc(s.ones, 1)
                dve.wait_ge(s.ones, 1)
                for half in range(2):
                    rows = slice(half * SEQ, (half + 1) * SEQ)
                    dve.memset(vblk[rows, :, :, half * AUG + HD], 1.0).then_inc(s.ones, 1)
                dve.wait_ge(weight.loaded, was.loaded + 16 * 5)
                dve.tensor_scalar(bias, raw_b, gates[:, 2:3], None, ALU.mult).then_inc(s.bias, 1)
                dve.wait_ge(norm.rstd, norm.rstd_there)
                for t in range(PT):
                    vector_norm(dve, t, t)

                def step(i, x):
                    if x % PART == 0 and inside(i, x + PART, UNITS):
                        for e in range(PT):
                            vector_norm(dve, (nth(i, x, PART) + 1) * PT + e, (x // PART + 1) % 2 * PT + e)
                    if inside(i, x, UNITS):
                        U = i * ROUND + x
                        got = SOFT[x % 2][:, :].rearrange("p (g k) -> p g k", g=GROUPS)
                        dve.wait_ge(s.score, U + 1)
                        dve.tensor_reduce(top[:, x % 2, :], got, AX.X, ALU.max).then_inc(s.top, 1)
                        dve.wait_ge(s.top, U + 1)
                        if not isinstance(i, int) or x >= 2:
                            dve.wait_ge(s.exp, U - 1)
                        dve.tensor_tensor(score[:, x % 2, :].rearrange("p (g k) -> p g k", g=GROUPS), got,
                                          top[:, x % 2, :].unsqueeze(2).to_broadcast([P, GROUPS, SEQ]), ALU.subtract).then_inc(s.shifted, 1)
                    if x % 2 == 0 and inside(i, x - 4, UNITS):
                        B = nth(i, x - 4, BATCH_U)
                        j = (x - 4) // 2 % 2
                        got = READ[j][:, 0:PAIRS * SC * 2 * AUG].rearrange("p (m g a) -> p m g a", m=PAIRS, g=GROUPS)
                        hold(dve, s.read, B + 1)
                        dve.reciprocal(inv[:, j], got[:, :, :, HD]).then_inc(s.inv, 1)
                        dve.wait_ge(s.inv, B + 1)
                        dve.tensor_tensor(attended[:, j].rearrange("p m (g d) -> p m g d", g=GROUPS), got[:, :, :, 0:HD],
                                          inv[:, j].unsqueeze(3).to_broadcast([P, PAIRS, GROUPS, HD]), ALU.mult).then_inc(s.att, 1)
                    if x % 4 == 1 and inside(i, x - 9, UNITS):
                        t = nth(i, x - 9, TILE_U)
                        dve.wait_ge(s.out, t + 1)
                        dve.wait_ge(s.biased, t + 1)
                        dve.scalar_tensor_tensor(x_tile(t), OUT[:, 2 * P:2 * P + D], gates[:, 2:3], x_tile(t), ALU.mult, ALU.add).then_inc(done, 1)
                over_units(dve, step, 10)

            def tensor_context(pe, h, at):
                if not isinstance(h, int) or h:
                    hold(pe, s.qT, h)
                for e in range(PT):
                    k = at * PT + e
                    hold(pe, ctx_here[k], RING_LOADS + h * 8 - at * 8 + 16)
                for c in range(DC):
                    for e in range(PT):
                        tp = pe.transpose(IN[:, (c * PT + e) * P:(c * PT + e + 1) * P], ctx_in[:, at * PT + e, c * P:(c + 1) * P], ident[:, :])
                tp.then_inc(s.ctx_ps, 1)

            def tensor_tokens(pe, h, at):
                hold(pe, norm.xn, norm.first * BT + h * PT + PT)
                hold(pe, s.cT, h * DC + DC)
                for c in range(DC):
                    for e in range(PT):
                        tp = pe.transpose(IN[:, (c * PT + e) * P:(c * PT + e + 1) * P], xn[:, at * PT + e, c * P:(c + 1) * P], ident[:, :])
                tp.then_inc(s.x_ps, 1)

            def tensor_keys(pe, h, at):
                hold(pe, s.xT, h + 1)
                for c in range(DC):
                    pe.matmul(IN[:, 0:QB * SEQ], wkT[:, c, :], cT[:, c, :, 0, :], start=c == 0, stop=c == DC - 1)
                for b in range(QB):
                    for c in range(DC):
                        to = QB * SEQ + b * GD
                        mm = pe.matmul(IN[:, to:to + GD], cT[:, c, b].rearrange("p h t -> p (h t)"), wvT[:, c, :], start=c == 0, stop=c == DC - 1)
                mm.then_inc(s.kv_ps, 1)

            def tensor_queries(pe, h, at):
                hold(pe, s.vblk, h * 2 + 2)
                for m in range(2):
                    for c in range(DC):
                        mm = pe.matmul(IN[:, m * QB * SEQ:(m + 1) * QB * SEQ], wqT[:, c, m, :], xT[:, c, :], start=c == 0, stop=c == DC - 1)
                mm.then_inc(s.q_ps, 1)

            tensor_stages = (tensor_context, tensor_tokens, tensor_keys, tensor_queries)

            def tensor_scores(pe, i, x):
                slot, pair = x // PAIRS % SLOTS, x % PAIRS
                if x % PART == 0:
                    hold(pe, s.qT, nth(i, x, PART) + 1)
                if pair == 0:
                    hold(pe, s.kblk, nth(i, x, BATCH_U) + 1)
                if not isinstance(i, int) or x >= 2:
                    hold(pe, s.shifted, i * ROUND + x - 1)
                rows = slice(pair * GD, (pair + 1) * GD)
                pe.matmul(SOFT[x % 2][:, :], qT[rows, slot, :], kblk[rows, slot % QB].rearrange("p g k -> p (g k)"),
                          start=True, stop=True).then_inc(s.score, 1)

            def tensor(pe):
                pe.wait_ge(*before)
                pe.wait_ge(s.fold, 2 * DC)
                for c in range(DC):
                    for a in range(DC):
                        pe.transpose(bank[0][:, c * D + a * P:c * D + (a + 1) * P], raw_q[:, a, c * P:(c + 1) * P], ident[:, :])
                for m in range(2):
                    for a in range(DC):
                        pe.transpose(bank[1][:, m * D + a * P:m * D + (a + 1) * P], fold_f[:, a, m, :], ident[:, :])
                for j, w in enumerate((raw_k, raw_v)):
                    for c in range(DC):
                        at = (j * DC + c) * GD
                        tp = pe.transpose(bank[2][:, at:at + GD], w[0:GD, c * P:(c + 1) * P], ident[0:GD, 0:GD])
                tp.then_inc(weight.turned, 1)
                pe.wait_ge(weight.ready, was.ready + 2 * DC + 4)
                for stage in tensor_stages:
                    stage(pe, 0, 0)
                for x in range(2):
                    tensor_scores(pe, 0, x)

                def step(i, x):
                    if inside(i, x + 2, UNITS):
                        tensor_scores(pe, i, x + 2)
                    if inside(i, x, UNITS):
                        hold(pe, s.exp, i * ROUND + x + 1)
                        for c in range(SC):
                            tp = pe.transpose(TURN[x % 2][:, c * P:(c + 1) * P], prob[:, x % 2, c * P:(c + 1) * P], ident[:, :])
                        tp.then_inc(s.probT_ps, 1)
                    if inside(i, x - 1, UNITS):
                        slot, pair = (x - 1) // PAIRS % SLOTS, (x - 1) % PAIRS
                        B = nth(i, x - 1, BATCH_U)
                        hold(pe, s.probT, i * ROUND + x)
                        if pair == 0 and (not isinstance(B, int) or B >= 2):
                            hold(pe, s.att, B - 1)
                        for c in range(SC):
                            at = (pair * SC + c) * 2 * AUG
                            mm = pe.matmul(READ[slot % 2][:, at:at + 2 * AUG], probT[:, (x - 1) % 2, c * P:(c + 1) * P], vblk[:, slot, c, :],
                                           start=True, stop=True)
                        if pair == PAIRS - 1:
                            mm.then_inc(s.read, 1)
                    if x % 2 == 1 and inside(i, x - 5, UNITS):
                        B = nth(i, x - 5, BATCH_U)
                        j = (x - 5) // 2 % 2
                        hold(pe, s.att, B + 1)
                        if j == 0 and (not isinstance(B, int) or B):
                            hold(pe, done, before[1] + nth(i, x - 5, TILE_U))
                        tp = pe.transpose(OUT[:, j * P:(j + 1) * P], attended[:, j].rearrange("p m k -> p (m k)"), ident[:, :])
                        if j:
                            tp.then_inc(s.attT_ps, 1)
                    if x % 4 == 0 and inside(i, x - 8, UNITS):
                        hold(pe, s.attT, nth(i, x - 8, TILE_U) + 1)
                        for m in range(2):
                            mm = pe.matmul(OUT[:, 2 * P:2 * P + D], attendedT[:, m].rearrange("p b t -> p (b t)"), wfT[:, m, :], start=m == 0, stop=m == 1)
                        mm.then_inc(s.out, 1)
                    if x % PART < 4 and inside(i, x + PART, UNITS):
                        tensor_stages[x % PART](pe, nth(i, x, PART) + 1, (x // PART + 1) % 2)
                over_units(pe, step, 10)

            return sync, gpsimd, scalar, vector, tensor

        def layer2_experts(before, done):
            EXPERTS = 7

            def load(sp, n, raw_up, raw_down, signal):
                for mat, (routed, shared) in enumerate((("L2_ffn_W1", "L2_ffn_Ws1"), ("L2_ffn_Wg", "L2_ffn_Wsg"), ("L2_ffn_W2", "L2_ffn_Ws2"))):
                    w = io[shared] if isinstance(n, int) and n == EXPERTS else io[routed][ds(n, 1)].rearrange("o a b -> (o a) b")
                    sp.dma_start(raw_down if mat == 2 else raw_up[:, mat], w.rearrange("(c p) h -> p c h", p=P)).then_inc(signal, 16)
            load.count = 3

            return gated_experts("f2", 5, 2, 3, gates[:, 6:7], before, done, EXPERTS, 3,
                                 (False, io["L2_ffn_gate_w"], io["L2_ffn_gate_b"], io["L2_ffn_biases"]),
                                 chunks=[(0, P), (P, P)], outputs=[[(0, 0, P)], [(0, 0, P)]], groups=EXPERTS + 1,
                                 load=load, up_width=2 * P, down_chunks=2)

        def layer3_attention(before, done):
            NB = BLK // SEQ
            STEPS = int(np.log2(SEQ))
            lay = Layout()
            w_in, w_out = lay(DC, D), lay(DC, D)
            power, series = lay(STEPS), lay(SEQ)
            weigh = lay(SEQ)
            row_weight, weight_sum, weights = lay(1), lay(1), lay(2)
            pooled, state, summary = lay(DC, BATCH), lay(DC, BATCH), lay(BLOCKS, D)
            weight_sums = lay(BATCH)
            gain, offset = lay(D), lay(D)
            shifted, normed = lay(BT, D), lay(BT, D)
            stat, mean_var, rstd = lay(BT, 6), lay(BT, 2), lay(BT)
            var_eps = lay(BT)
            decay = lay(1)
            of_row = lay(SEQ)
            of_half = lay(2)
            spread = lay(BT, P)[0:NB]
            bias_in = lay(D)[0:1]
            bias_out = lay(D)[0:1]
            affine = lay(2, D)
            assert lay.at <= L3_ATTENTION, lay.at
            norm = make_norm(6)
            s = Names()
            (
                s.masks, s.keep, s.chain, s.pooled_ps, s.pooled, s.state_ps, s.state, s.summary_ps, s.summary,
                s.spread, s.y, s.stat, s.rstd, s.normed, s.scaled, s.affine, s.acc
            ) = sems("a3",
                 "masks keep chain pooled_ps pooled state_ps state summary_ps summary spread y stat rstd "
                 "normed scaled affine acc")
            was = count_weights(loaded=16 * 7, turned=1, ready=2)
            raw_in, raw_out = raw[:, 0:DC * D].rearrange("p (a k) -> p a k", a=DC), raw[:, DC * D:2 * DC * D].rearrange("p (a k) -> p a k", a=DC)
            ctx_buf = (ctx_in, ctx_sb)
            s.ctx = ctx_here[0:2]

            def sync(sp):
                sp.wait_ge(*before)
                for i in range(2):
                    sp.dma_start(ctx_buf[i][:, :, :], io["ctx_2048"].rearrange("b s d -> (b s) d").rearrange("(i k p) d -> i p k d", k=BT, p=P)[i]).then_inc(s.ctx[i % 2], 16)
                sp.dma_start(decay[:, :], io["L3_xattn_decay"].partition_broadcast(P)).then_inc(weight.loaded, 16)
                sp.dma_start(raw_in, io["L3_xattn_W_in"].rearrange("(a p) k -> p a k", p=P)).then_inc(weight.loaded, 16)
                sp.dma_start(raw_out, io["L3_xattn_W_out"].rearrange("(a p) k -> p a k", p=P)).then_inc(weight.loaded, 16)
                sp.dma_start(bias_in[:, :], io["L3_xattn_b_in"].partition_broadcast(1)).then_inc(weight.loaded, 16)
                sp.dma_start(bias_out[:, :], io["L3_xattn_b_out"].partition_broadcast(1)).then_inc(weight.loaded, 16)
                sp.dma_start(affine[:, 0, :], io["L3_xattn_gamma"].partition_broadcast(P)).then_inc(weight.loaded, 16)
                sp.dma_start(affine[:, 1, :], io["L3_xattn_beta"].partition_broadcast(P)).then_inc(weight.loaded, 16)
                for i in range(2, BLOCKS):
                    sp.wait_ge(s.pooled_ps, i - 1)
                    sp.dma_start(ctx_buf[i % 2][:, :, :], io["ctx_2048"].rearrange("b s d -> (b s) d").rearrange("(i k p) d -> i p k d", k=BT, p=P)[i]).then_inc(s.ctx[i % 2], 16)

            def gpsimd(pool):
                pool.wait_ge(*before)
                pool.memset(of_row[:, :], 0.0).then_inc(s.masks, 1)
                pool.memset(spread[:, :, :], 0.0).then_inc(s.masks, 1)
                pool.wait_ge(s.masks, 2)
                at = spread[:, :, :].rearrange("r k (h t) -> r k h t", h=2)
                pool.affine_select(out=at, in_=at, compare_op=ALU.not_equal, fill=1.0, base=0,
                                   pattern=[[2, BT], [1, 2], [0, SEQ]], channel_multiplier=-1).then_inc(s.masks, 1)
                for h in range(2):
                    pool.wait_ge(s.masks, 3 + h)
                    pool.affine_select(out=of_row[:, :], in_=of_row[:, :], compare_op=ALU.not_equal, fill=1.0,
                                       base=1 - SEQ * (h + 1), pattern=[[1, SEQ]], channel_multiplier=1).then_inc(s.masks, 1)
                pool.wait_ge(s.affine, 2)
                norm.gpsimd_stats(pool)
                with pool.Fori(0, BLOCKS) as i:
                    hold(pool, s.stat, i * 2 * BT + 2 * BT)
                    pool.tensor_scalar(var_eps, mean_var[:, :, 1], LN_EPS, 1.0, ALU.add, ALU.mult).then_inc(s.rstd, 1)
                    pool.wait_ge(s.rstd, i * 2 + 1)
                    pool.tensor_tensor(rstd, var_eps, neg_half[:, 0:BT], ALU.pow).then_inc(s.rstd, 1)
                    pool.wait_ge(s.normed, i * BT + BT)
                    pool.tensor_tensor(normed, normed, gain.unsqueeze(1).to_broadcast([P, BT, D]), ALU.mult).then_inc(s.scaled, 1)
                    pool.wait_ge(s.scaled, i * 2 + 1)
                    pool.tensor_tensor(normed, normed, offset.unsqueeze(1).to_broadcast([P, BT, D]), ALU.add).then_inc(s.scaled, 1)

            def scalar(act):
                act.wait_ge(weight.loaded, was.loaded + 16 * 7)
                act.activation(decay[:, :], decay[:, :], ACT.Sigmoid).then_inc(s.keep, 1)
                act.wait_ge(weight.turned, was.turned + 1)
                act.activation(flat(w_in), bank[0][:, :], ACT.Copy).then_inc(weight.ready, 1)
                act.activation(flat(w_out), bank[1][:, :], ACT.Copy).then_inc(weight.ready, 1)
                act.wait_ge(s.pooled_ps, BLOCKS)
                act.activation(flat(pooled), bank[2][:, 0:DC * BATCH], ACT.Copy).then_inc(s.pooled, 1)
                act.wait_ge(s.summary_ps, 1)
                for h in range(2):
                    act.activation(flat(summary[0:NB, 2 * h:2 * h + 2, :]), bank[4 + h][0:NB, :], ACT.Copy).then_inc(s.summary, 1)

            def vector(dve):
                dve.wait_ge(*before)
                norm.vector_stats(dve)
                dve.wait_ge(s.keep, 1)
                dve.wait_ge(s.masks, 5)
                link = linker(dve, s.chain)
                link(dve.memset(of_half[:, :], 0.0))
                link(dve.memset(of_half[0:SEQ, 0:1], 1.0))
                link(dve.memset(of_half[SEQ:P, 1:2], 1.0))
                link(dve.tensor_copy(power[:, 0:1], decay[:, :]))
                for n in range(1, STEPS):
                    link(dve.tensor_tensor(power[:, n:n + 1], power[:, n - 1:n], power[:, n - 1:n], ALU.mult))
                link(dve.memset(series[:, 0:1], 1.0))
                for n in range(STEPS):
                    m = 1 << n
                    link(dve.tensor_scalar(series[:, m:2 * m], series[:, 0:m], power[:, n:n + 1], series[:, m - 1:m], ALU.mult, ALU.add))
                link(dve.tensor_reduce(weight_sum, series, AX.X, ALU.add))
                link(dve.tensor_tensor(weigh, series, of_row[:, :], ALU.mult))
                link(dve.tensor_reduce(row_weight, weigh, AX.X, ALU.add))
                link(dve.tensor_scalar(weights, of_half[:, :], row_weight, 1.0 / SEQ, ALU.mult, ALU.mult))
                link(dve.tensor_scalar(weight_sums, ones[:, 0:BATCH], weight_sum, 1.0 / SEQ, ALU.mult, ALU.mult))
                dve.tensor_scalar(gain, affine[:, 0, :], gates[:, 3:4], None, ALU.mult).then_inc(s.affine, 1)
                dve.tensor_scalar(offset, affine[:, 1, :], gates[:, 3:4], None, ALU.mult).then_inc(s.affine, 1)
                dve.wait_ge(s.state_ps, 1)
                for c in range(DC):
                    dve.tensor_copy(state[:, c, :], bank[3][:, c * BATCH:(c + 1) * BATCH]).then_inc(s.state, 1)
                dve.sem_inc(s.y, 1)
                with dve.Fori(0, BLOCKS) as i:
                    norm.vector_norm(dve, i)
                    for k in range(BT):
                        if k % 2 == 0:
                            dve.wait_ge(s.spread, i * 2 + k // 2 + 1)
                        if k == 0:
                            dve.wait_ge(norm.xn, (norm.first + i) * BT + BT)
                        dve.tensor_tensor(shifted[:, k, :], xn[:, k, :], bank[6 + k // 2][:, k % 2 * D:k % 2 * D + D], ALU.add).then_inc(s.y, 1)
                    dve.wait_ge(s.y, i * BT + BT + 1)
                    for k in range(BT):
                        dve.bn_stats(stat[:, k, :], shifted[:, k, :]).then_inc(s.stat, 1)
                    hold(dve, s.stat, i * 2 * BT + BT)
                    for k in range(BT):
                        dve.bn_aggr(mean_var[:, k, :], stat[:, k, :]).then_inc(s.stat, 1)
                    dve.wait_ge(s.rstd, i * 2 + 2)
                    for k in range(BT):
                        dve.tensor_scalar(normed[:, k, :], shifted[:, k, :], mean_var[:, k, 0:1], rstd[:, k:k + 1],
                                          ALU.subtract, ALU.mult).then_inc(s.normed, 1)
                    dve.wait_ge(s.scaled, i * 2 + 2)
                    tiles = X[:, ds(i * BT, BT), :]
                    dve.tensor_tensor(tiles, tiles, normed, ALU.add).then_inc(s.acc, 1)
                dve.wait_ge(s.acc, BLOCKS)
                dve.sem_inc(done, TILES)

            def tensor(pe):
                pe.wait_ge(*before)
                pe.wait_ge(weight.loaded, was.loaded + 16 * 7)
                for j, w in enumerate((raw_in, raw_out)):
                    for c in range(DC):
                        for a in range(DC):
                            tp = pe.transpose(bank[j][:, c * D + a * P:c * D + (a + 1) * P], w[:, a, c * P:(c + 1) * P], ident[:, :])
                tp.then_inc(weight.turned, 1)
                pe.wait_ge(weight.turned, was.turned + 1)
                pe.sem_inc(weights_free, 1)
                pe.wait_ge(s.chain, 2 * STEPS + 9)
                for i in range(BLOCKS):
                    pe.wait_ge(s.ctx[i % 2], 2 * RING_LOADS + 16 * (i // 2 + 1))
                    for k in range(BT):
                        for c in range(DC):
                            at = c * BATCH + (i * BT + k) * 2
                            mm = pe.matmul(bank[2][:, at:at + 2], ctx_buf[i % 2][:, k, c * P:(c + 1) * P], weights, start=True, stop=True)
                    mm.then_inc(s.pooled_ps, 1)
                pe.wait_ge(s.pooled, 1)
                pe.wait_ge(weight.ready, was.ready + 2)
                for m in range(DC):
                    for c in range(DC):
                        pe.matmul(bank[3][:, m * BATCH:(m + 1) * BATCH], w_in[:, c, m * P:(m + 1) * P], pooled[:, c, :],
                                  start=c == 0, stop=False)
                    mm = pe.matmul(bank[3][:, m * BATCH:(m + 1) * BATCH], bias_in[0:1, m * P:(m + 1) * P], weight_sums[0:1, :],
                                   start=False, stop=True)
                mm.then_inc(s.state_ps, 1)
                pe.wait_ge(s.state, DC)
                for i in range(BLOCKS):
                    out = bank[4 + i // 2][0:NB, i % 2 * D:i % 2 * D + D]
                    for c in range(DC):
                        pe.matmul(out, state[:, c, i * NB:(i + 1) * NB], w_out[:, c, :], start=c == 0, stop=False)
                    mm = pe.matmul(out, ones[0:1, 0:NB], bias_out[0:1, :], start=False, stop=True)
                mm.then_inc(s.summary_ps, 1)
                pe.wait_ge(s.summary, 2)
                with pe.Fori(0, BLOCKS) as i:
                    hold(pe, s.y, i * BT + 1)
                    for k in range(BT):
                        mm = pe.matmul(bank[6 + k // 2][:, k % 2 * D:k % 2 * D + D], spread[:, k, :], flat(summary[0:NB, ds(i, 1), :]),
                                       start=True, stop=True)
                        if k % 2:
                            mm.then_inc(s.spread, 1)

            return sync, gpsimd, scalar, vector, tensor

        def layer3_experts(before, done):
            I = 1024
            IC = I // P
            MAT = I * D // P
            UP, DOWN = 0, 1
            HALF = I // 2
            lay = Layout()
            lay.at = L3_ATTENTION
            xqT = lay(DC, TOK, dt=BF16)
            norm = make_norm(7)
            up_w, down_w = lay(DC, I, dt=BF16), lay(IC, D, dt=BF16)
            tern = lay(2, MAT, dt=BF16)
            size_sum, mean, per_mean, out_factor = lay(2), lay(2), lay(2), lay(1)
            gelu_scale = lay(TILES)
            hidden, shifted, wholeT = lay(2, I), lay(2, I), lay(2, I, dt=BF16)
            quant = make_quant(1, lay, flat(hidden), xqT)
            peak, unit, rate, out_scale = lay(2), lay(2), lay(2), lay(2)
            s = Names()
            (
                s.raw, s.size, s.total, s.chain, s.ternary, s.tern, s.shifted, s.w_tp, s.w, s.up, s.relu, s.once,
                s.prod, s.peak, s.pair, s.rate, s.turned, s.wholeT, s.down, s.acc
            ) = whole_sems
            was = whole_used
            raw_m = raw[:, 0:2 * MAT].rearrange("p (m k) -> p m k", m=2)
            stored = sem("stored")
            through = (xn, ctx_sb)

            def sync(sp):
                sp.wait_ge(weights_free, 1)
                for m, w in ((UP, "L3_ffn_w1"), (DOWN, "L3_ffn_w2")):
                    sp.dma_start(raw_m[:, m, :].rearrange("p (a k) -> p a k", k=I if m == DOWN else D),
                                 io[w].rearrange("(a p) k -> p a k", p=P)).then_inc(s.raw, 16)
                with sp.Fori(0, BLOCKS) as i:
                    sp.wait_ge(s.acc, was.acc + i * BT + BT)
                    sp.dma_start(block_of(io["out"], i), X[:, ds(i * BT, BT), :]).then_inc(stored, 16)
                sp.wait_ge(stored, 16 * BLOCKS)

            def gpsimd(pool):
                norm.gpsimd_stats(pool)

            def scalar_gelu(act, T, k):
                act.wait_ge(s.up, was.up + T + 1)
                act.wait_ge(s.shifted, was.shifted + T - 1)
                for h in range(2):
                    act.activation(hidden[:, k % 2, h * HALF:(h + 1) * HALF], bank[2 * (k % 2) + h][:, :], ACT.Gelu,
                                   scale=gelu_scale[:, ds(T, 1)]).then_inc(s.relu, 1)

            def scalar_back(act, T, k):
                act.wait_ge(s.turned, was.turned + T + 1)
                for h in range(2):
                    act.activation(wholeT[:, k % 2, h * HALF:(h + 1) * HALF], bank[4 + h][:, :], ACT.Copy, bias=-MAGIC).then_inc(s.wholeT, 1)

            def vector_front(dve, T, k):
                j = slice(k % 2, k % 2 + 1)
                dve.wait_ge(s.relu, was.relu + T * 2 + 2)
                dve.tensor_reduce(peak[:, j], hidden[:, k % 2, :], AX.X, ALU.max, apply_absolute_value=True).then_inc(s.peak, 1)
                dve.wait_ge(s.peak, was.peak + T + 1)
                dve.tensor_scalar(unit[:, j], peak[:, j], QUANT_EPS, 1.0 / 127, ALU.max, ALU.mult).then_inc(s.pair, 1)
                hold(dve, s.pair, was.pair + T * 2 + 1)
                dve.reciprocal(rate[:, j], unit[:, j]).then_inc(s.rate, 1)
                dve.tensor_scalar(out_scale[:, j], unit[:, j], out_factor, None, ALU.mult).then_inc(s.pair, 1)
                dve.wait_ge(s.rate, was.rate + T + 1)
                dve.tensor_scalar(shifted[:, k % 2, :], hidden[:, k % 2, :], rate[:, j], MAGIC, ALU.mult, ALU.add).then_inc(s.shifted, 1)

            def vector_back(dve, T, k):
                dve.wait_ge(s.down, was.down + T + 1)
                dve.wait_ge(s.pair, was.pair + T * 2 + 2)
                dve.scalar_tensor_tensor(x_tile(T), bank[6 + k % 2][:, 0:D], out_scale[:, k % 2:k % 2 + 1], x_tile(T),
                                         ALU.mult, ALU.add).then_inc(s.acc, 1)

            def tensor_up(pe, T, k):
                hold(pe, s.relu, was.relu + T * 2 - 2)
                for h in range(2):
                    for c in range(DC):
                        mm = pe.matmul(bank[2 * (k % 2) + h][:, :], flat(xqT[:, c:c + 1, ds(T * P, P)]), up_w[:, c, h * HALF:(h + 1) * HALF],
                                       start=c == 0, stop=c == DC - 1)
                mm.then_inc(s.up, 1)

            def tensor_turn(pe, T, k):
                hold(pe, s.shifted, was.shifted + T + 1)
                for c in range(IC):
                    tp = pe.transpose(bank[4 + c // 4][:, c % 4 * P:(c % 4 + 1) * P], shifted[:, k % 2, c * P:(c + 1) * P], ident[:, :])
                tp.then_inc(s.turned, 1)

            def tensor_down(pe, T, k):
                hold(pe, s.wholeT, was.wholeT + T * 2 + 2)
                hold(pe, s.acc, was.acc + T - 1)
                for c in range(IC):
                    mm = pe.matmul(bank[6 + k % 2][:, 0:D], wholeT[:, k % 2, c * P:(c + 1) * P], down_w[:, c, :],
                                   start=c == 0, stop=c == IC - 1)
                mm.then_inc(s.down, 1)

            def over_blocks(eng, step):
                with eng.Fori(0, BLOCKS - 1) as i:
                    step(i, True)
                step(BLOCKS - 1, False)

            def scalar(act):
                act.wait_ge(s.raw, was.raw + 32)
                for m in range(2):
                    act.activation(tern[:, m, :], raw_m[:, m, :], ACT.Abs, accum_out=size_sum[:, m:m + 1]).then_inc(s.size, 1)
                for i in range(BLOCKS):
                    quant.scalar(act, i)
                for q in range(4):
                    act.wait_ge(s.w_tp, was.w_tp + q + 1)
                    to = up_w[:, q, :] if q < 2 else flat(down_w[:, q % 2 * IC // 2:(q % 2 + 1) * IC // 2, :])
                    act.activation(to, bank[4 + q][:, :].bitcast(BF16), ACT.Copy).then_inc(s.w, 1)
                for T in range(2):
                    scalar_gelu(act, T, T)

                def step(i, more):
                    for k in range(BT):
                        T = i * BT + k
                        scalar_back(act, T, k)
                        if k + 2 < BT or more:
                            scalar_gelu(act, T + 2, k)
                over_blocks(act, step)

            def vector(dve):
                dve.wait_ge(*before)
                norm.vector_stats(dve)
                dve.wait_ge(s.total, was.total + 1)
                link = linker(dve, s.chain, was.chain)
                link(dve.tensor_scalar(mean, bank[0][:, 0:2], 1.0 / (I * D), QUANT_EPS, ALU.mult, ALU.max))
                link(dve.reciprocal(per_mean, mean))
                link(dve.tensor_scalar(out_factor, mean[:, DOWN:DOWN + 1], gates[:, 7:8], None, ALU.mult))
                for m in range(2):
                    w = raw_m[:, m, :]
                    link(dve.tensor_scalar(w, w, per_mean[:, m:m + 1], MAGIC, ALU.mult, ALU.add))
                    link(dve.tensor_scalar(tern[:, m, :], w, MAGIC, -1.0, ALU.subtract, ALU.max))
                    dve.tensor_scalar(tern[:, m, :], tern[:, m, :], 1.0, None, ALU.min).then_inc(s.tern, 1)
                for i in range(BLOCKS):
                    norm.vector_norm(dve, i, through[i % 2])
                    quant.vector(dve, norm, i, through[i % 2])
                dve.wait_ge(quant.chain, 2 * 2 * BLOCKS)
                link(dve.tensor_scalar(gelu_scale, quant.step, mean[:, UP:UP + 1], None, ALU.mult))
                vector_front(dve, 0, 0)

                def step(i, more):
                    for k in range(BT):
                        T = i * BT + k
                        if k + 1 < BT or more:
                            vector_front(dve, T + 1, k + 1)
                        vector_back(dve, T, k)
                over_blocks(dve, step)
                dve.wait_ge(s.acc, was.acc + TILES)
                dve.sem_inc(done, TILES)

            def tensor(pe):
                hold(pe, s.size, was.size + 2)
                pe.matmul(bank[0][:, 0:2], ones[:, :], size_sum, start=True, stop=True).then_inc(s.total, 1)
                for i in range(BLOCKS):
                    quant.tensor(pe, i)
                pe.wait_ge(quant.turned, (quant.first + BLOCKS) * DC)
                for q in range(4):
                    m, half = divmod(q, 2)
                    pe.wait_ge(s.tern, was.tern + m + 1)
                    for j in range(IC):
                        at = j * D + half * P if m == UP else (j % 2) * I + (half * IC // 2 + j // 2) * P
                        tp = pe.transpose(bank[4 + q][:, :].bitcast(BF16)[:, j * P:(j + 1) * P], tern[:, m, at:at + P], identb[:, :])
                    tp.then_inc(s.w_tp, 1)
                pe.wait_ge(s.w, was.w + 4)
                pe.wait_ge(s.chain, was.chain + 8)
                for T in range(2):
                    tensor_up(pe, T, T)

                def step(i, more):
                    for k in range(BT):
                        T = i * BT + k
                        tensor_turn(pe, T, k)
                        if k + 2 < BT or more:
                            tensor_up(pe, T + 2, k)
                        tensor_down(pe, T, k)
                over_blocks(pe, step)

            return sync, gpsimd, scalar, vector, tensor

        done = sem("done")
        makers = [layer0_attention, layer0_experts, layer1_attention, layer1_experts,
                  layer2_attention, layer2_experts, layer3_attention, layer3_experts]
        sublayers = [make((done, j * TILES), done) for j, make in enumerate(makers)]

        block = ctx.enter_context(nc.Block())

        @block.sync
        def _(sp):
            setup_sync(sp)
            for sublayer in sublayers:
                sublayer[SYNC](sp)

        @block.gpsimd
        def _(pool):
            setup_gpsimd(pool)
            for sublayer in sublayers:
                sublayer[GPSIMD](pool)

        @block.scalar
        def _(act):
            setup_scalar(act)
            for sublayer in sublayers:
                sublayer[SCALAR](act)

        @block.vector
        def _(dve):
            setup_vector(dve)
            for sublayer in sublayers:
                sublayer[VECTOR](dve)

        @block.tensor
        def _(pe):
            setup_tensor(pe)
            for sublayer in sublayers:
                sublayer[TENSOR](pe)


INPUTS = ("x", "ctx_2048", "mask_BxS2_bk0", "g_xattn", "g_ffn",
          "L0_ffn_gate_w", "L0_ffn_w1", "L0_ffn_w3", "L0_ffn_w2", "L0_ffn_sw1", "L0_ffn_sw3", "L0_ffn_sw2",
          "L1_xattn_Wq", "L1_xattn_Wg", "L1_xattn_bg", "L1_xattn_Wkv", "L1_xattn_Wo",
          "L1_ffn_router_w", "L1_ffn_gate_w", "L1_ffn_up_w", "L1_ffn_down_w",
          "L2_xattn_Wq", "L2_xattn_Wk", "L2_xattn_Wv", "L2_xattn_Wfc", "L2_xattn_bfc",
          "L2_ffn_W1", "L2_ffn_Wg", "L2_ffn_W2", "L2_ffn_Ws1", "L2_ffn_Wsg", "L2_ffn_Ws2",
          "L2_ffn_gate_w", "L2_ffn_gate_b", "L2_ffn_biases",
          "L3_xattn_decay", "L3_xattn_W_in", "L3_xattn_b_in", "L3_xattn_W_out", "L3_xattn_b_out",
          "L3_xattn_gamma", "L3_xattn_beta", "L3_ffn_w1", "L3_ffn_w2")


def kernel(**inputs):
    import concourse.bacc as bacc
    from concourse.bass_utils import run_bass_kernel_spmd

    nc = bacc.Bacc("TRN2", target_bir_lowering=False, num_devices=1)
    arrays, io = {}, {}
    for name in INPUTS:
        a = np.ascontiguousarray(inputs[name])
        if a.ndim == 0:
            a = a.reshape(1)
        arrays["in_" + name] = a
        io[name] = nc.dram_tensor("in_" + name, a.shape, mybir.dt.from_np(a.dtype), kind="ExternalInput").ap()
    io["out"] = nc.dram_tensor("out", (BATCH, SEQ, D), F32, kind="ExternalOutput").ap()
    build_program(nc, io)
    return run_bass_kernel_spmd(nc, [arrays], core_ids=[0]).results[0]["out"]
```

```python
from contextlib import ExitStack

import numpy as np

import concourse.bass as bass
from concourse import mybir

ACT = mybir.ActivationFunctionType
ALU = mybir.AluOpType
AX = mybir.AxisListType
F32 = mybir.dt.float32
F32R = mybir.dt.float32r
BF16 = mybir.dt.bfloat16
U8 = mybir.dt.uint8
ds = bass.ds

P = 128
D = 256
DC = D // P
BATCH, SEQ = 32, 64
TOK = BATCH * SEQ
TILES = TOK // P
BT = 4
BLK = BT * P
BLOCKS = TILES // BT
LN_EPS = 1e-5
QUANT_EPS = 1e-5
MAGIC = 1.5 * 2.0 ** 23
L0_I = 176
RAW = 4096
SPLIT = 2 * DC * 3 * P + 3 * D
SYNC, GPSIMD, SCALAR, VECTOR, TENSOR = range(5)
WORK = 19600
L1_RAW = 14000
L2_EXPERTS = 3400
L3_ATTENTION = 7200


class Names:
    pass


def build_program(nc, io):
    ctx = ExitStack()
    with ctx:
        def sb(name, shape, dt=F32):
            return ctx.enter_context(nc.sbuf_tensor(name, shape, dt))

        def sem(name):
            return ctx.enter_context(nc.semaphore(name))

        def sems(prefix, names):
            return [sem(prefix + "_" + name) for name in names.split()]

        X = sb("resid", [P, TILES, D])
        ident = sb("ident", [P, P])
        identb = sb("identb", [P, P], BF16)
        ones = sb("ones", [P, P])
        neg_half = sb("neg_half", [P, TILES])
        magic = sb("magic", [P, 1])
        gates = sb("gates", [P, 8])
        xn = sb("xn", [P, BT, D])
        ln_stat = sb("ln_stat", [P, TILES, 6])
        ln_mv = sb("ln_mv", [P, TILES, 2])
        ln_ve = sb("ln_ve", [P, TILES])
        ln_rstd = sb("ln_rstd", [P, TILES])
        xhi = sb("xhi", [P, DC, TOK], F32R)
        xlo = sb("xlo", [P, DC, TOK], F32R)
        ctx_in = sb("ctx_in", [P, BT, D])
        ctx_sb = sb("ctx_sb", [P, BT, D])
        work = sb("work", [P, WORK])
        raw = sb("raw", [P, RAW])
        whi = sb("whi", [P, 2, SPLIT], F32R)
        wlo = sb("wlo", [P, 2, SPLIT], F32R)
        ahi = sb("ahi", [P, 2, BLK], F32R)
        alo = sb("alo", [P, 2, BLK], F32R)
        route_hi = sb("route_hi", [P, DC, P], F32R)
        route_lo = sb("route_lo", [P, DC, P], F32R)
        bank = [ctx.enter_context(nc.psum_tensor(f"bank{i}", [P, 512], F32)) for i in range(8)]

        class Layout:

            def __init__(self):
                self.at = 0

            def __call__(self, *shape, dt=F32):
                n = int(np.prod(shape))
                n32 = n if dt == F32 else (n + 1) // 2
                v = work[:, self.at:self.at + n32]
                self.at += n32
                assert self.at <= WORK, self.at
                if dt != F32:
                    v = v.bitcast(dt)
                if len(shape) == 2:
                    v = v.rearrange("p (a b) -> p a b", a=shape[0])
                if len(shape) == 3:
                    v = v.rearrange("p (a b c) -> p a b c", a=shape[0], b=shape[1])
                if len(shape) == 4:
                    v = v.rearrange("p (a b c d) -> p a b c d", a=shape[0], b=shape[1], c=shape[2])
                return v

        def flat(ap):
            return ap.rearrange("p a b -> p (a b)")

        def x_tile(t):
            return flat(X[:, ds(t, 1), :])

        def block_of(dram, i):
            v = dram.rearrange("b s d -> (b s) d").rearrange("(i k p) d -> i p k d", k=BT, p=P)
            return v[ds(i, 1)].rearrange("o p k d -> p (o k) d")

        passed = sem("passed")

        def hold(eng, s, value):
            eng.wait_ge(s, value)
            eng.sem_inc(passed, 1)

        def linker(eng, s, base=0):
            count = [0]

            def link(ins):
                ins.then_inc(s, 1)
                count[0] += 1
                eng.wait_ge(s, base + count[0])
            link.count = count
            return link

        weight = Names()
        weight.loaded, weight.turned, weight.ready = sems("weight", "loaded turned ready")
        weight_counts = [(0, 0, 0)]

        def count_weights(loaded, turned, ready):
            was = Names()
            was.loaded, was.turned, was.ready = weight_counts[-1]
            weight_counts.append((was.loaded + loaded, was.turned + turned, was.ready + ready))
            return was

        x_loaded, small_loaded = sems("x_loaded", "0 1 2 3"), sem("small_loaded")
        mask_in = sb("mask_in", [P, TILES, P], U8)
        const_set, gates_set, ident_set = sem("const_set"), sem("gates_set"), sem("ident_set")

        def setup_sync(sp):
            sp.dma_start(gates[:, 0:4], io["g_xattn"].partition_broadcast(P)).then_inc(small_loaded, 16)
            sp.dma_start(gates[:, 4:8], io["g_ffn"].partition_broadcast(P)).then_inc(small_loaded, 16)
            sp.dma_start(mask_in[:, :, :].rearrange("p t k -> p (t k)"),
                         io["mask_BxS2_bk0"].rearrange("b s -> (b s)").partition_broadcast(P)).then_inc(small_loaded, 16)
            for i in range(BLOCKS):
                sp.dma_start(X[:, BT * i:BT * i + BT, :], block_of(io["x"], i)).then_inc(x_loaded[i], 16)

        def setup_gpsimd(pool):
            pool.memset(ident[:, :], 0.0).then_inc(const_set, 1)
            pool.memset(ones[:, :], 1.0).then_inc(const_set, 1)
            pool.memset(neg_half[:, :], -0.5).then_inc(const_set, 1)
            pool.memset(magic[:, :], MAGIC).then_inc(const_set, 1)
            pool.wait_ge(const_set, 4)
            pool.affine_select(out=ident[:, :], in_=ident[:, :], compare_op=ALU.not_equal, fill=1.0, base=0,
                               pattern=[[-1, P]], channel_multiplier=1).then_inc(ident_set, 1)
            pool.wait_ge(ident_set, 1)
            pool.tensor_copy(identb[:, :], ident[:, :]).then_inc(ident_set, 1)

        def setup_scalar(act):
            act.wait_ge(small_loaded, 48)
            act.activation(gates[:, :], gates[:, :], ACT.Tanh).then_inc(gates_set, 1)

        def setup_vector(dve):
            dve.wait_ge(gates_set, 1)

        def setup_tensor(pe):
            pe.wait_ge(ident_set, 2)

        norm_sems = sems("norm", "stat rstd xn tp hi lo")

        def next_stat(dve, t):
            dve.bn_stats(flat(ln_stat[:, ds(t, 1), :]), x_tile(t)).then_inc(norm_sems[0], 1)

        def make_norm(sublayer, split=None, turn=0):
            n = Names()
            n.stat, n.rstd, n.xn, n.tp, n.hi, n.lo = norm_sems
            n.first = (sublayer - (sublayer == 7)) * BLOCKS
            n.first_tp = turn * BLOCKS
            n.first_lo = (split or 0) * BLOCKS

            def vector_stats(dve):
                for t in range(TILES):
                    next_stat(dve, t)

            def vector_means(dve):
                dve.wait_ge(n.stat, sublayer * 2 * TILES + TILES)
                for t in range(TILES):
                    dve.bn_aggr(ln_mv[:, t, :], ln_stat[:, t, :]).then_inc(n.stat, 1)

            def gpsimd_rstd(pool, i):
                tiles = slice(i * BT, (i + 1) * BT)
                pool.tensor_scalar(ln_ve[:, tiles], ln_mv[:, tiles, 1], LN_EPS, 1.0, ALU.add, ALU.mult).then_inc(n.rstd, 1)
                pool.wait_ge(n.rstd, sublayer * TILES + i * BT + 1)
                pool.tensor_tensor(ln_rstd[:, tiles], ln_ve[:, tiles], neg_half[:, tiles], ALU.pow).then_inc(n.rstd, BT - 1)

            def gpsimd_stats(pool, blocks=range(BLOCKS)):
                for i in blocks:
                    pool.wait_ge(n.stat, sublayer * 2 * TILES + TILES + (i + 1) * BT)
                    gpsimd_rstd(pool, i)

            def vector_tile(dve, t, k, into):
                there = sublayer * TILES + (t - k) + BT
                if isinstance(t, int):
                    dve.wait_ge(n.rstd, there)
                else:
                    hold(dve, n.rstd, there)
                dve.tensor_scalar(into, x_tile(t), flat(ln_mv[:, ds(t, 1), 0:1]), ln_rstd[:, ds(t, 1)],
                                  ALU.subtract, ALU.mult).then_inc(n.xn, 1)

            def vector_norm(dve, i, into=xn):
                for k in range(BT):
                    vector_tile(dve, i * BT + k, k, into[:, k, :])

            def vector_rest(dve, i, at=0):
                for c in range(DC):
                    dve.wait_ge(n.hi, (n.first_tp + i) * DC + c + 1)
                    dve.tensor_tensor(flat(xlo[:, c:c + 1, ds(i * BLK, BLK)]), bank[at + c][:, :],
                                      flat(xhi[:, c:c + 1, ds(i * BLK, BLK)]).bitcast(F32),
                                      ALU.subtract).then_inc(n.lo, 1)

            def tensor(pe, i, tiles=xn, at=0):
                for c in range(DC):
                    for k in range(BT):
                        if c == 0:
                            pe.wait_ge(n.xn, (n.first + i) * BT + k + 1)
                        tp = pe.transpose(bank[at + c][:, k * P:(k + 1) * P], tiles[:, k, c * P:(c + 1) * P], ident[:, :])
                    tp.then_inc(n.tp, 1)

            def scalar(act, i, at=0):
                for c in range(DC):
                    act.wait_ge(n.tp, (n.first_tp + i) * DC + c + 1)
                    act.activation(flat(xhi[:, c:c + 1, ds(i * BLK, BLK)]), bank[at + c][:, :], ACT.Copy).then_inc(n.hi, 1)

            n.stats_here = sublayer == 1
            n.all_there = (sublayer + 1) * TILES
            n.vector_stats, n.vector_means, n.gpsimd_stats, n.vector_tile = vector_stats, vector_means, gpsimd_stats, vector_tile
            n.gpsimd_rstd = gpsimd_rstd
            n.vector_norm, n.vector_rest, n.tensor, n.scalar = vector_norm, vector_rest, tensor, scalar
            return n

        scan = Names()
        scan.loaded, scan.masks, scan.keep, scan.chain = sems("scan", "loaded masks keep chain")
        scan.strip = sb("scan_strip", [P, 2 * BATCH - 2])
        scan.totals = sb("scan_totals", [1, BATCH])

        def make_scan():
            STEPS = int(np.log2(SEQ))
            lay = Layout()
            lay.at = L1_RAW + 11 * D
            decay, power, series, weigh = lay(1), lay(STEPS), lay(SEQ), lay(SEQ)
            row_weight, weight_sum = lay(1), lay(1)
            of_row = lay(SEQ)
            of_half = lay(2)

            def sync(sp):
                sp.dma_start(decay, io["L3_xattn_decay"].partition_broadcast(P)).then_inc(scan.loaded, 16)

            def gpsimd(pool):
                pool.memset(of_row, 0.0).then_inc(scan.masks, 1)
                for h in range(2):
                    pool.wait_ge(scan.masks, 1 + h)
                    pool.affine_select(out=of_row, in_=of_row, compare_op=ALU.not_equal, fill=1.0,
                                       base=1 - SEQ * (h + 1), pattern=[[1, SEQ]], channel_multiplier=1).then_inc(scan.masks, 1)

            def scalar(act):
                act.wait_ge(scan.loaded, 16)
                act.activation(decay, decay, ACT.Sigmoid).then_inc(scan.keep, 1)

            links = []

            def vector_powers(dve):
                dve.wait_ge(scan.keep, 1)
                dve.wait_ge(scan.masks, 3)
                link = linker(dve, scan.chain)
                links.append(link)
                link(dve.memset(scan.strip[:, :], 0.0))
                link(dve.memset(of_half, 0.0))
                link(dve.memset(of_half[0:SEQ, 0:1], 1.0))
                link(dve.memset(of_half[SEQ:P, 1:2], 1.0))
                link(dve.memset(series[:, 0:1], 1.0))
                link(dve.tensor_copy(power[:, 0:1], decay))
                for n in range(1, STEPS):
                    link(dve.tensor_tensor(power[:, n:n + 1], power[:, n - 1:n], power[:, n - 1:n], ALU.mult))

            def vector_series(dve):
                for n in range(STEPS):
                    m = 1 << n
                    links[0](dve.tensor_scalar(series[:, m:2 * m], series[:, 0:m], power[:, n:n + 1], series[:, m - 1:m], ALU.mult, ALU.add))

            def vector_weights(dve):
                link = links[0]
                link(dve.tensor_reduce(weight_sum, series, AX.X, ALU.add))
                link(dve.tensor_tensor(weigh, series, of_row, ALU.mult))
                link(dve.tensor_reduce(row_weight, weigh, AX.X, ALU.add))
                link(dve.tensor_scalar(scan.strip[:, BATCH - 2:BATCH], of_half, row_weight, 1.0 / SEQ, ALU.mult, ALU.mult))
                link(dve.tensor_scalar(scan.totals[:, :], ones[0:1, 0:BATCH], weight_sum[0:1], 1.0 / SEQ, ALU.mult, ALU.mult))
                scan.ready = link.count[0]

            scan.vector_steps = (vector_powers, vector_series, vector_weights)
            return sync, gpsimd, scalar

        scan_programs = make_scan()

        RING = 4
        ctx_here = sems("ctx_here", "0 1 2 3")
        RING_LOADS = 16 * TILES // RING

        def inside(t):
            return not isinstance(t, int) or 0 <= t < TILES

        def over_tiles(eng, step):
            for t in range(2):
                step(t, t)
            with eng.Fori(0, TILES // RING - 1) as i:
                for k in range(RING):
                    step(i * RING + 2 + k, (2 + k) % RING)
            for t in range(TILES - 2, TILES + 2):
                step(t, t % RING)

        def layer0_attention(before, done):
            lay = Layout()
            context = lay(TILES, D)
            same_batch = lay(P)
            mask = lay(TILES, P)
            mask_low = lay(TILES, P)
            seen = lay(TILES)
            inT = lay(2, 2 * DC, P)
            score, prob, probT = lay(2, P), lay(2, P), lay(2, P)
            neg_max, total, inv, scale = lay(2), lay(RING), lay(2), lay(2)
            assert lay.at <= L1_RAW, lay.at
            norm = make_norm(0)
            s = Names()
            (
                s.same, s.mask, s.ctx, s.here, s.in_ps, s.inT, s.score_ps, s.soft, s.exp, s.probT_ps, s.probT, s.sums, s.out
            ) = sems("a0", "same mask ctx here in_ps inT score_ps soft exp probT_ps probT sums out")
            SOFT = 3
            IN, SCORE, TURN, OUT = bank[0:2], bank[2:4], bank[4:6], bank[6:8]

            def sync(sp):
                for i in range(BLOCKS):
                    if i:
                        sp.wait_ge(s.ctx, 16 * i)
                    sp.dma_start(context[:, i * BT:(i + 1) * BT, :], block_of(io["ctx_2048"], i)).then_inc(s.ctx, 16)

            def gpsimd(pool):
                same3 = same_batch.rearrange("p (h j) -> p h j", h=2)
                pool.memset(same_batch, 1.0).then_inc(s.same, 1)
                pool.wait_ge(s.same, 1)
                pool.affine_select(out=same3, in_=same3, compare_op=ALU.is_ge, fill=0.0, base=0,
                                   pattern=[[-SEQ, 2], [0, SEQ]], channel_multiplier=1).then_inc(s.same, 1)
                pool.wait_ge(s.same, 2)
                pool.affine_select(out=same3, in_=same3, compare_op=ALU.is_ge, fill=0.0, base=SEQ - 1,
                                   pattern=[[SEQ, 2], [0, SEQ]], channel_multiplier=-1).then_inc(s.same, 1)
                norm.gpsimd_stats(pool, range(1))

                def here(i):
                    for k in range(RING):
                        t = i * RING + k
                        if k == 0:
                            hold(pool, s.ctx, i * 16 + 16)
                        if not isinstance(i, int) or i:
                            hold(pool, s.in_ps, t - RING + 1)
                        pool.tensor_copy(ctx_in[:, k, :], flat(context[:, ds(t, 1), :])).then_inc(s.here, 1)
                here(0)
                norm.gpsimd_stats(pool, range(1, BLOCKS))
                with pool.Fori(1, BLOCKS) as i:
                    here(i)
                pool.memset(raw[:, :], 0.0).then_inc(gated_sems[2], 1)

            def scalar_in(act, t, k):
                act.wait_ge(s.in_ps, t + 1)
                if not isinstance(t, int) or t >= 2:
                    act.wait_ge(s.score_ps, t - 1)
                act.activation(flat(inT[:, k % 2]), IN[k % 2][:, :], ACT.Copy).then_inc(s.inT, 1)

            def scalar(act):
                scalar_in(act, 0, 0)

                def step(t, k):
                    j = k % 2
                    if inside(t - 2):
                        act.wait_ge(s.probT_ps, t - 1)
                        act.activation(probT[:, j, :], TURN[j][:, 0:P], ACT.Copy).then_inc(s.probT, 1)
                    if inside(t + 1):
                        scalar_in(act, t + 1, k + 1)
                    if inside(t):
                        act.wait_ge(s.soft, t * SOFT + SOFT)
                        act.activation(prob[:, j, :], score[:, j, :], ACT.Exp, bias=neg_max[:, j:j + 1],
                                       accum_out=total[:, k:k + 1]).then_inc(s.exp, 1)
                over_tiles(act, step)

            def vector_norm(dve, t, k):
                if not isinstance(t, int) or t >= RING:
                    hold(dve, s.in_ps, t - RING + 1)
                norm.vector_tile(dve, t, k, xn[:, k, :])

            def vector(dve):
                for i in range(BLOCKS):
                    dve.wait_ge(x_loaded[i], 16)
                    for t in range(i * BT, (i + 1) * BT):
                        next_stat(dve, t)
                    if i == 0:
                        dve.wait_ge(small_loaded, 48)
                        dve.wait_ge(s.same, 3)
                        dve.tensor_tensor(mask, mask_in[:, :, :], same_batch.unsqueeze(1).to_broadcast([P, TILES, P]), ALU.mult).then_inc(s.mask, 1)
                    elif i == 1:
                        dve.wait_ge(s.mask, 1)
                        dve.tensor_scalar(flat(mask_low), flat(mask), 1e30, -1e30, ALU.mult, ALU.add).then_inc(s.mask, 1)
                norm.vector_means(dve)
                for t in range(2):
                    vector_norm(dve, t, t)
                dve.tensor_reduce(seen, mask, AX.X, ALU.max).then_inc(s.mask, 1)
                dve.wait_ge(s.mask, 3)

                def step(t, k):
                    j = k % 2
                    k2 = (k + 2) % RING
                    if inside(t + 2):
                        vector_norm(dve, t + 2, k2)
                    if inside(t):
                        dve.wait_ge(s.score_ps, t + 1)
                        if not isinstance(t, int) or t >= 2:
                            hold(dve, s.exp, t - 1)
                        dve.scalar_tensor_tensor(score[:, j, :], SCORE[j][:, 0:P], D ** -0.5, flat(mask[:, ds(t, 1), :]), ALU.mult, ALU.mult).then_inc(s.soft, 1)
                    if inside(t - 2):
                        hold(dve, s.exp, t - 1)
                        dve.reciprocal(inv[:, j:j + 1], total[:, k2:k2 + 1]).then_inc(s.sums, 1)
                    if inside(t):
                        hold(dve, s.soft, t * SOFT + 1)
                        dve.tensor_tensor(score[:, j, :], score[:, j, :], flat(mask_low[:, ds(t, 1), :]), ALU.add).then_inc(s.soft, 1)
                    if inside(t - 2):
                        hold(dve, s.sums, t * 2 - 3)
                        dve.scalar_tensor_tensor(scale[:, j:j + 1], inv[:, j:j + 1], gates[:, 0:1], seen[:, ds(t - 2, 1)], ALU.mult, ALU.mult).then_inc(s.sums, 1)
                    if inside(t):
                        hold(dve, s.soft, t * SOFT + 2)
                        dve.tensor_reduce(neg_max[:, j:j + 1], score[:, j, :], AX.X, ALU.max, negate=True).then_inc(s.soft, 1)
                    if inside(t - 2):
                        dve.wait_ge(s.out, t - 1)
                        hold(dve, s.sums, t * 2 - 2)
                        dve.scalar_tensor_tensor(x_tile(t - 2), OUT[j][:, 0:D], scale[:, j:j + 1], x_tile(t - 2), ALU.mult, ALU.add).then_inc(done, 1)
                over_tiles(dve, step)

            def tensor_in(pe, t, k):
                hold(pe, s.here, t + 1)
                hold(pe, norm.xn, norm.first * BT + t + 1)
                if not isinstance(t, int) or t >= 2:
                    hold(pe, s.inT, t - 1)
                for c in range(DC):
                    pe.transpose(IN[k % 2][:, c * P:(c + 1) * P], xn[:, k, c * P:(c + 1) * P], ident[:, :])
                for c in range(DC):
                    tp = pe.transpose(IN[k % 2][:, D + c * P:D + (c + 1) * P], ctx_in[:, k, c * P:(c + 1) * P], ident[:, :])
                tp.then_inc(s.in_ps, 1)

            def tensor(pe):
                tensor_in(pe, 0, 0)

                def step(t, k):
                    j = k % 2
                    if inside(t + 1):
                        tensor_in(pe, t + 1, (k + 1) % RING)
                    if inside(t):
                        hold(pe, s.inT, t + 1)
                        if not isinstance(t, int) or t >= 2:
                            hold(pe, s.soft, t * SOFT - 2 * SOFT + 1)
                        for c in range(DC):
                            mm = pe.matmul(SCORE[j][:, 0:P], inT[:, j, c, :], inT[:, j, DC + c, :], start=c == 0, stop=c == DC - 1)
                        mm.then_inc(s.score_ps, 1)
                    if inside(t - 1):
                        hold(pe, s.exp, t)
                        pe.transpose(TURN[1 - j][:, 0:P], prob[:, 1 - j, :], ident[:, :]).then_inc(s.probT_ps, 1)
                    if inside(t - 2):
                        hold(pe, s.probT, t - 1)
                        if not inside(t):
                            hold(pe, done, t - 3)
                        pe.matmul(OUT[j][:, 0:D], probT[:, j, :], flat(context[:, ds(t - 2, 1), :]), start=True, stop=True).then_inc(s.out, 1)
                over_tiles(pe, step)

            return sync, gpsimd, scalar, vector, tensor

        route_sems = sems("route", "loaded zeroed w_tp w logits_ps logitsT turned_ps kept chain soft exp")
        route_counts = [(0, 0)]

        def make_router(name, use, lay, scratch, lead, experts, top, gate, w_rows, dram_w, dram_b=None, dram_bias=None):
            r = Names()
            r.loaded, r.zeroed, r.w_tp, r.w, r.logits_ps, r.logitsT, r.turned_ps, r.kept, r.chain, r.soft, r.exp = route_sems
            first_block = use * BLOCKS
            E = experts
            w_in = sb(f"{name}_win", [P, D] if w_rows else [P, DC, E])
            w_hi, w_lo = route_hi, route_lo
            logitsT = lay(BLK)
            r.logits, prob, key = lay(TILES, E), lay(TILES, E), lay(TILES, E)
            small, inv = lay(TILES), lay(TILES)
            pairs = TILES * E * E
            beats, ties = [v[:, 0:pairs].rearrange("p (t a b) -> p t a b", t=TILES, a=E) for v in scratch]
            earlier = lay(E, E)
            rank = lay(TILES, E)
            r.shares = lay(lead + E, TILES)
            bias_in = sb(f"{name}_bias", [P, 2, E])
            extra = (dram_b is not None) + (dram_bias is not None)
            loaded0, chain0 = route_counts[-1]
            loads = loaded0 + 16 * ((1 if w_rows else DC) + extra)
            chained = 15 + extra + (lead > 0)
            route_counts.append((loads, chain0 + chained))

            def sync(sp):
                if w_rows:
                    sp.dma_start(w_in[0:E, :], dram_w).then_inc(r.loaded, 16)
                else:
                    for c in range(DC):
                        sp.dma_start(w_in[:, c, :], dram_w[c * P:(c + 1) * P, :]).then_inc(r.loaded, 16)
                if dram_b is not None:
                    sp.dma_start(bias_in[:, 0, :], dram_b.partition_broadcast(P)).then_inc(r.loaded, 16)
                if dram_bias is not None:
                    sp.dma_start(bias_in[:, 1, :], dram_bias.partition_broadcast(P)).then_inc(r.loaded, 16)

            def gpsimd(pool):
                pool.memset(earlier, 1.0).then_inc(r.zeroed, 1)
                pool.wait_ge(r.zeroed, use * 2 + 1)
                pool.affine_select(out=earlier, in_=earlier, compare_op=ALU.is_gt, fill=0.0, base=0,
                                   pattern=[[1, E], [-1, E]], channel_multiplier=0).then_inc(r.zeroed, 1)

            def vector_weights(dve):
                dve.memset(w_hi[:, :, :].bitcast(F32), 0.0).then_inc(r.w, 1)
                dve.memset(w_lo[:, :, :].bitcast(F32), 0.0).then_inc(r.w, 1)
                dve.wait_ge(r.loaded, loads)
                dve.wait_ge(r.w, use * 4 + 2)
                if w_rows:
                    dve.wait_ge(r.w_tp, use + 1)
                    src = bank[4][:, 0:DC * E].rearrange("p (c e) -> p c e", c=DC)
                else:
                    src = w_in[:, :, :]
                dve.tensor_copy(w_hi[:, :, 0:E], src).then_inc(r.w, 1)
                dve.wait_ge(r.w, use * 4 + 3)
                dve.tensor_tensor(w_lo[:, :, 0:E], src, w_hi[:, :, 0:E].bitcast(F32), ALU.subtract).then_inc(r.w, 1)

            def tensor_weights(pe):
                if w_rows:
                    pe.wait_ge(r.loaded, loads)
                    for c in range(DC):
                        tp = pe.transpose(bank[4][:, c * E:(c + 1) * E], w_in[0:E, c * P:(c + 1) * P], ident[0:E, 0:E])
                    tp.then_inc(r.w_tp, 1)
                pe.wait_ge(r.w, use * 4 + 4)

            def tensor_logits(pe, norm, i):
                pe.wait_ge(norm.lo, (norm.first_lo + i) * DC + DC)
                n = 0
                for c in range(DC):
                    for w, x in ((w_hi, xhi), (w_hi, xlo), (w_lo, xhi)):
                        mm = pe.matmul(bank[4][:, :], w[:, c, :], flat(x[:, c:c + 1, ds(i * BLK, BLK)]), start=n == 0, stop=n == 5)
                        n += 1
                mm.then_inc(r.logits_ps, 1)

            def tensor_turn(pe, i):
                hold(pe, r.logitsT, first_block + i + 1)
                for k in range(BT):
                    tp = pe.transpose(bank[5][:, k * E:(k + 1) * E], logitsT[0:E, k * P:(k + 1) * P], ident[0:E, 0:E])
                tp.then_inc(r.turned_ps, 1)

            def scalar_logits(act, i):
                act.wait_ge(r.logits_ps, first_block + i + 1)
                act.activation(logitsT[0:E, :], bank[4][0:E, :], ACT.Copy).then_inc(r.logitsT, 1)

            def scalar_keep(act, i):
                act.wait_ge(r.turned_ps, first_block + i + 1)
                act.activation(r.logits[:, ds(i * BT, BT), :], bank[5][:, 0:BT * E].rearrange("p (k e) -> p k e", k=BT),
                               ACT.Copy).then_inc(r.kept, 1)
            r.all_kept = first_block + BLOCKS

            def scalar_last(act):
                act.wait_ge(r.soft, use + 1)
                act.activation(prob, r.logits, ACT.Exp).then_inc(r.exp, 1)

            def over(v):
                return v.unsqueeze(2).to_broadcast([P, TILES, E])

            links = []

            def vector_lead(dve):
                links.append(linker(dve, r.chain, chain0))
                if lead:
                    links[0](dve.tensor_scalar(flat(r.shares[:, 0:lead, :]), ones[:, 0:lead * TILES], gate, None, ALU.mult))

            def vector_soft(dve):
                dve.wait_ge(r.kept, r.all_kept)
                dve.wait_ge(r.zeroed, use * 2 + 2)
                link = links[0]
                if dram_b is not None:
                    link(dve.tensor_tensor(r.logits, r.logits, bias_in[:, 0:1, :].to_broadcast([P, TILES, E]), ALU.add))
                link(dve.tensor_reduce(small, r.logits, AX.X, ALU.max))
                dve.tensor_tensor(r.logits, r.logits, over(small), ALU.subtract).then_inc(r.soft, 1)

            rated = prob if dram_bias is None else key

            def vector_prob(dve):
                link = links[0]
                dve.wait_ge(r.exp, use + 1)
                link(dve.tensor_reduce(small, prob, AX.X, ALU.add))
                link(dve.reciprocal(inv, small))
                link(dve.tensor_tensor(prob, prob, over(inv), ALU.mult))
                if dram_bias is not None:
                    link(dve.tensor_tensor(key, prob, bias_in[:, 1:2, :].to_broadcast([P, TILES, E]), ALU.add))

            other = rated.unsqueeze(2).to_broadcast([P, TILES, E, E])
            own = rated.unsqueeze(3).to_broadcast([P, TILES, E, E])

            def vector_compare(dve):
                links[0](dve.tensor_tensor(beats, other, own, ALU.is_gt))
                links[0](dve.tensor_tensor(ties, other, own, ALU.is_equal))

            def vector_ties(dve):
                links[0](dve.tensor_tensor(ties, ties, earlier.unsqueeze(1).to_broadcast([P, TILES, E, E]), ALU.mult))
                links[0](dve.tensor_tensor(beats, beats, ties, ALU.add))

            def vector_rank(dve):
                links[0](dve.tensor_reduce(rank, beats, AX.X, ALU.add))
                links[0](dve.tensor_scalar(rank, rank, float(top), None, ALU.is_lt))
                links[0](dve.tensor_tensor(prob, prob, rank, ALU.mult))

            def vector_shares(dve):
                link = links[0]
                link(dve.tensor_reduce(small, prob, AX.X, ALU.add))
                link(dve.reciprocal(inv, small))
                link(dve.tensor_tensor(prob, prob, over(inv), ALU.mult))
                dve.tensor_scalar(r.shares[:, lead:lead + E, :].rearrange("p e t -> p t e"), prob, gate, None, ALU.mult).then_inc(r.chain, 1)
                dve.wait_ge(r.chain, chain0 + chained)
                assert link.count[0] + 1 == chained, link.count

            r.vector_lead = vector_lead
            r.vector_steps = (vector_soft, vector_prob, vector_compare, vector_ties, vector_rank, vector_shares)

            r.sync, r.gpsimd, r.vector_weights, r.tensor_weights = sync, gpsimd, vector_weights, tensor_weights
            r.tensor_logits, r.tensor_turn, r.scalar_logits, r.scalar_keep = tensor_logits, tensor_turn, scalar_logits, scalar_keep
            r.scalar_last = scalar_last
            return r

        def make_entry(norm, router, quant=None):
            n = Names()
            through = (xn, ctx_sb)

            def vector(dve):
                if norm.stats_here:
                    norm.vector_stats(dve)
                norm.vector_means(dve)
                for i in range(BLOCKS + 1):
                    if i < BLOCKS:
                        norm.vector_norm(dve, i, through[i % 2])
                        if quant:
                            quant.vector(dve, norm, i, through[i % 2])
                    if i:
                        norm.vector_rest(dve, i - 1, (i - 1) % 2 * DC)

            def gpsimd(pool):
                norm.gpsimd_stats(pool)

            def scalar(act):
                for i in range(BLOCKS + 2):
                    if i < BLOCKS:
                        norm.scalar(act, i, i % 2 * DC)
                        if quant:
                            quant.scalar(act, i)
                    if i >= 2:
                        router.scalar_keep(act, i - 2)
                    if 1 <= i <= BLOCKS:
                        router.scalar_logits(act, i - 1)

            def tensor(pe):
                for i in range(BLOCKS + 2):
                    if i < BLOCKS:
                        norm.tensor(pe, i, through[i % 2], i % 2 * DC)
                        if quant:
                            quant.tensor(pe, i)
                    if i >= 2:
                        router.tensor_turn(pe, i - 2)
                    if 1 <= i <= BLOCKS:
                        router.tensor_logits(pe, norm, i - 1)

            n.vector, n.gpsimd, n.scalar, n.tensor = vector, gpsimd, scalar, tensor
            return n

        gated_sems = sems("gated", "raw raw_free zeroed whi wlo w_free up1 up2 silu hid ahi alo down shares acc")
        gated_counts = [(0, 0, 0, 0, 0)]

        def gated_experts(name, sublayer, split, turn, gate, before, done, experts, top, router_args, chunks, outputs, groups, load, up_width, down_chunks, more_steps=()):
            lay = Layout()
            hidden = lay(4, BLK)
            silu, act32 = hidden[:, 0:2, :], hidden[:, 2:4, :]
            per = 1 + max(e for pieces in outputs for e, _, _ in pieces)
            router = make_router(name, split, lay, (flat(xn), flat(ctx_sb)), per, experts, top, gate, *router_args)
            norm = make_norm(sublayer, split=split, turn=turn)
            entry = make_entry(norm, router)
            steps = router.vector_steps + more_steps
            shares_now = lay(2 * per, TILES)
            s = Names()
            (
                s.raw, s.raw_free, s.zeroed, s.whi, s.wlo, s.w_free, s.up1, s.up2, s.silu, s.hid, s.ahi, s.alo,
                s.down, s.shares, s.acc
            ) = gated_sems
            NC = len(chunks)
            UNITS = BLOCKS * NC
            ACCS = BLOCKS * per
            NL = load.count
            width = up_width
            used = 2 * DC * width + down_chunks * D
            looped = (groups - 2) // 2 * 2
            was = Names()
            was.raw, was.groups, was.units, was.shares, was.accs = gated_counts[-1]
            gated_counts.append((was.raw + groups * 16 * NL, was.groups + groups, was.units + groups * UNITS,
                                 was.shares + groups, was.accs + groups * ACCS))

            def up_w(w, slot, mat, c, q):
                at = (mat * DC + c) * width + chunks[q][0]
                return w[:, slot, at:at + chunks[q][1]]

            def down_w(w, slot, q, p0, n):
                at = 2 * DC * width + q * D
                return w[p0:p0 + n, slot, at:at + D]

            raw_up = raw[:, 0:2 * DC * width].rearrange("p (m c w) -> p m c w", m=2, c=DC)
            raw_down = raw[:, 2 * DC * width:used].rearrange("p (q d) -> p q d", q=down_chunks)

            raw_ready = (s.zeroed, 1) if was.groups == 0 else (weight.turned, weight_counts[-1][1])

            def sync(sp):
                router.sync(sp)
                sp.wait_ge(*raw_ready)

                def group(n):
                    sp.wait_ge(s.raw_free, was.groups + n + 1)
                    load(sp, n, raw_up, raw_down, s.raw)
                group(0)
                with sp.Fori(0, looped) as i:
                    group(i + 1)
                for n in range(1 + looped, groups):
                    group(n)

            def gpsimd(pool):
                if was.groups == 0:
                    pool.sem_inc(s.raw_free, 1)
                pool.wait_ge(*before)
                router.gpsimd(pool)
                entry.gpsimd(pool)

                def split_low(n, slot):
                    hold(pool, s.whi, was.groups + n + 1)
                    pool.tensor_tensor(wlo[:, slot, 0:used], raw[:, 0:used], whi[:, slot, 0:used].bitcast(F32),
                                       ALU.subtract).then_inc(s.wlo, 1)
                    hold(pool, s.wlo, was.groups + n + 1)
                    pool.sem_inc(s.raw_free, 1)

                with pool.Fori(0, groups // 2) as i:
                    for slot in range(2):
                        split_low(2 * i + slot, slot)
                if groups % 2:
                    split_low(groups - 1, 0)

            def split_high(act, n, slot):
                act.wait_ge(s.raw, was.raw + (n + 1) * 16 * NL)
                act.wait_ge(s.w_free, was.groups + n + 1)
                act.activation(whi[:, slot, 0:used], raw[:, 0:used], ACT.Copy).then_inc(s.whi, 1)

            def over_groups(eng, step):
                with eng.Fori(0, looped // 2) as i:
                    for j in range(2):
                        step(2 * i + 1 + j, 1 - j, True)
                for n in range(1 + looped, groups):
                    step(n, n % 2, n + 1 < groups)

            def scalar_group(act, n, slot, more, routing=False):
                for u in range(UNITS):
                    U = was.units + n * UNITS + u
                    m = chunks[u % NC][1]
                    act.wait_ge(s.up1, U + 1)
                    act.activation(silu[0:m, u % 2, :], bank[u % 2][0:m, :], ACT.Silu).then_inc(s.silu, 1)
                    act.wait_ge(s.hid, U + 3)
                    act.wait_ge(s.down, U + 1)
                    act.activation(ahi[0:m, u % 2, :], act32[0:m, u % 2, :], ACT.Copy).then_inc(s.ahi, 1)
                    if u == 1 and routing:
                        router.scalar_last(act)
                    if u == NC and more:
                        split_high(act, n + 1, 1 - slot)

            def scalar(act):
                split_high(act, 0, 0)
                entry.scalar(act)
                scalar_group(act, 0, 0, True, routing=True)
                over_groups(act, lambda n, slot, more: scalar_group(act, n, slot, more))

            def vector_group(dve, n, slot, routing=False):
                dve.wait_ge(s.acc, was.accs + n * ACCS + 2)
                dve.tensor_copy(shares_now[:, slot * per:(slot + 1) * per, :], router.shares[:, ds(n * per, per), :]).then_inc(s.shares, 1)
                hold(dve, s.shares, was.shares + n + 1)
                for u in range(UNITS):
                    U = was.units + n * UNITS + u
                    b, q = divmod(u, NC)
                    m = chunks[q][1]
                    dve.wait_ge(s.silu, U + 1)
                    dve.wait_ge(s.up2, U + 1)
                    dve.tensor_tensor(act32[0:m, u % 2, :], silu[0:m, u % 2, :], bank[2 + u % 2][0:m, :], ALU.mult).then_inc(s.hid, 1)
                    dve.wait_ge(s.ahi, U + 1)
                    dve.tensor_tensor(alo[0:m, u % 2, :], act32[0:m, u % 2, :], ahi[0:m, u % 2, :].bitcast(F32),
                                      ALU.subtract).then_inc(s.alo, 1)
                    if u:
                        add_outputs(dve, n, slot, u - 1)
                    if routing and u < len(steps):
                        steps[u](dve)
                add_outputs(dve, n, slot, UNITS - 1)

            last_chunk = {e: max(q for q in range(NC) for x, _, _ in outputs[q] if x == e) for e in range(per)}

            def add_outputs(dve, n, slot, u):
                b, q = divmod(u, NC)
                for e in range(per):
                    if last_chunk[e] == q:
                        add_output(dve, n, slot, b, e, was.units + n * UNITS + u)

            def add_output(dve, n, slot, b, e, U):
                Y = was.accs + (n * BLOCKS + b) * per + e
                y_slot = (b * per + e) % 2
                dve.wait_ge(s.acc, Y + 2)
                dve.wait_ge(s.down, U + 3)
                for k in range(BT):
                    t = b * BT + k
                    ins = dve.scalar_tensor_tensor(X[:, t, :], bank[4 + 2 * y_slot + k // 2][:, k % 2 * D:k % 2 * D + D],
                                                   shares_now[:, slot * per + e, t:t + 1], X[:, t, :], ALU.mult, ALU.add)
                ins.then_inc(s.acc, 1)
                if isinstance(n, int) and n == groups - 1 and e == per - 1:
                    dve.wait_ge(s.acc, Y + 3)
                    for k in range(BT):
                        next_stat(dve, b * BT + k)

            def vector(dve):
                dve.wait_ge(*before)
                router.vector_weights(dve)
                router.vector_lead(dve)
                entry.vector(dve)
                if was.groups == 0:
                    dve.sem_inc(s.hid, 2)
                    dve.sem_inc(s.acc, 2)
                vector_group(dve, 0, 0, routing=True)
                over_groups(dve, lambda n, slot, more: vector_group(dve, n, slot))
                dve.wait_ge(s.acc, was.accs + groups * ACCS + 2)
                dve.sem_inc(done, TILES)

            def tensor_group(pe, n, slot):
                hold(pe, s.wlo, was.groups + n + 1)

                def up(u):
                    U = was.units + n * UNITS + u
                    b, q = divmod(u, NC)
                    cols = slice(b * BLK, (b + 1) * BLK)
                    m = chunks[q][1]
                    hold(pe, s.hid, U + 1)
                    for mat, signal in ((0, s.up1), (1, s.up2)):
                        j = 0
                        for c in range(DC):
                            for w, x in ((whi, xhi), (whi, xlo), (wlo, xhi)):
                                mm = pe.matmul(bank[2 * mat + u % 2][0:m, :], up_w(w, slot, mat, c, q), x[:, c, cols],
                                               start=j == 0, stop=j == 3 * DC - 1)
                                j += 1
                        mm.then_inc(signal, 1)

                opened = set()

                def down(u):
                    U = was.units + n * UNITS + u
                    b, q = divmod(u, NC)
                    hold(pe, s.alo, U + 1)
                    for e, p0, np_ in outputs[q]:
                        Y = was.accs + (n * BLOCKS + b) * per + e
                        y_slot = (b * per + e) % 2
                        first = (b, e) not in opened
                        if first:
                            opened.add((b, e))
                            hold(pe, s.acc, Y + 1)
                        for k in range(BT):
                            j = 0
                            for a, w in ((ahi, whi), (ahi, wlo), (alo, whi)):
                                mm = pe.matmul(bank[4 + 2 * y_slot + k // 2][:, k % 2 * D:k % 2 * D + D],
                                               a[p0:p0 + np_, u % 2, k * P:(k + 1) * P], down_w(w, slot, q, p0, np_),
                                               start=first and k % 2 == 0 and j == 0, stop=last_chunk[e] == q and j == 2,
                                               skip_group_check=True)
                                j += 1
                    mm.then_inc(s.down, 1)

                for u in range(UNITS + 1):
                    if u < UNITS:
                        up(u)
                    if u:
                        down(u - 1)

            def tensor(pe):
                pe.wait_ge(*before)
                if was.groups == 0:
                    pe.sem_inc(s.w_free, 2)
                    pe.sem_inc(s.down, 2)
                router.tensor_weights(pe)
                entry.tensor(pe)
                pe.wait_ge(router.kept, router.all_kept)
                def group(n, slot):
                    tensor_group(pe, n, slot)
                    pe.wait_ge(s.down, was.units + (n + 1) * UNITS + 2)
                    pe.sem_inc(s.w_free, 1)

                group(0, 0)
                over_groups(pe, lambda n, slot, more: group(n, slot))

            return sync, gpsimd, scalar, vector, tensor

        def layer0_experts(before, done):
            EXPERTS, HALF = 8, P // 2
            rest = L0_I - P

            def load(sp, n, raw_up, raw_down, signal):
                for mat, (routed, shared) in enumerate((("L0_ffn_w1", "L0_ffn_sw1"), ("L0_ffn_w3", "L0_ffn_sw3"))):
                    for c in range(DC):
                        for e in range(2):
                            if isinstance(n, int) and n == 0:
                                src = io[shared][c * P:(c + 1) * P, e * L0_I:(e + 1) * L0_I]
                            else:
                                src = io[routed][ds(2 * n + (e - 2), 1), c * P:(c + 1) * P, :].rearrange("o p i -> p (o i)")
                            at = e * (P + HALF)
                            sp.dma_start(raw_up[:, mat, c, at:at + L0_I], src).then_inc(signal, 16)
                for e in range(2):
                    def rows(a, b):
                        if isinstance(n, int) and n == 0:
                            return io["L0_ffn_sw2"][e * L0_I + a:e * L0_I + b, :]
                        return io["L0_ffn_w2"][ds(2 * n + (e - 2), 1), a:b, :].rearrange("o i d -> (o i) d")
                    if e == 0:
                        sp.dma_start(raw_down[:, 0, :], rows(0, P)).then_inc(signal, 16)
                        sp.dma_start(raw_down[0:rest, 1, :], rows(P, L0_I)).then_inc(signal, 16)
                    else:
                        sp.dma_start(raw_down[HALF:P, 1, :], rows(0, HALF)).then_inc(signal, 16)
                        sp.dma_start(raw_down[0:L0_I - HALF, 2, :], rows(HALF, L0_I)).then_inc(signal, 16)
            load.count = 12

            return gated_experts("f0", 1, 0, 0, gates[:, 4:5], before, done, EXPERTS, 2, (True, io["L0_ffn_gate_w"]),
                                 chunks=[(0, P), (P, P), (2 * P, L0_I - HALF)],
                                 outputs=[[(0, 0, P)], [(0, 0, rest), (1, HALF, HALF)], [(1, 0, L0_I - HALF)]],
                                 groups=EXPERTS // 2 + 1, load=load, up_width=3 * P, down_chunks=3,
                                 more_steps=scan.vector_steps)

        def layer1_attention(before, done):
            HEADS = 16
            HD = D // HEADS
            HC = P // HD
            AUG = P + HC
            EPS = 1e-6
            lay = Layout()
            wq, wg, wo, wkv = lay(DC, D), lay(DC, D), lay(DC, D), lay(DC, 2 * D)
            inT = lay(2, 2 * DC, P)
            neg, grown, keyq = lay(2, 2 * D), lay(2, 2 * D), lay(2, 2 * D)
            values = lay(2, DC, AUG)
            summary = lay(2, 2, DC, AUG)
            gate, scaled = lay(2, D), lay(2, D)
            den, per_den = lay(2, HEADS), lay(2, HEADS)
            attended, attendedT = lay(2, D), lay(2, D)
            lay.at = L1_RAW
            raw_w = lay(10, D)
            bias_row = lay(D)[0:1]
            head_mask = sb("a1_head_mask", [P, AUG])
            norm = make_norm(2)
            s = Names()
            (
                s.mask, s.ones, s.in_ps, s.inT, s.keyq_ps, s.val_ps, s.neg, s.grown, s.keyq, s.values,
                s.gate, s.sum_ps, s.sum, s.num, s.den, s.att, s.attT_ps, s.attT, s.out
            ) = sems("a1", "mask ones in_ps inT keyq_ps val_ps neg grown keyq values gate sum_ps sum num den att "
                     "attT_ps attT out")
            was = count_weights(loaded=16 * 5, turned=4, ready=DC * 4)
            weights = (("L1_xattn_Wq", wq, 0, 2), ("L1_xattn_Wg", wg, 2, 2), ("L1_xattn_Wo", wo, 4, 2),
                       ("L1_xattn_Wkv", wkv, 6, 4))
            IN, KEYQ, VAL, SUM, NUM, OUT = bank[0], bank[1], bank[2], (bank[3], bank[4]), bank[5], bank[6]

            def sync(sp):
                for name, _, a, n in weights:
                    sp.dma_start(raw_w[:, a:a + n, :], io[name].rearrange("(a p) k -> p a k", p=P)).then_inc(weight.loaded, 16)
                sp.dma_start(bias_row, io["L1_xattn_bg"].partition_broadcast(1)).then_inc(weight.loaded, 16)
                sp.wait_ge(*before)
                tiles = io["ctx_2048"].rearrange("b s d -> (b s) d").rearrange("(t p) d -> t p d", p=P)
                for k in range(RING):
                    sp.dma_start(ctx_in[:, k, :], tiles[k]).then_inc(ctx_here[k], 16)
                with sp.Fori(1, TILES // RING) as i:
                    for k in range(RING):
                        t = i * RING + k
                        sp.wait_ge(s.in_ps, t - RING + 1)
                        sp.dma_start(ctx_in[:, k, :], tiles[ds(t, 1)].rearrange("o p d -> p (o d)")).then_inc(ctx_here[k], 16)

            def gpsimd(pool):
                v = head_mask[:, 0:P].rearrange("p (h j) -> p h j", h=HC)
                pool.memset(head_mask[:, :], 1.0).then_inc(s.mask, 1)
                pool.wait_ge(s.mask, 1)
                for half, (base, sign) in enumerate(((0, 1), (HD - 1, -1))):
                    if half:
                        pool.wait_ge(s.mask, 3)
                    pool.affine_select(out=v, in_=v, compare_op=ALU.is_ge, fill=0.0, base=base,
                                       pattern=[[-sign * HD, HC], [0, HD]], channel_multiplier=sign).then_inc(s.mask, 1)
                    pool.affine_select(out=head_mask[:, P:AUG], in_=head_mask[:, P:AUG], compare_op=ALU.is_ge, fill=0.0, base=base,
                                       pattern=[[-sign * HD, HC]], channel_multiplier=sign).then_inc(s.mask, 1)
                norm.gpsimd_stats(pool)

            def scalar_in(act, t, k):
                act.wait_ge(s.in_ps, t + 1)
                act.activation(flat(inT[:, k % 2]), IN[:, :], ACT.Copy).then_inc(s.inT, 1)

            def scalar(act):
                for j, (_, w, _, n) in enumerate(weights):
                    act.wait_ge(weight.turned, was.turned + j + 1)
                    for c in range(DC):
                        at = c * n * P
                        act.activation(w[:, c, :], bank[j + at // 512][:, at % 512:at % 512 + n * P], ACT.Copy).then_inc(weight.ready, 1)
                scalar_in(act, 0, 0)

                def step(t, k):
                    j = k % 2
                    if inside(t - 2):
                        act.wait_ge(s.attT_ps, t - 1)
                        act.activation(attendedT[:, j, :], OUT[:, 0:D], ACT.Copy).then_inc(s.attT, 1)
                    if inside(t + 1):
                        scalar_in(act, t + 1, k + 1)
                    if inside(t):
                        act.wait_ge(s.keyq_ps, t + 1)
                        act.activation(neg[:, j, :], KEYQ[:, :], ACT.Relu, scale=-1.0).then_inc(s.neg, 1)
                        act.wait_ge(s.neg, t + 1)
                        act.activation(grown[:, j, :], neg[:, j, :], ACT.Exp, scale=-1.0).then_inc(s.grown, 1)
                        act.wait_ge(s.val_ps, t + 1)
                        act.activation(values[:, j, :, 0:P], VAL[:, 0:D].rearrange("p (c e) -> p c e", c=DC), ACT.Copy).then_inc(s.values, 1)
                        act.activation(gate[:, j, :], VAL[:, D:2 * D], ACT.Tanh, scale=0.5).then_inc(s.gate, 1)
                over_tiles(act, step)

            def vector(dve):
                dve.wait_ge(*before)
                norm.vector_means(dve)
                dve.memset(values[:, :, :, P:AUG].rearrange("p j c h -> p (j c) h"), 1.0).then_inc(s.ones, 1)
                dve.wait_ge(s.mask, 5)
                for t in range(2):
                    norm.vector_tile(dve, t, t, xn[:, t, :])

                def step(t, k):
                    j = k % 2
                    if inside(t + 2):
                        if not isinstance(t, int) or t >= 2:
                            dve.wait_ge(s.in_ps, t - 1)
                        norm.vector_tile(dve, t + 2, (k + 2) % RING, xn[:, (k + 2) % RING, :])
                    if inside(t - 1):
                        dve.wait_ge(s.sum_ps, t)
                        for b in range(2):
                            dve.tensor_tensor(summary[:, 1 - j, b], SUM[b][:, 0:DC * AUG].rearrange("p (c a) -> p c a", c=DC),
                                              head_mask[:, :].unsqueeze(1).to_broadcast([P, DC, AUG]), ALU.mult).then_inc(s.sum, 1)
                    if inside(t - 2):
                        dve.wait_ge(s.out, t - 1)
                        dve.scalar_tensor_tensor(x_tile(t - 2), OUT[:, D:2 * D], gates[:, 1:2], x_tile(t - 2), ALU.mult, ALU.add).then_inc(done, 1)
                    if inside(t - 1):
                        dve.wait_ge(s.num, t)
                        got = NUM[:, 0:DC * AUG].rearrange("p (c a) -> p c a", c=DC)
                        dve.tensor_scalar(den[:, 1 - j, :].rearrange("p (c h) -> p c h", c=DC), got[:, :, P:AUG], EPS, 2.0, ALU.add, ALU.mult).then_inc(s.den, 1)
                        dve.wait_ge(s.gate, t)
                        dve.scalar_tensor_tensor(scaled[:, 1 - j, :].rearrange("p (c e) -> p c e", c=DC), gate[:, 1 - j, :].rearrange("p (c e) -> p c e", c=DC),
                                                 1.0, got[:, :, 0:P], ALU.add, ALU.mult).then_inc(s.den, 1)
                        hold(dve, s.den, t * 3 - 1)
                        dve.reciprocal(per_den[:, 1 - j, :], den[:, 1 - j, :]).then_inc(s.den, 1)
                        dve.wait_ge(s.den, t * 3)
                        dve.tensor_tensor(attended[:, 1 - j, :].rearrange("p (h e) -> p h e", h=HEADS), scaled[:, 1 - j, :].rearrange("p (h e) -> p h e", h=HEADS),
                                          per_den[:, 1 - j, :].unsqueeze(2).to_broadcast([P, HEADS, HD]), ALU.mult).then_inc(s.att, 1)
                    if inside(t):
                        dve.wait_ge(s.grown, t + 1)
                        dve.scalar_tensor_tensor(keyq[:, j, :], KEYQ[:, :], 0.0, grown[:, j, :], ALU.max, ALU.add).then_inc(s.keyq, 1)
                    if inside(t - 2):
                        hold(dve, done, before[1] + t - 1)
                        next_stat(dve, t - 2)
                over_tiles(dve, step)

            def tensor_in(pe, t, k):
                hold(pe, ctx_here[k], t // RING * 16 + 16 if isinstance(t, int) else (t - k) * (16 // RING) + 16)
                hold(pe, norm.xn, norm.first * BT + t + 1)
                for c in range(DC):
                    pe.transpose(IN[:, c * P:(c + 1) * P], xn[:, k, c * P:(c + 1) * P], ident[:, :])
                for c in range(DC):
                    tp = pe.transpose(IN[:, D + c * P:D + (c + 1) * P], ctx_in[:, k, c * P:(c + 1) * P], ident[:, :])
                tp.then_inc(s.in_ps, 1)

            def tensor(pe):
                pe.wait_ge(*before)
                pe.wait_ge(weight.loaded, was.loaded + 16 * 5)
                for j, (_, _, a0, n) in enumerate(weights):
                    for c in range(DC):
                        for a in range(n):
                            at = (c * n + a) * P
                            tp = pe.transpose(bank[j + at // 512][:, at % 512:at % 512 + P], raw_w[:, a0 + a, c * P:(c + 1) * P], ident[:, :])
                    tp.then_inc(weight.turned, 1)
                pe.wait_ge(weight.ready, was.ready + DC * len(weights))
                pe.wait_ge(s.ones, 1)
                tensor_in(pe, 0, 0)

                def step(t, k):
                    j = k % 2
                    if inside(t - 1):
                        hold(pe, s.keyq, t)
                        hold(pe, s.values, t)
                        hold(pe, s.gate, t)
                        for b in range(2):
                            rows = slice(b * SEQ, (b + 1) * SEQ)
                            for c in range(DC):
                                mm = pe.matmul(SUM[b][:, c * AUG:(c + 1) * AUG], keyq[rows, 1 - j, c * P:(c + 1) * P], values[rows, 1 - j, c, :],
                                               start=True, stop=True)
                        mm.then_inc(s.sum_ps, 1)
                    if inside(t - 2):
                        hold(pe, s.attT, t - 1)
                        for c in range(DC):
                            mm = pe.matmul(OUT[:, D:2 * D], attendedT[:, j, c * P:(c + 1) * P], wo[:, c, :], start=c == 0, stop=c == DC - 1)
                        mm.then_inc(s.out, 1)
                    if inside(t):
                        hold(pe, s.inT, t + 1)
                    if inside(t + 1):
                        tensor_in(pe, t + 1, (k + 1) % RING)
                    if inside(t):
                        for c in range(DC):
                            pe.matmul(KEYQ[:, 0:D], inT[:, j, DC + c, :], wkv[:, c, 0:D], start=c == 0, stop=c == DC - 1)
                        for m in range(DC):
                            for c in range(DC):
                                mm = pe.matmul(KEYQ[:, D + m * P:D + (m + 1) * P], wq[:, c, m * P:(m + 1) * P], inT[:, j, c, :],
                                               start=c == 0, stop=c == DC - 1)
                        mm.then_inc(s.keyq_ps, 1)
                    if inside(t - 1):
                        hold(pe, s.sum, t * 2)
                        for b in range(2):
                            rows = slice(b * SEQ, (b + 1) * SEQ)
                            for c in range(DC):
                                at = D + c * P + b * SEQ
                                mm = pe.matmul(NUM[rows, c * AUG:(c + 1) * AUG], keyq[:, 1 - j, at:at + SEQ], summary[:, 1 - j, b, c, :],
                                               start=True, stop=True)
                        mm.then_inc(s.num, 1)
                    if inside(t):
                        for c in range(DC):
                            pe.matmul(VAL[:, 0:D], inT[:, j, DC + c, :], wkv[:, c, D:2 * D], start=c == 0, stop=c == DC - 1)
                        for c in range(DC):
                            pe.matmul(VAL[:, D:2 * D], inT[:, j, c, :], wg[:, c, :], start=c == 0, stop=False)
                        pe.matmul(VAL[:, D:2 * D], ones[0:1, :], bias_row, start=False, stop=True).then_inc(s.val_ps, 1)
                    if inside(t - 1):
                        hold(pe, s.att, t)
                        if not isinstance(t, int) or t >= 2:
                            hold(pe, done, before[1] + t - 1)
                        for c in range(DC):
                            tp = pe.transpose(OUT[:, c * P:(c + 1) * P], attended[:, 1 - j, c * P:(c + 1) * P], ident[:, :])
                        tp.then_inc(s.attT_ps, 1)
                over_tiles(pe, step)

            return sync, gpsimd, scalar, vector, tensor

        quant_sems = sems("quant", "chain scale shifted tp turned")

        def make_quant(use, lay, scratch, dst):
            n = Names()
            n.chain, n.scale, n.shifted, n.tp, n.turned = quant_sems
            n.first = use * BLOCKS
            peak, rate = lay(BT), lay(TILES)
            n.step = lay(TILES)
            shifted = scratch.rearrange("p (j k d) -> p j k d", j=2, k=BT)

            def vector(dve, norm, i, tiles):
                g = n.first + i
                block = slice(i * BT, (i + 1) * BT)
                dve.wait_ge(norm.xn, (norm.first + i) * BT + BT)
                dve.tensor_reduce(peak, tiles[:, :, :], AX.X, ALU.max, apply_absolute_value=True).then_inc(n.chain, 1)
                dve.wait_ge(n.chain, g * 2 + 1)
                dve.tensor_scalar(n.step[:, block], peak, QUANT_EPS, 1.0 / 127, ALU.max, ALU.mult).then_inc(n.chain, 1)
                dve.wait_ge(n.chain, g * 2 + 2)
                dve.reciprocal(rate[:, block], n.step[:, block]).then_inc(n.scale, 1)
                dve.wait_ge(n.scale, g + 1)
                if i >= 2:
                    dve.wait_ge(n.tp, g - 1)
                for k in range(BT):
                    dve.tensor_scalar(shifted[:, i % 2, k, :], tiles[:, k, :], rate[:, i * BT + k:i * BT + k + 1], MAGIC,
                                      ALU.mult, ALU.add).then_inc(n.shifted, 1)

            def tensor(pe, i):
                pe.wait_ge(n.shifted, (n.first + i) * BT + BT)
                if i:
                    pe.wait_ge(n.turned, (n.first + i) * DC)
                for c in range(DC):
                    for k in range(BT):
                        tp = pe.transpose(bank[6 + c][:, k * P:(k + 1) * P], shifted[:, i % 2, k, c * P:(c + 1) * P], ident[:, :])
                tp.then_inc(n.tp, 1)

            def scalar(act, i):
                act.wait_ge(n.tp, n.first + i + 1)
                for c in range(DC):
                    act.activation(dst[:, c, i * BLK:(i + 1) * BLK], bank[6 + c][:, :], ACT.Copy, bias=-MAGIC).then_inc(n.turned, 1)

            n.vector, n.scalar, n.tensor = vector, scalar, tensor
            return n

        whole_sems = sems("whole", "raw size total chain ternary tern shifted w_tp w up relu once prod peak pair rate turned "
                            "wholeT down acc")
        whole_used = Names()

        def layer1_experts(before, done):
            E, I = 8, 512
            IC = I // P
            AHEAD, PEAK_AHEAD, SHIFT_AHEAD = 6, 5, 1
            RING = 8
            RELUS = 4
            TURN_AT = (4, 7, 10)
            SIZE_AT = (0, 2, 5)
            TOTAL_AT = 8
            SCALES_AT = 9
            MAT = I * D // P
            GATE, UP, DOWN = 0, 1, 2
            lay = Layout()
            prod = lay(RING, I)
            router = make_router("f1", 1, lay, (flat(prod[:, 0:2, :]), flat(prod[:, 2:4, :])), 0, E, 2, gates[:, 5:6], True, io["L1_ffn_router_w"])
            norm = make_norm(3, split=1, turn=1)
            xqT = lay(DC, TOK, dt=BF16)
            quant = make_quant(0, lay, flat(prod[:, RING // 2:, :]), xqT)
            entry = make_entry(norm, router, quant)
            step3 = lay(TILES)
            relu, once = lay(RELUS, I), lay(2, I)
            shifted, wholeT = lay(2, I), lay(2, I, dt=BF16)
            up_w = lay(2, 2, DC, I, dt=BF16)
            down_w = lay(2, IC, D, dt=BF16)
            tern = lay(3, MAT, dt=BF16)
            size_sum, mean, per_mean = lay(3), lay(3), lay(3)
            factor, inv = lay(TILES), lay(TILES)
            least, out_factor = lay(2, TILES), lay(2, TILES)
            peak, unit, rate, out_scale = lay(TILES), lay(TILES), lay(TILES), lay(TILES)
            s = Names()
            (
                s.raw, s.size, s.total, s.chain, s.ternary, s.tern, s.shifted, s.w_tp, s.w, s.up, s.relu, s.once,
                s.prod, s.peak, s.pair, s.rate, s.turned, s.wholeT, s.down, s.acc
            ) = whole_sems
            raw_m = [[raw[:, m * MAT:(m + 1) * MAT] for m in range(3)], [flat(v[:, :, :]) for v in (xn, ctx_sb, ctx_in)]]
            unused = flat(whi[:, :, :])[:, 0:3 * MAT].rearrange("p (m k) -> p m k", m=3)
            turn = bank[4][:, :]
            w_turn = bank[5][:, :].bitcast(BF16)
            totals = bank[5][:, 0:3]
            CHAIN = 7
            units = E * TILES
            after = whole_used
            after.tern_signal = s.tern
            after.raw, after.size, after.total, after.chain, after.tern = E * 48, E * 3, E, 2 + E * CHAIN, E * 3 + 3
            after.w_tp, after.w = E * 3, E * 3 + 1
            after.up = after.relu = after.peak = after.pair = after.wholeT = after.down = units
            after.rate, after.shifted, after.turned, after.acc = units // 2, units + RING, units + 2, units + 2
            raw_free = gated_counts[-1][1] + 1
            even = E - 2

            def sync(sp):
                router.sync(sp)
                sp.wait_ge(gated_sems[1], raw_free)
                def load(n, slot):
                    for m, w in ((GATE, "L1_ffn_gate_w"), (UP, "L1_ffn_up_w"), (DOWN, "L1_ffn_down_w")):
                        width = I if m == DOWN else D
                        src = io[w][ds(n, 1)].rearrange("o (a p) k -> p (o a) k", p=P)
                        sp.dma_start(raw_m[slot][m].rearrange("p (a k) -> p a k", k=width), src).then_inc(s.raw, 16)
                load(0, 0)
                sp.wait_ge(s.tern, 6)
                load(1, 1)
                with sp.Fori(1, E // 2) as i:
                    for slot in range(2):
                        n = 2 * i + slot
                        sp.wait_ge(s.size, n * 3)
                        sp.wait_ge(s.tern, n * 3)
                        load(n, slot)

            def scalar_size(act, n, slot, m):
                act.wait_ge(s.raw, n * 48 + 48)
                if not isinstance(n, int) or n:
                    act.wait_ge(s.size, n * 3 + m)
                act.activation(unused[:, m, :], raw_m[slot][m], ACT.Abs, accum_out=size_sum[:, m:m + 1]).then_inc(s.size, 1)

            def tensor_total(pe, n):
                hold(pe, s.size, n * 3 + 3)
                if not isinstance(n, int) or n:
                    hold(pe, s.w, n * 3)
                pe.matmul(totals, ones[:, :], size_sum, start=True, stop=True).then_inc(s.total, 1)

            def vector_scale(dve, n, slot, op):
                if op == 0:
                    dve.wait_ge(s.total, n + 1)
                dve.wait_ge(s.chain, n * CHAIN + 2 + op)
                of_gate, of_up, of_down = (mean[:, m:m + 1] for m in (GATE, UP, DOWN))
                if op == 0:
                    ins = dve.tensor_scalar(mean, totals, 1.0 / (I * D), QUANT_EPS, ALU.mult, ALU.max)
                elif op == 1:
                    ins = dve.reciprocal(per_mean, mean)
                elif op == 2:
                    ins = dve.tensor_scalar(factor, step3, of_gate, of_gate, ALU.mult, ALU.mult)
                elif op == 3:
                    ins = dve.tensor_scalar(factor, factor, of_up, None, ALU.mult)
                elif op == 4:
                    ins = dve.reciprocal(inv, factor)
                elif op == 5:
                    ins = dve.tensor_scalar(least[:, slot, :], inv, QUANT_EPS / 127, None, ALU.mult)
                else:
                    share = router.shares[:, n, :] if isinstance(n, int) else flat(router.shares[:, ds(n, 1), :])
                    ins = dve.scalar_tensor_tensor(out_factor[:, slot, :], factor, of_down, share, ALU.mult, ALU.mult)
                ins.then_inc(s.chain, 1)

            def ternary(eng, n, slot, m, part):
                w = raw_m[slot][m]
                if part == 0:
                    hold(eng, s.chain, n * CHAIN + 4)
                    eng.tensor_scalar(w, w, per_mean[:, m:m + 1], MAGIC, ALU.mult, ALU.add).then_inc(s.ternary, 1)
                elif part == 1:
                    hold(eng, s.ternary, (n * 3 + m) * 2 + 1)
                    eng.tensor_scalar(tern[:, m, :], w, MAGIC, -1.0, ALU.subtract, ALU.max).then_inc(s.ternary, 1)
                else:
                    hold(eng, s.ternary, (n * 3 + m) * 2 + 2)
                    eng.tensor_scalar(tern[:, m, :], tern[:, m, :], 1.0, None, ALU.min).then_inc(s.tern, 1)

            def tensor_turn(pe, n, m):
                hold(pe, s.tern, n * 3 + m + 4)
                hold(pe, s.w, n * 3 + m + 1)
                rows, cols = (DC, IC) if m == DOWN else (IC, DC)
                for c in range(cols):
                    for a in range(rows):
                        at = (c * rows + a) * P
                        tp = pe.transpose(w_turn[:, at:at + P], tern[:, m, (a * cols + c) * P:(a * cols + c + 1) * P], identb[:, :])
                tp.then_inc(s.w_tp, 1)

            def scalar_weights(act, n, slot, m):
                act.wait_ge(s.w_tp, n * 3 + m + 1)
                to = down_w[:, slot, :, :] if m == DOWN else up_w[:, slot, m, :, :]
                act.activation(flat(to), w_turn, ACT.Copy).then_inc(s.w, 1)

            def scalar_relu(act, n, t):
                act.wait_ge(s.up, n * TILES + t + 1)
                act.wait_ge(s.prod, n * TILES + t + 1)
                act.activation(relu[:, t % RELUS, :], bank[t % 2][:, :], ACT.Relu).then_inc(s.relu, 1)

            def scalar_shift(act, n, t):
                U = n * TILES + t
                act.wait_ge(s.rate, n * (TILES // 2) + t // 2 + 1)
                act.wait_ge(s.turned, U + 1)
                act.activation(shifted[:, t % 2, :], prod[:, t % RING, :], ACT.Copy, scale=rate[:, t:t + 1],
                               bias=MAGIC).then_inc(s.shifted, 1)

            def scalar_back(act, n, t):
                act.wait_ge(s.turned, n * TILES + t + 3)
                act.activation(wholeT[:, t % 2, :], turn, ACT.Copy, bias=-MAGIC).then_inc(s.wholeT, 1)

            def vector_once(dve, n, t):
                U = n * TILES + t
                dve.wait_ge(s.relu, U + 1)
                dve.wait_ge(s.prod, U + RELUS - 1)
                dve.tensor_tensor(once[:, t % 2, :], relu[:, t % RELUS, :], bank[2 + t % 2][:, :], ALU.mult).then_inc(s.once, 1)

            def gpsimd_prod(pool, n, t):
                U = n * TILES + t
                pool.wait_ge(s.once, U + 3)
                hold(pool, s.shifted, U + 1)
                pool.tensor_tensor(prod[:, t % RING, :], once[:, t % 2, :], relu[:, t % RELUS, :], ALU.mult).then_inc(s.prod, 1)

            def vector_peak(dve, n, t):
                dve.wait_ge(s.prod, n * TILES + t + RELUS + 1)
                dve.tensor_reduce(peak[:, t:t + 1], prod[:, t % RING, :], AX.X, ALU.max, apply_absolute_value=True).then_inc(s.peak, 1)

            def vector_unit(dve, n, t, slot):
                two = slice(t - 1, t + 1)
                dve.wait_ge(s.peak, n * TILES + t + 1)
                dve.scalar_tensor_tensor(unit[:, two], peak[:, two], 1.0 / 127, least[:, slot, two], ALU.mult, ALU.max).then_inc(s.pair, 1)

            def vector_rate(dve, n, t, slot):
                two = slice(t - 1, t + 1)
                hold(dve, s.pair, (n * (TILES // 2) + t // 2) * 2 + 1)
                dve.reciprocal(rate[:, two], unit[:, two]).then_inc(s.rate, 1)
                dve.tensor_tensor(out_scale[:, two], unit[:, two], out_factor[:, slot, two], ALU.mult).then_inc(s.pair, 1)

            def vector_back(dve, n, t):
                U = n * TILES + t
                dve.wait_ge(s.down, U + 1)
                dve.wait_ge(s.pair, (n * (TILES // 2) + t // 2) * 2 + 2)
                dve.scalar_tensor_tensor(X[:, t, :], bank[6 + t % 2][:, 0:D], out_scale[:, t:t + 1], X[:, t, :],
                                         ALU.mult, ALU.add).then_inc(s.acc, 1)
                if isinstance(n, int) and n == E - 1:
                    dve.wait_ge(s.acc, U + 3)
                    next_stat(dve, t)

            def tensor_up(pe, n, t, slot):
                hold(pe, s.once, n * TILES + t + 1)
                for m in (GATE, UP):
                    for c in range(DC):
                        mm = pe.matmul(bank[2 * m + t % 2][:, :], xqT[:, c, t * P:(t + 1) * P], up_w[:, slot, m, c, :],
                                       start=c == 0, stop=c == DC - 1)
                mm.then_inc(s.up, 1)

            def tensor_turn_tile(pe, n, t):
                hold(pe, s.shifted, n * TILES + t + RING + 1)
                for c in range(IC):
                    tp = pe.transpose(turn[:, c * P:(c + 1) * P], shifted[:, t % 2, c * P:(c + 1) * P], ident[:, :])
                tp.then_inc(s.turned, 1)

            def tensor_down(pe, n, t, slot):
                hold(pe, s.wholeT, n * TILES + t + 1)
                hold(pe, s.acc, n * TILES + t + 1)
                for c in range(IC):
                    mm = pe.matmul(bank[6 + t % 2][:, 0:D], wholeT[:, t % 2, c * P:(c + 1) * P], down_w[:, slot, c, :],
                                   start=c == 0, stop=c == IC - 1)
                mm.then_inc(s.down, 1)

            def over_experts(eng, step):
                with eng.Fori(0, even // 2) as i:
                    for slot in range(2):
                        step(2 * i + slot, slot, True)
                for n in range(even, E):
                    step(n, n % 2, n + 1 < E)

            def another(n):
                return not isinstance(n, int) or n + 2 < E

            def following(n, t, slot, lead):
                return (n, t + lead, slot) if t + lead < TILES else (n + 1, t + lead - TILES, 1 - slot)

            def gpsimd(pool):
                pool.wait_ge(*before)
                router.gpsimd(pool)
                entry.gpsimd(pool)
                pool.sem_inc(s.prod, RELUS)
                for t in range(AHEAD):
                    gpsimd_prod(pool, 0, t)

                def step(n, slot, more):
                    for t in range(TILES):
                        if t + AHEAD < TILES or more:
                            gpsimd_prod(pool, *following(n, t, slot, AHEAD)[0:2])
                        if t < 9 and t % 3 == 0 and more:
                            ternary(pool, n + 1, 1 - slot, *divmod(t, 3))
                over_experts(pool, step)

            def scalar(act):
                act.wait_ge(*before)
                act.sem_inc(s.w, 1)
                for m in range(3):
                    scalar_size(act, 0, 0, m)
                entry.scalar(act)
                for m in range(3):
                    scalar_weights(act, 0, 0, m)
                router.scalar_last(act)
                for m in range(3):
                    scalar_size(act, 1, 1, m)
                act.sem_inc(s.shifted, RING)
                for t in range(AHEAD):
                    scalar_relu(act, 0, t)
                for t in range(SHIFT_AHEAD):
                    scalar_shift(act, 0, t)

                def step(n, slot, more):
                    for t in range(TILES):
                        if t in SIZE_AT and another(n):
                            scalar_size(act, n + 2, slot, SIZE_AT.index(t))
                        if t + SHIFT_AHEAD < TILES or more:
                            scalar_shift(act, *following(n, t, slot, SHIFT_AHEAD)[0:2])
                        if t - 1 in TURN_AT and more:
                            scalar_weights(act, n + 1, 1 - slot, TURN_AT.index(t - 1))
                        scalar_back(act, n, t)
                        if t + AHEAD < TILES or more:
                            scalar_relu(act, *following(n, t, slot, AHEAD)[0:2])
                over_experts(act, step)

            def vector(dve):
                dve.wait_ge(*before)
                dve.sem_inc(s.tern, 3)
                dve.sem_inc(s.once, 2)
                dve.sem_inc(s.acc, 2)
                router.vector_weights(dve)
                entry.vector(dve)
                dve.wait_ge(quant.chain, 2 * BLOCKS)
                dve.tensor_tensor(step3, quant.step, quant.step, ALU.mult).then_inc(s.chain, 1)
                dve.wait_ge(s.chain, 1)
                dve.tensor_tensor(step3, step3, quant.step, ALU.mult).then_inc(s.chain, 1)
                dve.wait_ge(s.chain, 2)
                for op in range(2):
                    vector_scale(dve, 0, 0, op)
                for m in range(3):
                    for part in range(3):
                        ternary(dve, 0, 0, m, part)
                router.vector_lead(dve)
                for step in router.vector_steps:
                    step(dve)
                for op in range(2, CHAIN):
                    vector_scale(dve, 0, 0, op)
                for t in range(AHEAD):
                    vector_once(dve, 0, t)
                    if t >= AHEAD - PEAK_AHEAD:
                        vector_peak(dve, 0, t - (AHEAD - PEAK_AHEAD))
                for t in range(1, PEAK_AHEAD, 2):
                    vector_unit(dve, 0, t, 0)
                    if t < PEAK_AHEAD - 1:
                        vector_rate(dve, 0, t, 0)
                for op in range(CHAIN):
                    vector_scale(dve, 1, 1, op)

                def step(n, slot, more):
                    for t in range(TILES):
                        if t + AHEAD < TILES or more:
                            vector_once(dve, *following(n, t, slot, AHEAD)[0:2])
                        if (t + PEAK_AHEAD - 1) % 2 and (t + PEAK_AHEAD - 1 < TILES or more):
                            vector_rate(dve, *following(n, t, slot, PEAK_AHEAD - 1))
                        if t + PEAK_AHEAD < TILES or more:
                            vector_peak(dve, *following(n, t, slot, PEAK_AHEAD)[0:2])
                        vector_back(dve, n, t)
                        if (t + PEAK_AHEAD) % 2 and (t + PEAK_AHEAD < TILES or more):
                            vector_unit(dve, *following(n, t, slot, PEAK_AHEAD))
                        if t < 9 and t % 3 and more:
                            ternary(dve, n + 1, 1 - slot, *divmod(t, 3))
                        if t >= SCALES_AT and another(n):
                            vector_scale(dve, n + 2, slot, t - SCALES_AT)
                over_experts(dve, step)
                dve.wait_ge(s.acc, E * TILES + 2)
                dve.sem_inc(done, TILES)

            def tensor(pe):
                pe.wait_ge(*before)
                router.tensor_weights(pe)
                entry.tensor(pe)
                pe.wait_ge(quant.turned, DC * BLOCKS)
                pe.wait_ge(router.kept, router.all_kept)
                tensor_total(pe, 0)
                for m in range(3):
                    tensor_turn(pe, 0, m)
                pe.wait_ge(s.w, 4)
                pe.sem_inc(s.turned, 2)
                for t in range(2):
                    tensor_up(pe, 0, t, 0)
                tensor_total(pe, 1)
                for t in range(2, AHEAD):
                    tensor_up(pe, 0, t, 0)

                def step(n, slot, more):
                    for t in range(TILES):
                        if t == TOTAL_AT and another(n):
                            tensor_total(pe, n + 2)
                        tensor_turn_tile(pe, n, t)
                        if t + AHEAD < TILES or more:
                            if t + AHEAD == TILES:
                                hold(pe, s.w, (n + 1) * 3 + 3)
                            tensor_up(pe, *following(n, t, slot, AHEAD))
                        if t == 0:
                            hold(pe, s.w, n * 3 + 4)
                        tensor_down(pe, n, t, slot)
                        if t in TURN_AT and more:
                            if TOTAL_AT < t and another(n):
                                hold(pe, s.chain, (n + 2) * CHAIN + 3)
                            tensor_turn(pe, n + 1, TURN_AT.index(t))
                over_experts(pe, step)

            return sync, gpsimd, scalar, vector, tensor

        def layer2_attention(before, done):
            HEADS, GROUPS, HD = 32, 8, 8
            GD = GROUPS * HD
            PAIRS = HEADS // GROUPS // 2
            UNITS = BATCH * PAIRS
            QB = 4
            PARTS = BATCH // QB
            PT = QB * SEQ // P
            SLOTS = 2 * QB
            ROUND = SLOTS * PAIRS
            SC = GROUPS * SEQ // P
            AUG = HD + 1
            lay = Layout()
            wqT, wkT, wvT, wfT = lay(DC, 2, P), lay(DC, P), lay(DC, GD), lay(2, D)
            xT, cT = lay(DC, QB * SEQ), lay(DC, QB, 2, SEQ)
            qT = lay(SLOTS, 2 * SEQ)
            kT = lay(QB, SEQ)
            kblk = lay(QB, GROUPS, SEQ)
            vblk = lay(SLOTS, SC, 2 * AUG)
            score, prob, probT = lay(2, GROUPS * SEQ), lay(2, GROUPS * SEQ), lay(2, GROUPS * SEQ)
            top, inv = lay(2, GROUPS), lay(2, PAIRS, GROUPS)
            attended, attendedT = lay(2, PAIRS, GD), lay(2, 2, SEQ)
            band, in_group = lay(2, GROUPS), lay(GROUPS)
            bias = lay(D)
            norm = make_norm(4)
            s = Names()
            (
                s.fold, s.group, s.ones, s.bias, s.biased, s.ctx_ps, s.cT, s.x_ps, s.xT, s.kv_ps, s.kT,
                s.vblk, s.q_ps, s.qT, s.kblk, s.score, s.top, s.shifted, s.exp, s.probT_ps, s.probT, s.read, s.inv, s.att, s.attT_ps,
                s.attT, s.out
            ) = sems("a2", "fold group ones bias biased ctx_ps cT x_ps xT kv_ps kT vblk q_ps qT kblk score top "
                     "shifted exp probT_ps probT read inv att attT_ps attT out")
            was = count_weights(loaded=16 * 5, turned=1, ready=2 * DC + 4)
            raw_q, raw_f = raw[:, 0:2 * D].rearrange("p (a k) -> p a k", a=2), raw[:, 2 * D:4 * D].rearrange("p (a k) -> p a k", a=2)
            raw_k, raw_v = raw[:, 4 * D:5 * D], raw[:, 5 * D:6 * D]
            fold_f = raw[:, 6 * D:8 * D].rearrange("p (a m k) -> p a m k", a=DC, m=2)
            raw_b = raw[:, 8 * D:9 * D]
            SOFT, IN, TURN, READ, OUT = (bank[0], bank[1]), bank[2], (bank[3], bank[4]), (bank[5], bank[6]), bank[7]

            def inside(i, x, units):
                return not isinstance(i, int) or 0 <= x < units

            def over_units(eng, step, last):
                for x in range(ROUND // 2):
                    step(0, x)
                with eng.Fori(0, UNITS // ROUND - 1) as i:
                    for x in range(ROUND // 2, ROUND + ROUND // 2):
                        step(i, x)
                for x in range(UNITS - ROUND // 2, UNITS + last):
                    step(0, x)

            def nth(i, x, per):
                return i * (ROUND // per) + x // per

            PART = QB * PAIRS
            BATCH_U, TILE_U = PAIRS, 2 * PAIRS

            def sync(sp):
                sp.wait_ge(whole_used.tern_signal, whole_used.tern)
                sp.dma_start(raw_q, io["L2_xattn_Wq"].rearrange("(a p) k -> p a k", p=P)).then_inc(weight.loaded, 16)
                sp.dma_start(raw_f, io["L2_xattn_Wfc"].rearrange("(a p) k -> p a k", p=P)).then_inc(weight.loaded, 16)
                sp.dma_start(raw_k[0:GD, :], io["L2_xattn_Wk"]).then_inc(weight.loaded, 16)
                sp.dma_start(raw_v[0:GD, :], io["L2_xattn_Wv"]).then_inc(weight.loaded, 16)
                sp.dma_start(raw_b, io["L2_xattn_bfc"].partition_broadcast(P)).then_inc(weight.loaded, 16)
                tiles = io["ctx_2048"].rearrange("b s d -> (b s) d").rearrange("(t p) d -> t p d", p=P)
                for k in range(RING):
                    sp.dma_start(ctx_in[:, k, :], tiles[k]).then_inc(ctx_here[k], 16)
                with sp.Fori(1, TILES // RING) as i:
                    for k in range(RING):
                        sp.wait_ge(s.ctx_ps, (i - 1) * (RING // PT) + k // PT + 1)
                        sp.dma_start(ctx_in[:, k, :], tiles[ds(i * RING + k, 1)].rearrange("o p d -> p (o d)")).then_inc(ctx_here[k], 16)

            def gpsimd(pool):
                pool.wait_ge(*before)
                flat_band = band.rearrange("p h g -> p (h g)")
                pool.memset(flat_band, 1.0).then_inc(s.group, 1)
                pool.wait_ge(s.group, 1)
                pool.affine_select(out=flat_band, in_=flat_band, compare_op=ALU.is_ge, fill=0.0, base=0,
                                   pattern=[[-HD, 2 * GROUPS]], channel_multiplier=1).then_inc(s.group, 1)
                pool.wait_ge(s.group, 2)
                pool.affine_select(out=flat_band, in_=flat_band, compare_op=ALU.is_ge, fill=0.0, base=HD - 1,
                                   pattern=[[HD, 2 * GROUPS]], channel_multiplier=-1).then_inc(s.group, 1)
                pool.wait_ge(s.group, 3)
                pool.tensor_tensor(in_group, band[:, 0, :], band[:, 1, :], ALU.add).then_inc(s.group, 1)
                norm.gpsimd_stats(pool)
                pool.wait_ge(s.group, 4)
                pool.wait_ge(s.bias, 1)

                def part(h):
                    for e in range(PT):
                        t = h * PT + e
                        pool.wait_ge(norm.xn, norm.first * BT + t + 1)
                        pool.tensor_tensor(x_tile(t), x_tile(t), bias, ALU.add).then_inc(s.biased, 1)
                    n = [P, GROUPS, SEQ]
                    for b in range(QB):
                        pool.wait_ge(s.kT, h + 1)
                        if not isinstance(h, int) or h:
                            pool.wait_ge(s.score, (h * QB + b - QB + 1) * PAIRS)
                        pool.tensor_tensor(kblk[:, b], kT[:, b, :].unsqueeze(1).to_broadcast(n), in_group.unsqueeze(2).to_broadcast(n),
                                           ALU.mult).then_inc(s.kblk, 1)
                part(0)
                with pool.Fori(1, PARTS) as h:
                    part(h)

            def scalar_context(act, h, at):
                act.wait_ge(s.ctx_ps, h + 1)
                for c in range(DC):
                    got = IN[:, c * QB * SEQ:(c + 1) * QB * SEQ].rearrange("p (b t) -> p b t", b=QB)
                    act.activation(cT[:, c], got.unsqueeze(2).to_broadcast([P, QB, 2, SEQ]), ACT.Copy).then_inc(s.cT, 1)

            def scalar_tokens(act, h, at):
                act.wait_ge(s.x_ps, h + 1)
                act.activation(flat(xT), IN[:, :], ACT.Copy).then_inc(s.xT, 1)

            def scalar_keys(act, h, at):
                act.wait_ge(s.kv_ps, h + 1)
                if not isinstance(h, int) or h:
                    act.wait_ge(s.kblk, h * QB)
                act.activation(flat(kT), IN[:, 0:QB * SEQ], ACT.Copy).then_inc(s.kT, 1)
                got = IN[:, QB * SEQ:].rearrange("p (b c g d) -> p b c g d", b=QB, c=SC, g=2)
                for half in range(2):
                    rows = slice(half * SEQ, (half + 1) * SEQ)
                    act.activation(vblk[rows, at * QB:(at + 1) * QB, :, half * AUG:half * AUG + HD], got[rows, :, :, half, :], ACT.Copy).then_inc(s.vblk, 1)

            def scalar_queries(act, h, at):
                act.wait_ge(s.q_ps, h + 1)
                act.activation(qT[:, at * QB:(at + 1) * QB, :].rearrange("p b (m t) -> p m b t", m=2),
                               IN[:, :].rearrange("p (m b t) -> p m b t", m=2, b=QB), ACT.Copy).then_inc(s.qT, 1)

            scalar_stages = (scalar_context, scalar_tokens, scalar_keys, scalar_queries)

            def scalar(act):
                act.wait_ge(weight.loaded, was.loaded + 16 * 5)
                for a in range(DC):
                    cols = raw_f[:, a, :].rearrange("p (g q m d) -> p m q g d", g=GROUPS, q=PAIRS, m=2)
                    for m in range(2):
                        act.activation(fold_f[:, a, m, :].rearrange("p (q g d) -> p q g d", q=PAIRS, g=GROUPS), cols[:, m], ACT.Copy).then_inc(s.fold, 1)
                act.wait_ge(weight.turned, was.turned + 1)
                for c in range(DC):
                    cols = bank[0][:, c * D:(c + 1) * D].rearrange("p (g q m d) -> p m q g d", g=GROUPS, q=PAIRS, m=2)
                    for m in range(2):
                        act.activation(wqT[:, c, m, :].rearrange("p (q g d) -> p q g d", q=PAIRS, g=GROUPS), cols[:, m], ACT.Copy).then_inc(weight.ready, 1)
                act.activation(flat(wfT), bank[1][:, :], ACT.Copy).then_inc(weight.ready, 1)
                for half in range(2):
                    act.activation(wkT[:, :, half * GD:(half + 1) * GD], bank[2][:, 0:DC * GD].rearrange("p (c k) -> p c k", c=DC), ACT.Copy).then_inc(weight.ready, 1)
                act.activation(flat(wvT), bank[2][:, DC * GD:2 * DC * GD], ACT.Copy).then_inc(weight.ready, 1)
                act.wait_ge(s.ones, 3)
                for stage in scalar_stages:
                    stage(act, 0, 0)

                def step(i, x):
                    if inside(i, x, UNITS):
                        act.wait_ge(s.shifted, i * ROUND + x + 1)
                        act.activation(prob[:, x % 2, :], score[:, x % 2, :], ACT.Exp, scale=HD ** -0.5).then_inc(s.exp, 1)
                    if inside(i, x - 1, UNITS):
                        act.wait_ge(s.probT_ps, i * ROUND + x)
                        act.activation(probT[:, (x - 1) % 2, :], TURN[(x - 1) % 2][:, :], ACT.Copy).then_inc(s.probT, 1)
                    if x % 4 == 3 and inside(i, x - 7, UNITS):
                        act.wait_ge(s.attT_ps, nth(i, x - 7, TILE_U) + 1)
                        act.activation(attendedT, OUT[:, 0:2 * P].rearrange("p (b m t) -> p m b t", b=2, m=2), ACT.Copy).then_inc(s.attT, 1)
                    if 1 <= x % PART <= 4 and inside(i, x + PART, UNITS):
                        scalar_stages[x % PART - 1](act, nth(i, x, PART) + 1, (x // PART + 1) % 2)
                over_units(act, step, 9)

            def vector(dve):
                dve.wait_ge(*before)
                norm.vector_means(dve)
                dve.memset(vblk.rearrange("p b c a -> p (b c a)"), 0.0).then_inc(s.ones, 1)
                dve.wait_ge(s.ones, 1)
                for half in range(2):
                    rows = slice(half * SEQ, (half + 1) * SEQ)
                    dve.memset(vblk[rows, :, :, half * AUG + HD], 1.0).then_inc(s.ones, 1)
                dve.wait_ge(weight.loaded, was.loaded + 16 * 5)
                dve.tensor_scalar(bias, raw_b, gates[:, 2:3], None, ALU.mult).then_inc(s.bias, 1)
                for t in range(PT):
                    norm.vector_tile(dve, t, t, xn[:, t, :])

                def step(i, x):
                    if x % PART == 0 and inside(i, x + PART, UNITS):
                        for e in range(PT):
                            at = (x // PART + 1) % 2 * PT + e
                            norm.vector_tile(dve, (nth(i, x, PART) + 1) * PT + e, at, xn[:, at, :])
                    if inside(i, x, UNITS):
                        U = i * ROUND + x
                        got = SOFT[x % 2][:, :].rearrange("p (g k) -> p g k", g=GROUPS)
                        dve.wait_ge(s.score, U + 1)
                        dve.tensor_reduce(top[:, x % 2, :], got, AX.X, ALU.max).then_inc(s.top, 1)
                        dve.wait_ge(s.top, U + 1)
                        if not isinstance(i, int) or x >= 2:
                            dve.wait_ge(s.exp, U - 1)
                        dve.tensor_tensor(score[:, x % 2, :].rearrange("p (g k) -> p g k", g=GROUPS), got,
                                          top[:, x % 2, :].unsqueeze(2).to_broadcast([P, GROUPS, SEQ]), ALU.subtract).then_inc(s.shifted, 1)
                    if x % 2 == 0 and inside(i, x - 4, UNITS):
                        B = nth(i, x - 4, BATCH_U)
                        j = (x - 4) // 2 % 2
                        got = READ[j][:, 0:PAIRS * SC * 2 * AUG].rearrange("p (m g a) -> p m g a", m=PAIRS, g=GROUPS)
                        hold(dve, s.read, B + 1)
                        dve.reciprocal(inv[:, j], got[:, :, :, HD]).then_inc(s.inv, 1)
                        dve.wait_ge(s.inv, B + 1)
                        dve.tensor_tensor(attended[:, j].rearrange("p m (g d) -> p m g d", g=GROUPS), got[:, :, :, 0:HD],
                                          inv[:, j].unsqueeze(3).to_broadcast([P, PAIRS, GROUPS, HD]), ALU.mult).then_inc(s.att, 1)
                    if x % 4 == 1 and inside(i, x - 9, UNITS):
                        t = nth(i, x - 9, TILE_U)
                        dve.wait_ge(s.out, t + 1)
                        dve.wait_ge(s.biased, t + 1)
                        dve.scalar_tensor_tensor(x_tile(t), OUT[:, 2 * P:2 * P + D], gates[:, 2:3], x_tile(t), ALU.mult, ALU.add).then_inc(done, 1)
                        hold(dve, done, before[1] + t + 1)
                        next_stat(dve, t)
                over_units(dve, step, 10)

            def tensor_context(pe, h, at):
                if not isinstance(h, int) or h:
                    hold(pe, s.qT, h)
                for e in range(PT):
                    k = at * PT + e
                    hold(pe, ctx_here[k], RING_LOADS + h * 8 - at * 8 + 16)
                for c in range(DC):
                    for e in range(PT):
                        tp = pe.transpose(IN[:, (c * PT + e) * P:(c * PT + e + 1) * P], ctx_in[:, at * PT + e, c * P:(c + 1) * P], ident[:, :])
                tp.then_inc(s.ctx_ps, 1)

            def tensor_tokens(pe, h, at):
                hold(pe, norm.xn, norm.first * BT + h * PT + PT)
                hold(pe, s.cT, h * DC + DC)
                for c in range(DC):
                    for e in range(PT):
                        tp = pe.transpose(IN[:, (c * PT + e) * P:(c * PT + e + 1) * P], xn[:, at * PT + e, c * P:(c + 1) * P], ident[:, :])
                tp.then_inc(s.x_ps, 1)

            def tensor_keys(pe, h, at):
                hold(pe, s.xT, h + 1)
                for c in range(DC):
                    pe.matmul(IN[:, 0:QB * SEQ], wkT[:, c, :], cT[:, c, :, 0, :], start=c == 0, stop=c == DC - 1)
                for b in range(QB):
                    for c in range(DC):
                        to = QB * SEQ + b * GD
                        mm = pe.matmul(IN[:, to:to + GD], cT[:, c, b].rearrange("p h t -> p (h t)"), wvT[:, c, :], start=c == 0, stop=c == DC - 1)
                mm.then_inc(s.kv_ps, 1)

            def tensor_queries(pe, h, at):
                hold(pe, s.vblk, h * 2 + 2)
                for m in range(2):
                    for c in range(DC):
                        mm = pe.matmul(IN[:, m * QB * SEQ:(m + 1) * QB * SEQ], wqT[:, c, m, :], xT[:, c, :], start=c == 0, stop=c == DC - 1)
                mm.then_inc(s.q_ps, 1)

            tensor_stages = (tensor_context, tensor_tokens, tensor_keys, tensor_queries)

            def tensor_scores(pe, i, x):
                slot, pair = x // PAIRS % SLOTS, x % PAIRS
                if x % PART == 0:
                    hold(pe, s.qT, nth(i, x, PART) + 1)
                if pair == 0:
                    hold(pe, s.kblk, nth(i, x, BATCH_U) + 1)
                if not isinstance(i, int) or x >= 2:
                    hold(pe, s.shifted, i * ROUND + x - 1)
                rows = slice(pair * GD, (pair + 1) * GD)
                pe.matmul(SOFT[x % 2][:, :], qT[rows, slot, :], kblk[rows, slot % QB].rearrange("p g k -> p (g k)"),
                          start=True, stop=True).then_inc(s.score, 1)

            def tensor(pe):
                pe.wait_ge(*before)
                pe.wait_ge(s.fold, 2 * DC)
                for c in range(DC):
                    for a in range(DC):
                        pe.transpose(bank[0][:, c * D + a * P:c * D + (a + 1) * P], raw_q[:, a, c * P:(c + 1) * P], ident[:, :])
                for m in range(2):
                    for a in range(DC):
                        pe.transpose(bank[1][:, m * D + a * P:m * D + (a + 1) * P], fold_f[:, a, m, :], ident[:, :])
                for j, w in enumerate((raw_k, raw_v)):
                    for c in range(DC):
                        at = (j * DC + c) * GD
                        tp = pe.transpose(bank[2][:, at:at + GD], w[0:GD, c * P:(c + 1) * P], ident[0:GD, 0:GD])
                tp.then_inc(weight.turned, 1)
                pe.wait_ge(weight.ready, was.ready + 2 * DC + 4)
                for stage in tensor_stages:
                    stage(pe, 0, 0)
                for x in range(2):
                    tensor_scores(pe, 0, x)

                def step(i, x):
                    if inside(i, x + 2, UNITS):
                        tensor_scores(pe, i, x + 2)
                    if inside(i, x, UNITS):
                        hold(pe, s.exp, i * ROUND + x + 1)
                        for c in range(SC):
                            tp = pe.transpose(TURN[x % 2][:, c * P:(c + 1) * P], prob[:, x % 2, c * P:(c + 1) * P], ident[:, :])
                        tp.then_inc(s.probT_ps, 1)
                    if inside(i, x - 1, UNITS):
                        slot, pair = (x - 1) // PAIRS % SLOTS, (x - 1) % PAIRS
                        B = nth(i, x - 1, BATCH_U)
                        hold(pe, s.probT, i * ROUND + x)
                        if pair == 0 and (not isinstance(B, int) or B >= 2):
                            hold(pe, s.att, B - 1)
                        for c in range(SC):
                            at = (pair * SC + c) * 2 * AUG
                            mm = pe.matmul(READ[slot % 2][:, at:at + 2 * AUG], probT[:, (x - 1) % 2, c * P:(c + 1) * P], vblk[:, slot, c, :],
                                           start=True, stop=True)
                        if pair == PAIRS - 1:
                            mm.then_inc(s.read, 1)
                    if x % 2 == 1 and inside(i, x - 5, UNITS):
                        B = nth(i, x - 5, BATCH_U)
                        j = (x - 5) // 2 % 2
                        hold(pe, s.att, B + 1)
                        if j == 0 and (not isinstance(B, int) or B):
                            hold(pe, done, before[1] + nth(i, x - 5, TILE_U))
                        tp = pe.transpose(OUT[:, j * P:(j + 1) * P], attended[:, j].rearrange("p m k -> p (m k)"), ident[:, :])
                        if j:
                            tp.then_inc(s.attT_ps, 1)
                    if x % 4 == 0 and inside(i, x - 8, UNITS):
                        hold(pe, s.attT, nth(i, x - 8, TILE_U) + 1)
                        for m in range(2):
                            mm = pe.matmul(OUT[:, 2 * P:2 * P + D], attendedT[:, m].rearrange("p b t -> p (b t)"), wfT[:, m, :], start=m == 0, stop=m == 1)
                        mm.then_inc(s.out, 1)
                    if x % PART < 4 and inside(i, x + PART, UNITS):
                        tensor_stages[x % PART](pe, nth(i, x, PART) + 1, (x // PART + 1) % 2)
                over_units(pe, step, 10)

            return sync, gpsimd, scalar, vector, tensor

        def layer2_experts(before, done):
            EXPERTS = 7

            def load(sp, n, raw_up, raw_down, signal):
                for mat, (routed, shared) in enumerate((("L2_ffn_W1", "L2_ffn_Ws1"), ("L2_ffn_Wg", "L2_ffn_Wsg"), ("L2_ffn_W2", "L2_ffn_Ws2"))):
                    w = io[shared] if isinstance(n, int) and n == 0 else io[routed][ds(n - 1, 1)].rearrange("o a b -> (o a) b")
                    sp.dma_start(raw_down if mat == 2 else raw_up[:, mat], w.rearrange("(c p) h -> p c h", p=P)).then_inc(signal, 16)
            load.count = 3

            return gated_experts("f2", 5, 2, 2, gates[:, 6:7], before, done, EXPERTS, 3,
                                 (False, io["L2_ffn_gate_w"], io["L2_ffn_gate_b"], io["L2_ffn_biases"]),
                                 chunks=[(0, P), (P, P)], outputs=[[(0, 0, P)], [(0, 0, P)]], groups=EXPERTS + 1,
                                 load=load, up_width=2 * P, down_chunks=2)

        def make_whole_weights():
            w = Names()
            I = 1024
            IC = I // P
            MAT = I * D // P
            UP, DOWN = 0, 1
            lay = Layout()
            lay.at = L3_ATTENTION
            w.up, w.down = lay(DC, I, dt=BF16), lay(IC, D, dt=BF16)
            tern = lay(2, MAT, dt=BF16)
            size_sum, w.mean, per_mean, w.out_factor = lay(2), lay(2), lay(2), lay(1)
            w.free = lay.at
            whole = Names()
            (
                whole.raw, whole.size, whole.total, whole.chain, _, whole.tern, _, whole.w_tp, whole.w
            ) = whole_sems[0:9]
            was = whole_used
            raw_m = raw[:, 0:2 * MAT].rearrange("p (m k) -> p m k", m=2)
            w.CHAIN = 7

            def sync(sp):
                sp.wait_ge(gated_sems[1], gated_counts[-1][1] + 1)
                for m, name in ((UP, "L3_ffn_w1"), (DOWN, "L3_ffn_w2")):
                    sp.dma_start(raw_m[:, m, :].rearrange("p (a k) -> p a k", k=I if m == DOWN else D),
                                 io[name].rearrange("(a p) k -> p a k", p=P)).then_inc(whole.raw, 16)

            def scalar_sizes(act):
                act.wait_ge(whole.raw, was.raw + 32)
                for m in range(2):
                    act.activation(tern[:, m, :], raw_m[:, m, :], ACT.Abs, accum_out=size_sum[:, m:m + 1]).then_inc(whole.size, 1)

            def tensor_total(pe):
                pe.wait_ge(whole.size, was.size + 2)
                pe.matmul(bank[5][:, 0:2], ones[:, :], size_sum, start=True, stop=True).then_inc(whole.total, 1)

            def vector(dve):
                dve.wait_ge(whole.total, was.total + 1)
                link = linker(dve, whole.chain, was.chain)
                link(dve.tensor_scalar(w.mean, bank[5][:, 0:2], 1.0 / (I * D), QUANT_EPS, ALU.mult, ALU.max))
                link(dve.reciprocal(per_mean, w.mean))
                link(dve.tensor_scalar(w.out_factor, w.mean[:, DOWN:DOWN + 1], gates[:, 7:8], None, ALU.mult))
                for m in range(2):
                    v = raw_m[:, m, :]
                    link(dve.tensor_scalar(v, v, per_mean[:, m:m + 1], MAGIC, ALU.mult, ALU.add))
                    link(dve.tensor_scalar(tern[:, m, :], v, MAGIC, -1.0, ALU.subtract, ALU.max))
                    dve.tensor_scalar(tern[:, m, :], tern[:, m, :], 1.0, None, ALU.min).then_inc(whole.tern, 1)

            def tensor_turn(pe):
                for q in range(4):
                    m, half = divmod(q, 2)
                    pe.wait_ge(whole.tern, was.tern + m + 1)
                    for j in range(IC):
                        at = j * D + half * P if m == UP else (j % 2) * I + (half * IC // 2 + j // 2) * P
                        tp = pe.transpose(bank[q][:, :].bitcast(BF16)[:, j * P:(j + 1) * P], tern[:, m, at:at + P], identb[:, :])
                    tp.then_inc(whole.w_tp, 1)

            def scalar_keep(act):
                for q in range(4):
                    act.wait_ge(whole.w_tp, was.w_tp + q + 1)
                    to = w.up[:, q, :] if q < 2 else flat(w.down[:, q % 2 * IC // 2:(q % 2 + 1) * IC // 2, :])
                    act.activation(to, bank[q][:, :].bitcast(BF16), ACT.Copy).then_inc(whole.w, 1)

            w.sync, w.scalar_sizes, w.tensor_total, w.vector, w.tensor_turn, w.scalar_keep = (
                sync, scalar_sizes, tensor_total, vector, tensor_turn, scalar_keep)
            return w

        whole_weights = Names()

        def layer3_attention(before, done):
            whole_weights.made = make_whole_weights()
            whole = whole_weights.made
            lay = Layout()
            summary = lay(D)[0:BATCH]
            spread = lay(TILES, P)[0:BATCH]
            gain, offset = lay(D), lay(D)
            stat, mean_var, var_eps, rstd, shift = lay(TILES, 6), lay(TILES, 2), lay(TILES), lay(TILES), lay(TILES)
            assert lay.at <= L2_EXPERTS, lay.at
            lay.at = L2_EXPERTS
            raw_in, raw_out, affine = lay(DC, D), lay(DC, D), lay(2, D)
            bias_in, bias_out = lay(D)[0:1], lay(D)[0:1]
            w_in, w_out = lay(DC, D), lay(DC, D)
            pooled_rows = lay(D)[0:BATCH]
            pooled, state = lay(DC, BATCH), lay(DC, BATCH)
            assert lay.at <= L3_ATTENTION, lay.at
            lay.at = whole.free
            y = lay(TILES, D)
            scaled = lay(2, BT, D)
            norm = make_norm(6)
            NEXT = 7
            s = Names()
            (
                s.masks, s.pooled_ps, s.pooled, s.state_ps, s.state, s.summary_ps, s.summary, s.spread, s.normed, s.y,
                s.stat, s.rstd, s.affine, s.offset, s.scaled
            ) = sems("a3",
                 "masks pooled_ps pooled state_ps state summary_ps summary spread normed y stat rstd affine offset scaled")
            was = count_weights(loaded=16 * 6, turned=1, ready=2)
            ctx_buf = (ctx_in, ctx_sb, xn, ctx_in)

            def sync(sp):
                sp.dma_start(raw_in, io["L3_xattn_W_in"].rearrange("(a p) k -> p a k", p=P)).then_inc(weight.loaded, 16)
                sp.dma_start(raw_out, io["L3_xattn_W_out"].rearrange("(a p) k -> p a k", p=P)).then_inc(weight.loaded, 16)
                for i in range(BLOCKS):
                    if i == 3:
                        sp.dma_start(bias_in, io["L3_xattn_b_in"].partition_broadcast(1)).then_inc(weight.loaded, 16)
                        sp.dma_start(bias_out, io["L3_xattn_b_out"].partition_broadcast(1)).then_inc(weight.loaded, 16)
                        sp.dma_start(affine[:, 0, :], io["L3_xattn_gamma"].partition_broadcast(P)).then_inc(weight.loaded, 16)
                        sp.dma_start(affine[:, 1, :], io["L3_xattn_beta"].partition_broadcast(P)).then_inc(weight.loaded, 16)
                        whole.sync(sp)
                        sp.wait_ge(s.pooled_ps, 1)
                    sp.dma_start(ctx_buf[i][:, :, :], block_of(io["ctx_2048"], i)).then_inc(ctx_here[i % 3], 16)

            def gpsimd(pool):
                pool.wait_ge(*before)
                pool.memset(spread, 0.0).then_inc(s.masks, 1)
                pool.wait_ge(s.masks, 1)
                at = spread.rearrange("r k (h t) -> r k h t", h=2)
                pool.affine_select(out=at, in_=at, compare_op=ALU.not_equal, fill=1.0, base=0,
                                   pattern=[[2, TILES], [1, 2], [0, SEQ]], channel_multiplier=-1).then_inc(s.masks, 1)
                norm.gpsimd_stats(pool)
                pool.wait_ge(s.affine, 3)

                def block(i):
                    hold(pool, s.normed, i * BT + BT)
                    tiles = X[:, ds(i * BT, BT), :]
                    pool.tensor_tensor(tiles, tiles, offset.unsqueeze(1).to_broadcast([P, BT, D]), ALU.add).then_inc(s.offset, 1)
                    hold(pool, s.stat, i * 2 * BT + 2 * BT)
                    at = ds(i * BT, BT)
                    pool.tensor_scalar(var_eps[:, at], mean_var[:, at, 1], LN_EPS, 1.0, ALU.add, ALU.mult).then_inc(s.rstd, 1)
                    hold(pool, s.rstd, i * 2 + 1)
                    pool.tensor_tensor(rstd[:, at], var_eps[:, at], neg_half[:, 0:BT], ALU.pow).then_inc(s.rstd, 1)
                for i in range(BLOCKS):
                    block(i)

            def scalar(act):
                whole.scalar_sizes(act)
                act.wait_ge(weight.turned, was.turned + 1)
                act.activation(flat(w_in), bank[0][:, :], ACT.Copy).then_inc(weight.ready, 1)
                act.activation(flat(w_out), bank[1][:, :], ACT.Copy).then_inc(weight.ready, 1)
                act.wait_ge(s.pooled_ps, BLOCKS)
                act.activation(pooled_rows, bank[2][0:BATCH, 0:D], ACT.Copy).then_inc(s.pooled, 1)
                act.wait_ge(s.pooled_ps, BLOCKS + 1)
                act.activation(flat(pooled), bank[2][:, D:D + DC * BATCH], ACT.Copy).then_inc(s.pooled, 1)
                act.wait_ge(s.affine, 3)

                def norm_block(i):
                    for t in range(i * BT, (i + 1) * BT):
                        act.activation(y[:, t, :], X[:, t, :], ACT.Identity, scale=ln_rstd[:, t:t + 1], bias=shift[:, t:t + 1]).then_inc(s.normed, 1)
                norm_block(0)
                act.wait_ge(s.state_ps, 1)
                act.activation(flat(state), bank[3][:, 0:DC * BATCH], ACT.Copy).then_inc(s.state, 1)
                act.wait_ge(s.summary_ps, 1)
                act.activation(summary, bank[4][0:BATCH, 0:D], ACT.Copy).then_inc(s.summary, 1)
                for i in range(1, BLOCKS):
                    norm_block(i)
                whole.scalar_keep(act)

            def vector(dve):
                dve.wait_ge(*before)
                norm.vector_means(dve)
                dve.wait_ge(weight.loaded, was.loaded + 16 * 6)
                dve.tensor_scalar(gain, affine[:, 0, :], gates[:, 3:4], None, ALU.mult).then_inc(s.affine, 1)
                dve.tensor_scalar(offset, affine[:, 1, :], gates[:, 3:4], None, ALU.mult).then_inc(s.affine, 1)
                whole.vector(dve)
                dve.wait_ge(norm.rstd, norm.all_there)
                dve.scalar_tensor_tensor(shift, ln_mv[:, :, 0], -1.0, ln_rstd[:, :], ALU.mult, ALU.mult).then_inc(s.affine, 1)

                def sums(i):
                    for k in range(BT):
                        t = i * BT + k
                        dve.wait_ge(s.spread, t // 2 + 1)
                        dve.wait_ge(s.normed, t + 1)
                        dve.tensor_tensor(y[:, t, :], y[:, t, :], bank[6 + k // 2][:, k % 2 * D:k % 2 * D + D], ALU.add).then_inc(s.y, 1)
                    for k in range(BT):
                        t = i * BT + k
                        dve.wait_ge(s.y, t + 1)
                        dve.bn_stats(stat[:, t, :], y[:, t, :]).then_inc(s.stat, 1)
                    for k in range(BT):
                        t = i * BT + k
                        dve.wait_ge(s.stat, i * 2 * BT + k + 1)
                        dve.bn_aggr(mean_var[:, t, :], stat[:, t, :]).then_inc(s.stat, 1)

                def outputs(i):
                    dve.wait_ge(s.rstd, i * 2 + 2)
                    dve.wait_ge(s.offset, i + 1)
                    dve.wait_ge(s.affine, 3)
                    for k in range(BT):
                        t = i * BT + k
                        dve.scalar_tensor_tensor(scaled[:, i % 2, k, :], y[:, t, :], mean_var[:, t, 0:1], gain, ALU.subtract, ALU.mult).then_inc(s.scaled, 1)
                    for k in range(BT):
                        t = i * BT + k
                        dve.wait_ge(s.scaled, t + 1)
                        dve.scalar_tensor_tensor(X[:, t, :], scaled[:, i % 2, k, :], rstd[:, t:t + 1], X[:, t, :], ALU.mult, ALU.add).then_inc(done, 1)
                    for k in range(BT):
                        dve.wait_ge(done, before[1] + i * BT + k + 1)
                        next_stat(dve, i * BT + k)
                    for k in range(BT):
                        dve.wait_ge(norm.stat, NEXT * 2 * TILES + i * 2 * BT + k + 1)
                        dve.bn_aggr(ln_mv[:, i * BT + k, :], ln_stat[:, i * BT + k, :]).then_inc(norm.stat, 1)

                for i in range(BLOCKS + 1):
                    if i < BLOCKS:
                        sums(i)
                    if i:
                        outputs(i - 1)

            def tensor(pe):
                pe.wait_ge(*before)
                whole.tensor_total(pe)
                pe.wait_ge(weight.loaded, was.loaded + 16 * 6)
                for j, w in enumerate((raw_in, raw_out)):
                    for c in range(DC):
                        for a in range(DC):
                            tp = pe.transpose(bank[j][:, c * D + a * P:c * D + (a + 1) * P], w[:, a, c * P:(c + 1) * P], ident[:, :])
                tp.then_inc(weight.turned, 1)
                pe.wait_ge(scan.chain, scan.ready)
                for i in range(BLOCKS):
                    pe.wait_ge(ctx_here[i % 3], 2 * RING_LOADS + 16 * (i // 3 + 1))
                    for k in range(BT):
                        b = 2 * (i * BT + k)
                        mm = pe.matmul(bank[2][0:BATCH, 0:D], scan.strip[:, BATCH - 2 - b:2 * BATCH - 2 - b], flat(ctx_buf[i][:, k:k + 1, :]),
                                       start=b == 0, stop=b == BATCH - 2)
                    mm.then_inc(s.pooled_ps, 1)
                pe.wait_ge(s.pooled, 1)
                for c in range(DC):
                    tp = pe.transpose(bank[2][:, D + c * BATCH:D + (c + 1) * BATCH], pooled_rows[:, c * P:(c + 1) * P], ident[0:BATCH, 0:BATCH])
                tp.then_inc(s.pooled_ps, 1)
                pe.wait_ge(s.pooled, 2)
                pe.wait_ge(weight.ready, was.ready + 2)
                for m in range(DC):
                    for c in range(DC):
                        pe.matmul(bank[3][:, m * BATCH:(m + 1) * BATCH], w_in[:, c, m * P:(m + 1) * P], pooled[:, c, :],
                                  start=c == 0, stop=False)
                    mm = pe.matmul(bank[3][:, m * BATCH:(m + 1) * BATCH], bias_in[0:1, m * P:(m + 1) * P], scan.totals[0:1, :],
                                   start=False, stop=True)
                mm.then_inc(s.state_ps, 1)
                pe.wait_ge(s.state, 1)
                for c in range(DC):
                    pe.matmul(bank[4][0:BATCH, 0:D], state[:, c, :], w_out[:, c, :], start=c == 0, stop=False)
                pe.matmul(bank[4][0:BATCH, 0:D], ones[0:1, 0:BATCH], bias_out, start=False, stop=True).then_inc(s.summary_ps, 1)
                pe.wait_ge(s.summary, 1)
                pe.wait_ge(s.masks, 2)
                for t in range(TILES):
                    k = t % BT
                    if t >= BT and k % 2 == 0:
                        pe.wait_ge(s.y, t - BT + 2)
                    mm = pe.matmul(bank[6 + k // 2][:, k % 2 * D:k % 2 * D + D], spread[:, t, :], summary, start=True, stop=True)
                    if k % 2:
                        mm.then_inc(s.spread, 1)
                whole.tensor_turn(pe)

            return sync, gpsimd, scalar, vector, tensor

        def layer3_experts(before, done):
            I = 1024
            IC = I // P
            HALF = I // 2
            UP = 0
            weights = whole_weights.made
            up_w, down_w, out_factor = weights.up, weights.down, weights.out_factor
            lay = Layout()
            lay.at = weights.free
            SUBLAYER = 7
            norm = make_norm(SUBLAYER)
            gelu_scale, shift = lay(TILES), lay(TILES)
            hidden, shifted, wholeT = lay(2, I), lay(2, I), lay(2, I, dt=BF16)
            xqT = lay(DC, TOK, dt=BF16)
            quant = make_quant(1, lay, flat(shifted), xqT)
            peak, unit, rate, out_scale = lay(2), lay(2), lay(2), lay(BT)
            s = Names()
            (
                s.raw, s.size, s.total, s.chain, s.ternary, s.tern, s.shifted, s.w_tp, s.w, s.up, s.relu, s.once,
                s.prod, s.peak, s.pair, s.rate, s.turned, s.wholeT, s.down, s.acc
            ) = whole_sems
            was = whole_used
            stored = sem("stored")
            through = (xn, ctx_sb)

            def sync(sp):
                with sp.Fori(0, BLOCKS) as i:
                    sp.wait_ge(s.acc, was.acc + i * BT + BT)
                    sp.dma_start(block_of(io["out"], i), X[:, ds(i * BT, BT), :]).then_inc(stored, 16)
                sp.wait_ge(stored, 16 * BLOCKS)

            def gpsimd(pool):
                for i in range(BLOCKS):
                    pool.wait_ge(norm.stat, SUBLAYER * 2 * TILES + (i + 1) * 2 * BT)
                    norm.gpsimd_rstd(pool, i)

            def scalar_norm(act, i):
                act.wait_ge(s.chain, was.chain + weights.CHAIN + i + 1)
                if i >= 2:
                    act.wait_ge(quant.shifted, (quant.first + i - 1) * BT)
                for k in range(BT):
                    t = i * BT + k
                    act.activation(through[i % 2][:, k, :], X[:, t, :], ACT.Identity, scale=ln_rstd[:, t:t + 1],
                                   bias=shift[:, t:t + 1]).then_inc(norm.xn, 1)

            def vector_offset(dve, i):
                tiles = slice(i * BT, (i + 1) * BT)
                dve.wait_ge(norm.rstd, norm.all_there - TILES + (i + 1) * BT)
                dve.scalar_tensor_tensor(shift[:, tiles], ln_mv[:, tiles, 0], -1.0, ln_rstd[:, tiles], ALU.mult, ALU.mult).then_inc(s.chain, 1)

            def scalar_gelu(act, T, k):
                act.wait_ge(s.up, was.up + T + 1)
                act.wait_ge(s.shifted, was.shifted + T - 1)
                for h in range(2):
                    act.activation(hidden[:, k % 2, h * HALF:(h + 1) * HALF], bank[2 * (k % 2) + h][:, :], ACT.Gelu,
                                   scale=gelu_scale[:, ds(T, 1)]).then_inc(s.relu, 1)

            def scalar_back(act, T, k):
                act.wait_ge(s.turned, was.turned + T + 1)
                for h in range(2):
                    act.activation(wholeT[:, k % 2, h * HALF:(h + 1) * HALF], bank[4 + h][:, :], ACT.Copy, bias=-MAGIC).then_inc(s.wholeT, 1)

            def vector_peak(dve, T, k):
                j = slice(k % 2, k % 2 + 1)
                dve.wait_ge(s.relu, was.relu + T * 2 + 2)
                dve.tensor_reduce(peak[:, j], hidden[:, k % 2, :], AX.X, ALU.max, apply_absolute_value=True).then_inc(s.peak, 1)
                dve.wait_ge(s.peak, was.peak + T + 1)
                dve.tensor_scalar(unit[:, j], peak[:, j], QUANT_EPS, 1.0 / 127, ALU.max, ALU.mult).then_inc(s.pair, 1)

            def vector_shift(dve, T, k):
                j = slice(k % 2, k % 2 + 1)
                hold(dve, s.pair, was.pair + T * 2 + 1)
                dve.reciprocal(rate[:, j], unit[:, j]).then_inc(s.rate, 1)
                dve.tensor_scalar(out_scale[:, k % BT:k % BT + 1], unit[:, j], out_factor, None, ALU.mult).then_inc(s.pair, 1)
                dve.wait_ge(s.rate, was.rate + T + 1)
                hold(dve, s.turned, was.turned + T - 1)
                dve.tensor_scalar(shifted[:, k % 2, :], hidden[:, k % 2, :], rate[:, j], MAGIC, ALU.mult, ALU.add).then_inc(s.shifted, 1)

            def vector_back(dve, T, k):
                dve.wait_ge(s.down, was.down + T + 1)
                dve.wait_ge(s.pair, was.pair + T * 2 + 2)
                dve.scalar_tensor_tensor(x_tile(T), bank[6 + k % 2][:, 0:D], out_scale[:, k % BT:k % BT + 1], x_tile(T),
                                         ALU.mult, ALU.add).then_inc(s.acc, 1)

            def tensor_up(pe, T, k):
                hold(pe, s.relu, was.relu + T * 2 - 2)
                for h in range(2):
                    for c in range(DC):
                        mm = pe.matmul(bank[2 * (k % 2) + h][:, :], flat(xqT[:, c:c + 1, ds(T * P, P)]), up_w[:, c, h * HALF:(h + 1) * HALF],
                                       start=c == 0, stop=c == DC - 1)
                mm.then_inc(s.up, 1)

            def tensor_turn(pe, T, k):
                hold(pe, s.shifted, was.shifted + T + 1)
                for c in range(IC):
                    tp = pe.transpose(bank[4 + c // 4][:, c % 4 * P:(c % 4 + 1) * P], shifted[:, k % 2, c * P:(c + 1) * P], ident[:, :])
                tp.then_inc(s.turned, 1)

            def tensor_down(pe, T, k):
                hold(pe, s.wholeT, was.wholeT + T * 2 + 2)
                hold(pe, s.acc, was.acc + T - 1)
                for c in range(IC):
                    mm = pe.matmul(bank[6 + k % 2][:, 0:D], wholeT[:, k % 2, c * P:(c + 1) * P], down_w[:, c, :],
                                   start=c == 0, stop=c == IC - 1)
                mm.then_inc(s.down, 1)

            def over_blocks(eng, step):
                step(0, True)
                with eng.Fori(1, BLOCKS - 1) as i:
                    step(i, True)
                step(BLOCKS - 1, False)

            def scalar(act):
                for i in range(2):
                    scalar_norm(act, i)
                for i in range(BLOCKS):
                    if i + 2 < BLOCKS:
                        scalar_norm(act, i + 2)
                    quant.scalar(act, i)
                    if 1 <= i <= 2:
                        act.wait_ge(s.chain, was.chain + weights.CHAIN + BLOCKS + 1)
                        scalar_gelu(act, i - 1, i - 1)
                act.wait_ge(s.chain, was.chain + weights.CHAIN + 2 * BLOCKS)

                def step(i, more):
                    for k in range(BT):
                        T = i * BT + k
                        if k + 2 < BT or more:
                            scalar_gelu(act, T + 2, k)
                        scalar_back(act, T, k)
                over_blocks(act, step)

            def vector(dve):
                dve.wait_ge(*before)
                for i in range(BLOCKS):
                    vector_offset(dve, i)
                for i in range(BLOCKS):
                    tiles = slice(i * BT, (i + 1) * BT)
                    quant.vector(dve, norm, i, through[i % 2])
                    dve.tensor_scalar(gelu_scale[:, tiles], quant.step[:, tiles], weights.mean[:, UP:UP + 1], None, ALU.mult).then_inc(s.chain, 1)
                vector_peak(dve, 0, 0)
                dve.wait_ge(quant.tp, quant.first + BLOCKS)
                vector_shift(dve, 0, 0)

                def step(i, more):
                    for k in range(BT):
                        T = i * BT + k
                        if k + 1 < BT or more:
                            vector_peak(dve, T + 1, k + 1)
                        if k >= 2 or not isinstance(i, int) or i:
                            vector_back(dve, T - 2, (k - 2) % BT)
                        if k + 1 < BT or more:
                            vector_shift(dve, T + 1, k + 1)
                over_blocks(dve, step)
                for k in range(BT - 2, BT):
                    vector_back(dve, TILES - BT + k, k)
                dve.wait_ge(s.acc, was.acc + TILES)
                dve.sem_inc(done, TILES)

            def tensor(pe):
                for i in range(BLOCKS):
                    quant.tensor(pe, i)
                    if i == 0:
                        pe.wait_ge(s.w, was.w + 4)
                    elif i <= 2:
                        tensor_up(pe, i - 1, i - 1)
                pe.wait_ge(quant.turned, (quant.first + BLOCKS) * DC)

                def step(i, more):
                    for k in range(BT):
                        T = i * BT + k
                        if k + 2 < BT or more:
                            tensor_up(pe, T + 2, k)
                        if k or not isinstance(i, int) or i:
                            tensor_down(pe, T - 1, (k - 1) % BT)
                        tensor_turn(pe, T, k)
                over_blocks(pe, step)
                tensor_down(pe, TILES - 1, BT - 1)

            return sync, gpsimd, scalar, vector, tensor

        done = sem("done")
        makers = [layer0_attention, layer0_experts, layer1_attention, layer1_experts,
                  layer2_attention, layer2_experts, layer3_attention, layer3_experts]
        sublayers = [make((done, j * TILES), done) for j, make in enumerate(makers)]

        block = ctx.enter_context(nc.Block())

        @block.sync
        def _(sp):
            setup_sync(sp)
            scan_programs[SYNC](sp)
            for sublayer in sublayers:
                sublayer[SYNC](sp)

        @block.gpsimd
        def _(pool):
            setup_gpsimd(pool)
            scan_programs[GPSIMD](pool)
            for sublayer in sublayers:
                sublayer[GPSIMD](pool)

        @block.scalar
        def _(act):
            setup_scalar(act)
            scan_programs[SCALAR](act)
            for sublayer in sublayers:
                sublayer[SCALAR](act)

        @block.vector
        def _(dve):
            setup_vector(dve)
            for sublayer in sublayers:
                sublayer[VECTOR](dve)

        @block.tensor
        def _(pe):
            setup_tensor(pe)
            for sublayer in sublayers:
                sublayer[TENSOR](pe)


INPUTS = ("x", "ctx_2048", "mask_BxS2_bk0", "g_xattn", "g_ffn",
          "L0_ffn_gate_w", "L0_ffn_w1", "L0_ffn_w3", "L0_ffn_w2", "L0_ffn_sw1", "L0_ffn_sw3", "L0_ffn_sw2",
          "L1_xattn_Wq", "L1_xattn_Wg", "L1_xattn_bg", "L1_xattn_Wkv", "L1_xattn_Wo",
          "L1_ffn_router_w", "L1_ffn_gate_w", "L1_ffn_up_w", "L1_ffn_down_w",
          "L2_xattn_Wq", "L2_xattn_Wk", "L2_xattn_Wv", "L2_xattn_Wfc", "L2_xattn_bfc",
          "L2_ffn_W1", "L2_ffn_Wg", "L2_ffn_W2", "L2_ffn_Ws1", "L2_ffn_Wsg", "L2_ffn_Ws2",
          "L2_ffn_gate_w", "L2_ffn_gate_b", "L2_ffn_biases",
          "L3_xattn_decay", "L3_xattn_W_in", "L3_xattn_b_in", "L3_xattn_W_out", "L3_xattn_b_out",
          "L3_xattn_gamma", "L3_xattn_beta", "L3_ffn_w1", "L3_ffn_w2")


def kernel(**inputs):
    import concourse.bacc as bacc
    from concourse.bass_utils import run_bass_kernel_spmd

    nc = bacc.Bacc("TRN2", target_bir_lowering=False, num_devices=1)
    arrays, io = {}, {}
    for name in INPUTS:
        a = np.ascontiguousarray(inputs[name])
        if a.ndim == 0:
            a = a.reshape(1)
        arrays["in_" + name] = a
        io[name] = nc.dram_tensor("in_" + name, a.shape, mybir.dt.from_np(a.dtype), kind="ExternalInput").ap()
    io["out"] = nc.dram_tensor("out", (BATCH, SEQ, D), F32, kind="ExternalOutput").ap()
    build_program(nc, io)
    return run_bass_kernel_spmd(nc, [arrays], core_ids=[0]).results[0]["out"]
```
